# Optimizing a Trainium2 kernel written in Bass

```python
import numpy as np
import jax
import jax.numpy as jnp

def _softmax(x, axis=-1):
    return jax.nn.softmax(x, axis=axis)

def _gelu(x):
    return jax.nn.gelu(x, approximate=True)

def _silu(x):
    return jax.nn.silu(x)

def _sigmoid(x):
    return jax.nn.sigmoid(x)

def _layernorm(x, axis=-1, eps=1e-05):
    m = jnp.mean(x, axis=axis, keepdims=True)
    v = jnp.var(x, axis=axis, keepdims=True)
    return (x - m) / jnp.sqrt(v + eps)

def _scatter_add(tgt, idx, src, axis=0):
    return tgt.at[idx].add(src)

def _segment_sum(src, seg, n):
    return jax.ops.segment_sum(src, seg, n)
kernel_name = 'mk_gps_d1_gnn_r32_3721e4'

def setup_inputs(seed: int=0):
    np.random.seed(seed)
    _w = jnp.asarray

    def _rec_inputs():
        import jax
        import jax.numpy as jnp
        _gk = jax.random.key(seed)
        x = -0.0002117 + 1 * jax.random.normal(jax.random.fold_in(_gk, 1), (3125, 256), jnp.float32)
        _s = jax.random.randint(jax.random.fold_in(_gk, 2), (25000,), 0, 3125, jnp.int32)
        _d = jax.random.randint(jax.random.fold_in(_gk, 3), (25000,), 0, 3125, jnp.int32)
        _loop = jnp.arange(3125, dtype=jnp.int32)
        src = jnp.concatenate([_s, _d, _loop])
        dst = jnp.concatenate([_d, _s, _loop])
        _o = jnp.argsort(dst, stable=True)
        src = src[_o]
        dst = dst[_o]
        edge_weight = jax.random.uniform(jax.random.fold_in(_gk, 12), (53125,), jnp.float32, 0.0, 1)
        return (x, src, dst, edge_weight)
    x, src, dst, edge_weight = _rec_inputs()

    def _L0_gnn_setup():
        import jax, jax.numpy as jnp
        import numpy as np
        N = 3125
        D_IN = 256
        D_OUT = 256
        E = 100000
        key = jax.random.key(seed)
        ks = jax.random.split(key, 9)
        x = jax.random.normal(ks[0], (N, D_IN), dtype=jnp.float32)
        edge_src = jax.random.randint(ks[1], (E,), 0, N, dtype=jnp.int32)
        edge_dst = jax.random.randint(ks[2], (E,), 0, N, dtype=jnp.int32)
        edge_weight = jax.random.uniform(ks[3], (E,), dtype=jnp.float32)
        eps = jnp.zeros((1,), dtype=jnp.float32)
        lim1 = 1.0 / np.sqrt(D_IN)
        w1 = jax.random.uniform(ks[4], (D_IN, D_OUT), minval=-lim1, maxval=lim1, dtype=jnp.float32)
        b1 = jax.random.uniform(ks[5], (D_OUT,), minval=-lim1, maxval=lim1, dtype=jnp.float32)
        lim2 = 1.0 / np.sqrt(D_OUT)
        w2 = jax.random.uniform(ks[6], (D_OUT, D_OUT), minval=-lim2, maxval=lim2, dtype=jnp.float32)
        b2 = jax.random.uniform(ks[7], (D_OUT,), minval=-lim2, maxval=lim2, dtype=jnp.float32)
        return {'x': x, 'edge_src': edge_src, 'edge_dst': edge_dst, 'edge_weight': edge_weight, 'eps': eps, 'w1': w1, 'b1': b1, 'w2': w2, 'b2': b2}
    _L0_gnn_all = _L0_gnn_setup()
    _L0_gnn_in = {k: v for k, v in _L0_gnn_all.items() if k in ('eps', 'w1', 'b1', 'w2', 'b2')}
    del _L0_gnn_all

    def _L0_mix_setup():
        import jax, jax.numpy as jnp
        import numpy as np
        B, L, D, H = (4, 512, 256, 8)
        DK = D // H

        def _heads(t):
            b, l, d = t.shape
            return t.reshape(b, l, H, DK).transpose(0, 2, 1, 3)
        key = jax.random.key(seed)
        ks = jax.random.split(key, 9)
        s = 0.02
        return {'x': jax.random.normal(ks[0], (B, L, D), dtype=jnp.float32), 'Wq': jax.random.normal(ks[1], (D, D), dtype=jnp.float32) * s, 'bq': jnp.zeros((D,), dtype=jnp.float32), 'Wk': jax.random.normal(ks[2], (D, D), dtype=jnp.float32) * s, 'bk': jnp.zeros((D,), dtype=jnp.float32), 'Wv': jax.random.normal(ks[3], (D, D), dtype=jnp.float32) * s, 'bv': jnp.zeros((D,), dtype=jnp.float32), 'Wfc': jax.random.normal(ks[4], (D, D), dtype=jnp.float32) * s, 'bfc': jnp.zeros((D,), dtype=jnp.float32)}
    _L0_mix_all = _L0_mix_setup()
    _L0_mix_in = {k: v for k, v in _L0_mix_all.items() if k in ('Wq', 'bq', 'Wk', 'bk', 'Wv', 'bv', 'Wfc', 'bfc')}
    del _L0_mix_all

    def _L0_ffn_setup():
        import jax, jax.numpy as jnp
        import numpy as np
        E = 8
        K = 2
        D = 256
        H = 512
        DOUT = 256
        EPS = 1e-05
        key = jax.random.key(seed)
        ks = jax.random.split(key, 9)
        s = 0.02
        return {'x': jax.random.normal(ks[0], (4, 256, D), jnp.float32), 'gamma': 1.0 + 0.05 * jax.random.normal(ks[1], (D,), jnp.float32), 'beta': 0.05 * jax.random.normal(ks[2], (D,), jnp.float32), 'Wr': 0.01 * jax.random.normal(ks[3], (D, E), jnp.float32), 'br': jnp.zeros((E,), jnp.float32), 'W1': s * jax.random.normal(ks[4], (E, D, H), jnp.float32), 'b1': s * jax.random.normal(ks[5], (E, H), jnp.float32), 'W2': s * jax.random.normal(ks[6], (E, H, DOUT), jnp.float32), 'b2': s * jax.random.normal(ks[7], (E, DOUT), jnp.float32)}
    _L0_ffn_all = _L0_ffn_setup()
    _L0_ffn_in = {k: v for k, v in _L0_ffn_all.items() if k in ('gamma', 'beta', 'Wr', 'br', 'W1', 'b1', 'W2', 'b2')}
    del _L0_ffn_all
    return {'x': x, 'src': src, 'dst': dst, 'edge_weight': edge_weight, 'L0_gnn_eps': _L0_gnn_in['eps'], 'L0_gnn_w1': _L0_gnn_in['w1'], 'L0_gnn_b1': _L0_gnn_in['b1'], 'L0_gnn_w2': _L0_gnn_in['w2'], 'L0_gnn_b2': _L0_gnn_in['b2'], 'L0_mix_Wq': _L0_mix_in['Wq'], 'L0_mix_bq': _L0_mix_in['bq'], 'L0_mix_Wk': _L0_mix_in['Wk'], 'L0_mix_bk': _L0_mix_in['bk'], 'L0_mix_Wv': _L0_mix_in['Wv'], 'L0_mix_bv': _L0_mix_in['bv'], 'L0_mix_Wfc': _L0_mix_in['Wfc'], 'L0_mix_bfc': _L0_mix_in['bfc'], 'L0_ffn_gamma': _L0_ffn_in['gamma'], 'L0_ffn_beta': _L0_ffn_in['beta'], 'L0_ffn_Wr': _L0_ffn_in['Wr'], 'L0_ffn_br': _L0_ffn_in['br'], 'L0_ffn_W1': _L0_ffn_in['W1'], 'L0_ffn_b1': _L0_ffn_in['b1'], 'L0_ffn_W2': _L0_ffn_in['W2'], 'L0_ffn_b2': _L0_ffn_in['b2']}

def reference(x, src, dst, edge_weight, L0_gnn_eps, L0_gnn_w1, L0_gnn_b1, L0_gnn_w2, L0_gnn_b2, L0_mix_Wq, L0_mix_bq, L0_mix_Wk, L0_mix_bk, L0_mix_Wv, L0_mix_bv, L0_mix_Wfc, L0_mix_bfc, L0_ffn_gamma, L0_ffn_beta, L0_ffn_Wr, L0_ffn_br, L0_ffn_W1, L0_ffn_b1, L0_ffn_W2, L0_ffn_b2):
    import jax
    import jax.numpy as jnp

    def _L0_gnn_ref(x, edge_src, edge_dst, edge_weight, eps, w1, b1, w2, b2):
        import jax, jax.numpy as jnp
        import numpy as np
        N = 3125
        D_IN = 256
        D_OUT = 256
        E = 100000
        msgs = edge_weight[:, None] * x[edge_src]
        agg = jax.ops.segment_sum(msgs, edge_dst, num_segments=N)
        h = (1.0 + eps[0]) * x + agg
        h = jax.nn.relu(h @ w1 + b1)
        return h @ w2 + b2

    def _L0_mix_ref(x, Wq, bq, Wk, bk, Wv, bv, Wfc, bfc):
        import jax, jax.numpy as jnp
        import numpy as np
        B, L, D, H = (4, 512, 256, 8)
        DK = D // H

        def _heads(t):
            b, l, d = t.shape
            return t.reshape(b, l, H, DK).transpose(0, 2, 1, 3)
        q = _heads(x @ Wq.T + bq)
        k = _heads(x @ Wk.T + bk)
        v = _heads(x @ Wv.T + bv)
        seq_len = q.shape[-2]
        p_attn = jnp.einsum('bhnd,bhne->bhde', k, v) / seq_len
        out = jnp.einsum('bhnd,bhde->bhne', q, p_attn)
        out = out.transpose(0, 2, 1, 3).reshape(x.shape[0], seq_len, H * DK)
        return out @ Wfc.T + bfc

    def _L0_ffn_ref(x, gamma, beta, Wr, br, W1, b1, W2, b2):
        import jax, jax.numpy as jnp
        import numpy as np
        E = 8
        K = 2
        D = 256
        H = 512
        DOUT = 256
        EPS = 1e-05
        mu = jnp.mean(x, axis=-1, keepdims=True)
        var = jnp.mean(jnp.square(x - mu), axis=-1, keepdims=True)
        xn = (x - mu) * jax.lax.rsqrt(var + EPS) * gamma + beta
        logits = jnp.einsum('bsd,de->bse', xn, Wr) + br
        top_vals, top_idx = jax.lax.top_k(logits, K)
        w = jax.nn.softmax(top_vals, axis=-1)
        w_full = jnp.einsum('bsk,bske->bse', w, jax.nn.one_hot(top_idx, E, dtype=w.dtype))
        y = jnp.zeros(x.shape[:-1] + (DOUT,), x.dtype)
        for e in range(E):
            h = jax.nn.gelu(jnp.einsum('bsd,dh->bsh', xn, W1[e]) + b1[e], approximate=False)
            y_e = jnp.einsum('bsh,hd->bsd', h, W2[e]) + b2[e]
            y = y + y_e * w_full[..., e, None]
        return y
    xn = _layernorm(x, axis=-1)
    x = x + _L0_gnn_ref(xn, src, dst, edge_weight, L0_gnn_eps, L0_gnn_w1, L0_gnn_b1, L0_gnn_w2, L0_gnn_b2) + _L0_mix_ref(xn[None], L0_mix_Wq, L0_mix_bq, L0_mix_Wk, L0_mix_bk, L0_mix_Wv, L0_mix_bv, L0_mix_Wfc, L0_mix_bfc)[0]
    x = x + _L0_ffn_ref(_layernorm(x, axis=-1)[None], L0_ffn_gamma, L0_ffn_beta, L0_ffn_Wr, L0_ffn_br, L0_ffn_W1, L0_ffn_b1, L0_ffn_W2, L0_ffn_b2)[0]
    return x

_drawn_inputs = setup_inputs


def setup_inputs(seed=0):
    import zlib

    import numpy as np

    out = dict(_drawn_inputs(seed))
    spreads = {'L0_mix_bq': (0.0, 0.8),
     'L0_mix_bk': (0.0, 0.8),
     'L0_mix_bv': (0.0, 0.8),
     'L0_mix_bfc': (0.0, 0.8),
     'L0_ffn_br': (0.0, 0.8)}
    factors = {'L0_gnn_b1': 35.68,
     'L0_mix_Wq': 8.0,
     'L0_mix_Wk': 8.0,
     'L0_mix_Wv': 8.0,
     'L0_mix_Wfc': 8.0,
     'L0_ffn_gamma': 57.64,
     'L0_ffn_beta': 45.904,
     'L0_ffn_b1': 200.0,
     'L0_ffn_b2': 196.987,
     'edge_weight': 6.279,
     'L0_gnn_w1': 3.029,
     'L0_gnn_b2': 8.0,
     'L0_ffn_Wr': 3.48,
     'L0_ffn_W1': 3.532,
     'L0_ffn_W2': 3.029}
    for name, (base, spread) in spreads.items():
        noise = np.random.default_rng([zlib.crc32(name.encode()), seed]).standard_normal(out[name].shape)
        drawn = base * np.exp(spread * noise) if base else spread * noise
        out[name] = jnp.asarray(drawn.astype(out[name].dtype))
    for name, factor in factors.items():
        out[name] = (out[name] * factor).astype(out[name].dtype)
    return out
```

```python
from contextlib import ExitStack

import numpy as np
import concourse.bass as bass
from concourse import mybir

F32 = mybir.dt.float32
BF16 = mybir.dt.bfloat16
I32 = mybir.dt.int32
U32 = mybir.dt.uint32
ALU = mybir.AluOpType
ACT = mybir.ActivationFunctionType
AX_X = mybir.AxisListType.X

P = 128
N, D = 3125, 256
KC = D // P
TP = 125
NT = N // TP
BT = 5
NB = NT // BT
EDGES = 53125
EP = 125
ET = EDGES // EP
G = 5
NG = ET // G
W = 64
RING = 4
NWIN = -(-N // W)
HEADS = 8
DK = D // HEADS
EX, HID = 8, 512
HC = HID // P
MT = 56
STRIDE = 26 * P
SLOTS = EX * STRIDE + MT * P
U = 4
LN_EPS = 1e-5


def wait_from(eng, sem, value):
    if isinstance(value, int) and value <= 0:
        return
    eng.wait_ge(sem, value)


def build(nc, x, src, dst, edge_weight, gnn_eps, gnn_w1, gnn_b1, gnn_w2, gnn_b2,
          Wq, bq, Wk, bk, Wv, bv, Wfc, bfc, gamma, beta, Wr, br, W1, b1, W2, b2, out):
    ctx = ExitStack()
    with ctx:
        def sb(name, shape, dt=F32):
            return ctx.enter_context(nc.sbuf_tensor(name, shape, dt))

        def sem(name):
            return ctx.enter_context(nc.semaphore(name))

        xn_rows = nc.dram_tensor("xn_rows", (N, D), F32, kind="Internal").ap()
        u_rows = nc.dram_tensor("u_rows", (N, D), F32, kind="Internal").ap()
        token_list = nc.dram_tensor("token_list", (SLOTS, 1), I32, kind="Internal").ap()
        y_rows = nc.dram_tensor("y_rows", (MT * P, D), F32, kind="Internal").ap()

        bank = [ctx.enter_context(nc.psum_tensor(f"bank{i}", [P, 512], F32)) for i in range(8)]

        xres = sb("xres", [TP, NT, D])
        shared = sb("shared", [P, NT * (D + 1)])
        xn = shared[0:TP, :].rearrange("p (t d) -> p t d", d=D + 1)
        u = shared[0:TP, 0:NT * D].rearrange("p (t d) -> p t d", d=D)
        xnT = sb("xnT", [P, KC, N])
        aggT = sb("aggT", [P, KC, N + W])
        ring = sb("ring", [P, RING * G * D])
        msg = ring[0:EP, :].rearrange("p (s d) -> p s d", d=D)
        onehot = sb("onehot", [EP, 2 * G, W])
        w2e = sb("w2e", [P, EX, HC, D])
        b2e = sb("b2e", [P, EX, D])

        def cutter(region):
            at = [0]

            def piece(n):
                at[0] += n
                return region[:, at[0] - n:at[0]]
            return piece
        mix_piece = cutter(w2e[:].rearrange("p e c d -> p (e c d)"))
        route_piece = cutter(ring)
        expert_piece = cutter(shared)

        srct = sb("srct", [EP, ET], I32)
        dstt = sb("dstt", [EP, ET], I32)
        wt = sb("wt", [EP, ET])
        dstf = sb("dstf", [EP, NG, G])
        rel = sb("rel", [EP, NG, G])
        gmin = sb("gmin", [EP, NG])
        gminT = sb("gminT", [NG, 1])
        gdiag = sb("gdiag", [NG, NG])
        basef = sb("basef", [EP, NG])
        basei = sb("basei", [1, NG], I32)
        relmax = sb("relmax", [EP, 1])
        flagf = sb("flagf", [1, 2])
        flagi = sb("flagi", [1, 1], I32)
        idxr = sb("idxr", [EP, RING * G], I32)
        relq = sb("relq", [EP, G])
        curf = sb("curf", [1, 1])
        curi = sb("curi", [1, 1], I32)

        ident = sb("ident", [P, P])
        ones = sb("ones", [P, P])
        onesb = sb("onesb", [P, P], BF16)
        before = sb("before", [P, P], BF16)
        hmask = sb("hmask", [P, P // DK, DK])
        iotaW = sb("iotaW", [P, W])
        iota8 = sb("iota8", [P, EX])
        eoff = sb("eoff", [P, EX])
        iotaM = sb("iotaM", [P, MT])
        baseM = sb("baseM", [P, MT])
        tri = sb("tri", [P, EX, EX])
        tokid = sb("tokid", [TP, NT], I32)
        zlist = sb("zlist", [P, SLOTS // P], I32)

        wq = sb("wq", [P, KC, D])
        wk = mix_piece(KC * D).rearrange("p (c i) -> p c i", c=KC)
        wv = mix_piece(KC * D).rearrange("p (c i) -> p c i", c=KC)
        wf = mix_piece(KC * D).rearrange("p (c i) -> p c i", c=KC)
        wkT = mix_piece(KC * D).rearrange("p (c i) -> p c i", c=KC)
        wvT = mix_piece(KC * D).rearrange("p (c i) -> p c i", c=KC)
        wfT = mix_piece(KC * D).rearrange("p (c i) -> p c i", c=KC)
        gram = sb("gram", [P, KC, D + 1])
        rows = sb("rows", [1, 7, D])
        bk_row, bv_row, bfc_row, b2_row, s_row, tl_row, bias_row = (rows[0:1, i, :] for i in range(7))
        bqc = sb("bqc", [P, KC])
        t1 = mix_piece(KC * D).rearrange("p (c i) -> p c i", c=KC)
        ptm = sb("ptm", [P, KC, P])
        a2 = mix_piece(KC * D).rearrange("p (c i) -> p c i", c=KC)
        mixm = sb("mixm", [P, KC, D])
        gw1 = sb("gw1", [P, KC, D])
        gw2 = sb("gw2", [P, KC, D])
        gb1 = sb("gb1", [P, KC])
        eps1 = sb("eps1", [P, 1])

        gammaT = sb("gammaT", [P, KC])
        betaT = sb("betaT", [P, KC])
        wr = sb("wr", [P, KC, EX])
        brb = sb("brb", [P, EX])
        b1T = sb("b1T", [P, EX * HC])

        st = sb("st", [TP, NT, 6])
        mv = sb("mv", [TP, NT, 2])
        veps = sb("veps", [TP, NT])
        sd = sb("sd", [TP, NT])
        rs = sb("rs", [TP, NT])
        st2 = sb("st2", [TP, NT, 6])
        mv2 = sb("mv2", [TP, NT, 2])
        veps2 = sb("veps2", [TP, 2, NT])
        sd2 = sb("sd2", [TP, 2, NT])
        rs2 = sb("rs2", [TP, 3, NT])
        lg = route_piece(NT * EX)[0:TP, :].rearrange("p (t e) -> p t e", e=EX)
        mx = sb("mx", [TP, NT, 8])
        ix = sb("ix", [TP, NT, 8], U32)
        ixf = sb("ixf", [TP, NT, 2])
        pick = sb("pick", [TP, 2, NT, EX])
        m12 = sb("m12", [TP, NT, EX], BF16)
        macc = sb("macc", [TP, NT + 1, EX], BF16)
        pp = route_piece(NT * EX)[0:TP, :].rearrange("p (t e) -> p t e", e=EX)
        ppm = route_piece(2 * NT * EX)[0:TP, :].rearrange("p (s t e) -> p s t e", s=2, e=EX)
        posf = sb("posf", [TP, 2, NT])
        posi = sb("posi", [TP, 2, NT], I32)
        diff = sb("diff", [TP, NT])
        exd = sb("exd", [TP, NT])
        den = sb("den", [TP, NT])
        wtop = sb("wtop", [TP, 2, NT])
        cnti = sb("cnti", [TP, 2, EX], I32)
        cntf = sb("cntf", [TP, 5, EX])
        backf = sb("backf", [TP, 2, 2, NT])
        backi = sb("backi", [TP, 2, NT], I32)
        trin = route_piece(EX * EX)[0:TP, :].rearrange("p (a e) -> p a e", e=EX)
        cond = route_piece(2 * MT * EX)[0:TP, :].rearrange("p (s i e) -> p s i e", s=2, e=EX)
        tabf = sb("tabf", [TP, 3, MT])
        tab_e = sb("tab_e", [TP, MT], I32)
        tab_b = sb("tab_b", [TP, MT], I32)

        w1s = expert_piece(2 * KC * HID).rearrange("p (s k h) -> p s k h", s=2, k=KC)
        hT = expert_piece(2 * HID).rearrange("p (s m n) -> p s m n", s=2, m=HC)
        xfTe = expert_piece(2 * D).rearrange("p (s k n) -> p s k n", s=2, k=KC)
        ye = expert_piece(2 * D).rearrange("p (s d) -> p s d", s=2)
        ue = expert_piece(U * D).rearrange("p (s d) -> p s d", s=U)
        tok = sb("tok", [P, U], I32)
        xfT = route_piece(2 * KC * TP).rearrange("p (s c n) -> p s c n", s=2, c=KC)

        x_in = [sem(f"x_in{c}") for c in range(NB)]
        edges_in = sem("edges_in")
        mixw_in = sem("mixw_in")
        gnnw_in = sem("gnnw_in")
        eps_in = sem("eps_in")
        ffnw_in = sem("ffnw_in")
        w2_in = sem("w2_in")
        list_zeroed = sem("list_zeroed")
        const_ready = sem("const_ready")
        dve_done = sem("dve_done")
        act_done = sem("act_done")
        var_ready = sem("var_ready")
        sd_ready = sem("sd_ready")
        xn_ready = sem("xn_ready")
        xn_stored = sem("xn_stored")
        xnT_psum = sem("xnT_psum")
        xnT_ready = sem("xnT_ready")
        agg_ready = sem("agg_ready")
        gram_psum = sem("gram_psum")
        mix_psum = sem("mix_psum")
        tl_ready = sem("tl_ready")
        ptm_ready = sem("ptm_ready")
        xbias_ready = sem("xbias_ready")
        gmin_ready = sem("gmin_ready")
        edge_psum = sem("edge_psum")
        gdiag_ready = sem("gdiag_ready")
        relmax_ready = sem("relmax_ready")
        flag_ready = sem("flag_ready")
        idx_ready = sem("idx_ready")
        turn = sem("turn")
        sp_turn = sem("sp_turn")
        msg_in = [sem(f"msg_in{r}") for r in range(RING)]
        onehot_ready = sem("onehot_ready")
        group_psum = sem("group_psum")
        group_added = sem("group_added")
        r_idx = sem("r_idx")
        r_msg = sem("r_msg")
        r_rel = sem("r_rel")
        r_onehot = sem("r_onehot")
        r_psum = sem("r_psum")
        r_cur = sem("r_cur")
        r_added = sem("r_added")
        z_psum = sem("z_psum")
        z_ready = sem("z_ready")
        y_psum = sem("y_psum")
        x1_ready = sem("x1_ready")
        var2_ready = sem("var2_ready")
        sd2_ready = sem("sd2_ready")
        u_ready = sem("u_ready")
        u_stored = sem("u_stored")
        uT_psum = sem("uT_psum")
        xfT_ready = sem("xfT_ready")
        logit_psum = sem("logit_psum")
        rank_psum = sem("rank_psum")
        pos_ready = sem("pos_ready")
        listed = sem("listed")
        count_psum = sem("count_psum")
        diff_ready = sem("diff_ready")
        exd_ready = sem("exd_ready")
        table_ready = sem("table_ready")
        tok_in = [sem(f"tok_in{s}") for s in range(U)]
        w1_in = [sem(f"w1_in{s}") for s in range(2)]
        ue_in = [sem(f"ue_in{s}") for s in range(U)]
        back_ready = sem("back_ready")
        eturn = sem("eturn")
        ueT_psum = sem("ueT_psum")
        xfTe_ready = sem("xfTe_ready")
        h_psum = sem("h_psum")
        h_ready = sem("h_ready")
        ye_psum = sem("ye_psum")
        ye_ready = sem("ye_ready")
        y_stored = [sem(f"y_stored{s}") for s in range(2)]
        FR = RING * G // 2
        yback_in = [sem(f"yback_in{s}") for s in range(FR)]
        res_ready = sem("res_ready")
        out_stored = sem("out_stored")

        x_t = x.rearrange("(t p) d -> p t d", p=TP)
        xn_t = xn_rows.rearrange("(t p) d -> p t d", p=TP)
        u_t = u_rows.rearrange("(t p) d -> p t d", p=TP)
        out_t = out.rearrange("(t p) d -> p t d", p=TP)

        picks = []
        PAIRS = [(t, min(2, NT - t)) for t in range(0, NT, 2)]
        ZG = [(t, min(4, NT - t)) for t in range(0, NT, 4)]
        CONSTS = 13
        UT, LOGIT, RANK = (6, 0), (7, 1), (2, 3)
        EPS_STEP = 1
        MIX_LOADS, GNN_LOADS, FFN_LOADS = 9, 3, 6

        block = ctx.enter_context(nc.Block())

        @block.sync
        def _(sp):
            for c in range(NB):
                sp.dma_start(xres[:, c * BT:(c + 1) * BT, :], x_t[:, c * BT:(c + 1) * BT, :]).then_inc(x_in[c], 16)
                if c == 0:
                    sp.dma_start(srct[:], src).then_inc(edges_in, 16)
                    sp.dma_start(dstt[:], dst).then_inc(edges_in, 16)
                    sp.dma_start(wt[:], edge_weight).then_inc(edges_in, 16)
            for c in range(NB):
                sp.wait_ge(xn_ready, c + 1)
                sp.dma_start(xn_t[:, c * BT:(c + 1) * BT, :], xn[:, c * BT:(c + 1) * BT, 0:D]).then_inc(xn_stored, 16)
            sp.wait_ge(const_ready, CONSTS)
            sp.dma_start(token_list.rearrange("(p k) a -> p (k a)", p=P), zlist[:]).then_inc(list_zeroed, 16)
            sp.wait_ge(mix_psum, 10)
            sp.dma_start(w2e[:].rearrange("p e c d -> p (e c) d"), W2.rearrange("e (c p) d -> p (e c) d", p=P)).then_inc(w2_in, 16)
            for b in range(NB):
                sp.wait_ge(u_ready, b + 1)
                sp.dma_start(u_t[:, b * BT:(b + 1) * BT, :], u[:, b * BT:(b + 1) * BT, :]).then_inc(u_stored, 16)

            def load_tokens(i, k):
                at = sp.value_load(tab_b[0:1, idx_slice(i, k)], min_val=0, max_val=SLOTS - P)
                if not isinstance(i, int) or i >= U:
                    sp.wait_ge(ue_in[k], (i // U if isinstance(i, int) else i[0]) * 16)
                sp.sem_inc(sp_turn, 1)
                sp.dma_start(tok[:, k:k + 1], token_list[bass.ds(at, P), :]).then_inc(tok_in[k], 16)

            def idx_slice(i, k):
                return slice(i, i + 1) if isinstance(i, int) else bass.ds(i[0] * U + k, 1)

            def num(i, k):
                return i if isinstance(i, int) else i[0] * U + k

            def load_w1(i, k):
                e = sp.value_load(tab_e[0:1, idx_slice(i, k)], min_val=0, max_val=EX - 1)
                wait_from(sp, h_psum, num(i, k) - 1)
                sp.sem_inc(sp_turn, 1)
                sp.dma_start(w1s[:, k % 2, :, :], W1.rearrange("e (k p) h -> e p k h", p=P)[bass.ds(e, 1), :, :, :].rearrange("e p k h -> p (e k) h")).then_inc(w1_in[k % 2], 16)

            def store_y(i, k):
                sp.wait_ge(ye_ready, num(i, k) + 1)
                sp.sem_inc(sp_turn, 1)
                sp.dma_start(y_rows[bass.ds(num(i, k) * P, P), :], ye[:, k % 2, :]).then_inc(y_stored[k % 2], 16)

            sp.wait_ge(table_ready, 1)
            sp.wait_ge(listed, 2 * NT * 16)
            sp.wait_ge(u_stored, NB * 16)
            sp.wait_ge(uT_psum, NT)
            load_tokens(0, 0)
            load_w1(0, 0)
            load_tokens(1, 1)

            def turn_sp(base):
                for k in range(U):
                    ahead = base * U + k + 2
                    if isinstance(base, int):
                        if ahead < MT:
                            load_tokens(ahead, (k + 2) % U)
                        if ahead - 1 < MT:
                            load_w1(ahead - 1, (k + 1) % U)
                        if base * U + k >= 1:
                            store_y(base * U + k - 1, (k - 1) % U)
                    else:
                        load_tokens((base + (k + 2) // U,), (k + 2) % U)
                        load_w1((base + (k + 1) // U,), (k + 1) % U)
                        store_y((base + (k - 1) // U,), (k - 1) % U)
            turn_sp(0)
            with sp.Fori(1, MT // U - 1) as it:
                turn_sp(it)
            turn_sp(MT // U - 1)
            store_y(MT - 1, (MT - 1) % U)

            for t in range(NT):
                sp.wait_ge(res_ready, t + 1)
                sp.dma_start(out_t[:, t, :], xres[:, t, :]).then_inc(out_stored, 16)
            sp.wait_ge(out_stored, NT * 16)

        @block.gpsimd
        def _(pool):
            def const(ins):
                ins.then_inc(const_ready, 1)
            const(pool.memset(ident[:], 0.0))
            const(pool.memset(ones[:], 1.0))
            const(pool.memset(xn[:, :, D:D + 1], 1.0))
            const(pool.memset(onesb[:], 1.0))
            const(pool.memset(hmask[:], 1.0 / N))
            const(pool.memset(tri[:], 1.0))
            pool.iota(iotaW[:], [[1, W]], base=0, channel_multiplier=0, allow_small_or_imprecise_dtypes=True)
            pool.iota(iota8[:], [[1, EX]], base=0, channel_multiplier=0, allow_small_or_imprecise_dtypes=True)
            pool.iota(eoff[:], [[STRIDE, EX]], base=0, channel_multiplier=0, allow_small_or_imprecise_dtypes=True)
            pool.iota(iotaM[:], [[1, MT]], base=0, channel_multiplier=0, allow_small_or_imprecise_dtypes=True)
            pool.iota(baseM[:], [[P, MT]], base=0, channel_multiplier=0, allow_small_or_imprecise_dtypes=True)
            const(pool.iota(tokid[:], [[TP, NT]], base=0, channel_multiplier=1))
            const(pool.memset(zlist[:], 0))
            pool.wait_ge(const_ready, 8)
            const(pool.affine_select(out=ident[:], in_=ident[:], compare_op=ALU.not_equal, fill=1.0, base=0,
                                     pattern=[[-1, P]], channel_multiplier=1))
            const(pool.affine_select(out=before[:], in_=onesb[:], compare_op=ALU.is_gt, fill=0.0, base=0,
                                     pattern=[[1, P]], channel_multiplier=-1))
            const(pool.affine_select(out=hmask[:], in_=hmask[:], compare_op=ALU.is_ge, fill=0.0, base=0,
                                     pattern=[[-DK, P // DK], [0, DK]], channel_multiplier=1))
            pool.wait_ge(const_ready, 11)
            const(pool.affine_select(out=hmask[:], in_=hmask[:], compare_op=ALU.is_ge, fill=0.0, base=DK - 1,
                                     pattern=[[DK, P // DK], [0, DK]], channel_multiplier=-1))
            const(pool.affine_select(out=tri[:], in_=tri[:], compare_op=ALU.is_ge, fill=0.0, base=0,
                                     pattern=[[1, EX], [-1, EX]], channel_multiplier=0))
            pool.memset(macc[:, 0, :], 0.0).then_inc(const_ready, 1)

            pool.wait_ge(xn_stored, NB * 16)

            def gather(g, r):
                pool.wait_ge(idx_ready, g + 1)
                pool.sem_inc(turn, 1)
                for j in range(G):
                    pool.indirect_dma_start(out=msg[:, r * G + j, :], out_offset=None, in_=xn_rows,
                                            in_offset=bass.IndirectOffsetOnAxis(ap=idxr[:, r * G + j:r * G + j + 1], axis=0)
                                            ).then_inc(msg_in[r], 16)
            for r in range(RING):
                gather(r, r)
            with pool.Fori(1, NG // RING) as it:
                for r in range(RING):
                    gather(it * RING + r, r)
            gather(NG - 1, 0)

            pool.wait_ge(flag_ready, 1)
            wide = pool.value_load(flagi[0:1, 0:1], min_val=0, max_val=1)
            with pool.If(wide == 1):
                with pool.Fori(0, NG) as g:
                    pool.wait_ge(r_idx, g + 1)
                    pool.sem_inc(turn, 1)
                    for j in range(G):
                        pool.indirect_dma_start(out=msg[:, j, :], out_offset=None, in_=xn_rows,
                                                in_offset=bass.IndirectOffsetOnAxis(ap=idxr[:, j:j + 1], axis=0)
                                                ).then_inc(r_msg, 16)

            pool.wait_ge(list_zeroed, 16)
            for b in range(NB):
                pool.wait_ge(pos_ready, b + 1)
                for t in range(b * BT, (b + 1) * BT):
                    for s in range(2):
                        pool.indirect_dma_start(out=token_list, out_offset=bass.IndirectOffsetOnAxis(ap=posi[:, s, t:t + 1], axis=0),
                                                in_=tokid[:, t:t + 1], in_offset=None).then_inc(listed, 16)

            def gather_tokens(q, k):
                i = q * U + k
                if not isinstance(q, int) or q >= 1:
                    pool.wait_ge(ueT_psum, i - U + 1)
                    pool.sem_inc(eturn, 1)
                pool.wait_ge(tok_in[k], (q + 1) * 16)
                pool.sem_inc(eturn, 1)
                pool.indirect_dma_start(out=ue[:, k, :], out_offset=None, in_=u_rows,
                                        in_offset=bass.IndirectOffsetOnAxis(ap=tok[:, k:k + 1], axis=0)).then_inc(ue_in[k], 16)
            for k in range(U):
                gather_tokens(0, k)
            with pool.Fori(1, MT // U) as it:
                for k in range(U):
                    gather_tokens(it, k)

            pool.wait_ge(back_ready, 1)
            for s in range(2):
                pool.wait_ge(y_stored[s], MT // 2 * 16)
            for t in range(NT):
                s = t % FR
                if t >= FR:
                    pool.wait_ge(res_ready, t - FR + 1)
                for a in range(2):
                    pool.indirect_dma_start(out=msg[:, 2 * s + a, :], out_offset=None, in_=y_rows,
                                            in_offset=bass.IndirectOffsetOnAxis(ap=backi[:, a, t:t + 1], axis=0)).then_inc(yback_in[s], 16)

        @block.scalar
        def _(act):
            act.dma_start(eps1[:], gnn_eps.rearrange("(a n) -> a n", a=1).broadcast_to([P, 1])).then_inc(eps_in, 16)
            for w, t in ((Wk, wk), (Wv, wv), (Wfc, wf), (Wq, wq)):
                act.dma_start(t[:, :, :], w.rearrange("(c p) i -> p c i", p=P)).then_inc(mixw_in, 16)
            for v, r in ((bk, bk_row), (bv, bv_row), (bfc, bfc_row), (gnn_b2, b2_row)):
                act.dma_start(r, v.rearrange("(a n) -> a n", a=1)).then_inc(mixw_in, 16)
            act.dma_start(bqc[:], bq).then_inc(mixw_in, 16)

            for c in range(NB):
                act.wait_ge(var_ready, c + 1)
                act.activation(sd[:, c * BT:(c + 1) * BT], veps[:, c * BT:(c + 1) * BT], ACT.Sqrt).then_inc(sd_ready, 1)
            for w, t in ((gnn_w1, gw1), (gnn_w2, gw2)):
                act.dma_start(t[:], w.rearrange("(c p) i -> p c i", p=P)).then_inc(gnnw_in, 16)
            act.dma_start(gb1[:], gnn_b1).then_inc(gnnw_in, 16)
            act.dma_start(gammaT[:], gamma).then_inc(ffnw_in, 16)
            act.dma_start(betaT[:], beta).then_inc(ffnw_in, 16)
            act.dma_start(wr[:], Wr.rearrange("(c p) e -> p c e", p=P)).then_inc(ffnw_in, 16)
            act.dma_start(brb[:], br.rearrange("(a n) -> a n", a=1).broadcast_to([P, EX])).then_inc(ffnw_in, 16)
            act.dma_start(b1T[:], b1).then_inc(ffnw_in, 16)
            act.dma_start(b2e[:].rearrange("p e d -> p (e d)"),
                          b2.rearrange("e d -> (e d)").rearrange("(a n) -> a n", a=1).broadcast_to([P, EX * D])).then_inc(ffnw_in, 16)

            def copy_idx(g, r):
                act.activation(idxr[:, r * G:(r + 1) * G], srct[:, bass.ds(g * G, G)], ACT.Copy).then_inc(idx_ready, 1)
            act.wait_ge(edges_in, 48)
            for r in range(RING):
                copy_idx(r, r)

            act.wait_ge(dve_done, EPS_STEP)
            for n, (t0, nt) in enumerate(PAIRS):
                act.wait_ge(xnT_psum, n + 1)
                v = bank[n % 2][:, 0:KC * nt * TP].rearrange("p (c n) -> p c n", c=KC)
                cols = slice(t0 * TP, (t0 + nt) * TP)
                act.activation(xnT[:, :, cols], v, ACT.Copy)
                act.activation(aggT[:, :, cols], v, ACT.Identity, scale=eps1[:, 0:1]).then_inc(xnT_ready, 1)

            def evac(n, o, i):
                act.wait_ge(mix_psum, n)
                act.activation(o, i, ACT.Copy).then_inc(act_done, 1)
            evac(1, wkT[:, :, :].rearrange("p c i -> p (c i)"), bank[4][:, :])
            evac(2, wvT[:, :, :].rearrange("p c i -> p (c i)"), bank[2 + 3][:, :])
            evac(3, wfT[:, :, :].rearrange("p c i -> p (c i)"), bank[4][:, :])
            act.wait_ge(gram_psum, 1)
            act.activation(gram[:, 0, :], bank[2][:, 0:D + 1], ACT.Copy)
            act.activation(gram[:, 1, :], bank[3][:, 0:D + 1], ACT.Copy).then_inc(act_done, 1)
            evac(4, s_row, bank[4][0:1, 0:D])
            evac(5, t1[:, :, :].rearrange("p c i -> p (c i)"), bank[0][:, :])
            evac(7, a2[:, :, :].rearrange("p c i -> p (c i)"), bank[2][:, :])
            evac(8, mixm[:].rearrange("p c i -> p (c i)"), bank[3][:, :])
            evac(9, bias_row, bank[4][0:1, 0:D])

            with act.Fori(1, NG // RING) as it:
                for r in range(RING):
                    g = it * RING + r
                    act.wait_ge(group_psum, g - RING + 1)
                    copy_idx(g, r)
            act.wait_ge(group_psum, NG - RING)
            copy_idx(NG - 1, 0)

            act.wait_ge(flag_ready, 1)
            wide = act.value_load(flagi[0:1, 0:1], min_val=0, max_val=1)
            with act.If(wide == 1):
                act.wait_ge(group_psum, NG)
                act.activation(idxr[:, 0:G], srct[:, 0:G], ACT.Copy).then_inc(r_idx, 1)
                with act.Fori(1, NG) as g:
                    act.wait_ge(r_psum, g * (NWIN - 1))
                    act.activation(idxr[:, 0:G], srct[:, bass.ds(g * G, G)], ACT.Copy).then_inc(r_idx, 1)

            act.wait_ge(gnnw_in, GNN_LOADS * 16)
            for n, (t0, nt) in enumerate(ZG):
                act.wait_ge(z_psum, n + 1)
                for m in range(KC):
                    ins = act.activation(aggT[:, m, t0 * TP:(t0 + nt) * TP], bank[2 * (n % 2) + m][:, 0:nt * TP], ACT.Relu,
                                         bias=gb1[:, m:m + 1])
                ins.then_inc(z_ready, 1)

            act.wait_ge(ffnw_in, FFN_LOADS * 16)
            for b in range(NB + 1):
                if b < NB:
                    for s in range(2):
                        act.wait_ge(var2_ready, 2 * b + s + 1)
                        act.activation(sd2[:, s, b * BT:(b + 1) * BT], veps2[:, s, b * BT:(b + 1) * BT], ACT.Sqrt).then_inc(sd2_ready, 1)
                if b >= 1:
                    for t in range((b - 1) * BT, b * BT):
                        act.wait_ge(uT_psum, t + 1)
                        if t >= 2:
                            act.wait_ge(logit_psum, t - 1)
                        for c in range(KC):
                            ins = act.activation(xfT[:, t % 2, c, :], bank[UT[t % 2]][:, c * P:c * P + TP], ACT.Identity,
                                                 scale=gammaT[:, c:c + 1], bias=betaT[:, c:c + 1])
                        ins.then_inc(xfT_ready, 1)
            act.wait_ge(diff_ready, 1)
            act.activation(exd[:], diff[:], ACT.Exp).then_inc(exd_ready, 1)

            act.wait_ge(table_ready, 1)

            def gelu(q, k):
                i = q * U + k
                e = act.value_load(tab_e[0:1, slice(i, i + 1) if isinstance(i, int) else bass.ds(i, 1)], min_val=0, max_val=EX - 1)
                wait_from(act, ye_psum, i - 1)
                act.wait_ge(h_psum, i + 1)
                for m in range(HC):
                    ins = act.activation(hT[:, k % 2, m, :], bank[2 + k % 2][:, m * P:(m + 1) * P], ACT.Gelu,
                                         bias=b1T[:, bass.ds(e * HC + m, 1)])
                ins.then_inc(h_ready, 1)
            for k in range(U):
                gelu(0, k)
            with act.Fori(1, MT // U) as it:
                for k in range(U):
                    gelu(it, k)



        @block.vector
        def _(dve):
            steps = [0]
            pick_done = picks

            def link(ins):
                steps[0] += 1
                ins.then_inc(dve_done, 1)
                dve.wait_ge(dve_done, steps[0])

            dve.wait_ge(eps_in, 16)
            link(dve.tensor_scalar(eps1[:], eps1[:], 1.0, None, ALU.add))

            for c in range(NB):
                ts = slice(c * BT, (c + 1) * BT)
                dve.wait_ge(x_in[c], 16)
                for t in range(c * BT, (c + 1) * BT):
                    ins = dve.bn_stats(st[:, t, :], xres[:, t, :])
                link(ins)
                for t in range(c * BT, (c + 1) * BT):
                    ins = dve.bn_aggr(mv[:, t, :], st[:, t, :])
                link(ins)
                dve.tensor_scalar(veps[:, ts], mv[:, ts, 1], LN_EPS, None, ALU.add).then_inc(var_ready, 1)
                dve.wait_ge(sd_ready, c + 1)
                link(dve.reciprocal(rs[:, ts], sd[:, ts]))
                for t in range(c * BT, (c + 1) * BT):
                    ins = dve.tensor_scalar(xn[:, t, 0:D], xres[:, t, :], mv[:, t, 0:1], rs[:, t:t + 1], ALU.subtract, ALU.mult)
                ins.then_inc(xn_ready, 1)

            dve.wait_ge(const_ready, CONSTS + 1)
            dve.wait_ge(edges_in, 48)
            link(dve.tensor_copy(dstf[:].rearrange("p g j -> p (g j)"), dstt[:]))
            dve.tensor_reduce(gmin[:], dstf[:], AX_X, ALU.min).then_inc(gmin_ready, 1)
            dve.wait_ge(edge_psum, 1)
            link(dve.tensor_reduce(gminT[:], bank[5][0:NG, 0:EP], AX_X, ALU.min))
            dve.tensor_scalar(gdiag[:], ident[0:NG, 0:NG], gminT[:, 0:1], None, ALU.mult).then_inc(gdiag_ready, 1)
            dve.wait_ge(edge_psum, 2)
            dve.tensor_copy(basei[:], bank[5][0:1, P:P + NG])
            link(dve.tensor_copy(basef[:], bank[5][0:EP, P:P + NG]))
            link(dve.tensor_tensor(rel[:], dstf[:], basef[:].unsqueeze(2).broadcast_to([EP, NG, G]), ALU.subtract))
            dve.tensor_reduce(relmax[:], rel[:].rearrange("p g j -> p (g j)"), AX_X, ALU.max).then_inc(relmax_ready, 1)
            dve.wait_ge(edge_psum, 3)
            link(dve.tensor_reduce(flagf[:, 0:1], bank[5][0:1, 256:256 + EP], AX_X, ALU.max))
            dve.tensor_scalar(flagi[:], flagf[:, 0:1], float(W), None, ALU.is_ge).then_inc(flag_ready, 1)

            rel_flat = rel[:].rearrange("p g j -> p (g j)")

            def onehots(g, b):
                for j in range(G):
                    ins = dve.tensor_scalar(onehot[:, b * G + j, :], iotaW[0:EP, :], rel_flat[:, bass.ds(g * G + j, 1)],
                                            wt[:, bass.ds(g * G + j, 1)], ALU.is_equal, ALU.mult)
                ins.then_inc(onehot_ready, 1)

            def add_window(g, b):
                base = dve.value_load(basei[0:1, bass.ds(g, 1)], min_val=0, max_val=N - 1)
                window = aggT[:, :, bass.ds(base, W)]
                dve.tensor_tensor(window, window, bank[6 + b][:, :].rearrange("p (c n) -> p c n", c=KC)[:, :, 0:W],
                                  ALU.add).then_inc(group_added, 1)

            onehots(0, 0)
            onehots(1, 1)
            dve.wait_ge(mix_psum, 5)
            dve.scalar_tensor_tensor(out=tl_row, in0=bk_row, scalar=float(N), in1=bank[1][0:1, 0:D], op0=ALU.mult,
                                     op1=ALU.add).then_inc(tl_ready, 1)
            dve.wait_ge(mix_psum, 6)
            for c in range(KC):
                ins = dve.tensor_tensor(ptm[:, c, :], bank[1][:, 256 + c * P:256 + (c + 1) * P], hmask[:].rearrange("p b d -> p (b d)"), ALU.mult)
            ins.then_inc(ptm_ready, 1)
            dve.memset(aggT[:, :, N:N + W], 0.0)
            dve.wait_ge(mix_psum, 10)
            link(dve.tensor_tensor(xres[:], xres[:], bank[4][0:TP, 256:256 + D].unsqueeze(1).broadcast_to([TP, NT, D]), ALU.add))

            dve.wait_ge(xnT_ready, len(PAIRS))
            dve.wait_ge(group_psum, 1)
            onehots(2, 0)
            add_window(0, 0)
            with dve.Fori(0, (NG - 3) // 2) as it:
                for k in range(2):
                    g = it * 2 + (k + 1)
                    b = (k + 1) % 2
                    dve.wait_ge(group_psum, g + 1)
                    onehots(g + 2, b)
                    dve.wait_ge(group_added, g)
                    add_window(g, b)
            for g in (NG - 2, NG - 1):
                dve.wait_ge(group_psum, g + 1)
                dve.wait_ge(group_added, g)
                add_window(g, g % 2)

            wide = dve.value_load(flagi[0:1, 0:1], min_val=0, max_val=1)
            with dve.If(wide == 1):
                dve.wait_ge(group_added, NG)
                with dve.Fori(0, NG) as g:
                    dve.tensor_copy(relq[:], rel_flat[:, bass.ds(g * G, G)]).then_inc(r_rel, 1)
                    dve.tensor_copy(curf[:], basef[0:1, bass.ds(g, 1)]).then_inc(r_rel, 1)
                    with dve.Fori(0, NWIN - 1) as q:
                        n = g * (NWIN - 1) + q
                        c = g * 2 + n * 2 + 2
                        dve.wait_ge(r_rel, c)
                        dve.tensor_scalar(relq[:], relq[:], float(W), None, ALU.subtract).then_inc(r_rel, 1)
                        dve.tensor_scalar(curf[:], curf[:], float(W), float(N), ALU.add, ALU.min).then_inc(r_rel, 1)
                        dve.wait_ge(r_rel, c + 2)
                        dve.tensor_copy(curi[:], curf[:]).then_inc(r_cur, 1)
                        for j in range(G):
                            ins = dve.tensor_scalar(onehot[:, j, :], iotaW[0:EP, :], relq[:, j:j + 1],
                                                    wt[:, bass.ds(g * G + j, 1)], ALU.is_equal, ALU.mult)
                        ins.then_inc(r_onehot, 1)
                        dve.wait_ge(r_cur, n + 1)
                        dve.sem_inc(turn, 1)
                        base = dve.value_load(curi[0:1, 0:1], min_val=0, max_val=N)
                        dve.wait_ge(r_psum, n + 1)
                        window = aggT[:, :, bass.ds(base, W)]
                        dve.tensor_tensor(window, window, bank[6][:, :].rearrange("p (c n) -> p c n", c=KC)[:, :, 0:W],
                                          ALU.add).then_inc(r_added, 1)
                        dve.wait_ge(r_added, n + 1)

            def x1_and_u(b):
                ts = slice(b * BT, (b + 1) * BT)
                for t in range(b * BT, (b + 1) * BT):
                    dve.wait_ge(y_psum, t + 1)
                    ins = dve.tensor_tensor(xres[:, t, :], xres[:, t, :],
                                            bank[4 + t % 2][0:TP, 0:D], ALU.add)
                    ins.then_inc(x1_ready, 1)
                dve.wait_ge(x1_ready, (b + 1) * BT)
                for t in range(b * BT, (b + 1) * BT):
                    ins = dve.bn_stats(st2[:, t, :], xres[:, t, :])
                link(ins)
                for t in range(b * BT, (b + 1) * BT):
                    ins = dve.bn_aggr(mv2[:, t, :], st2[:, t, :])
                link(ins)
                dve.tensor_scalar(veps2[:, 0, ts], mv2[:, ts, 1], LN_EPS, None, ALU.add).then_inc(var2_ready, 1)
                dve.wait_ge(sd2_ready, 2 * b + 1)
                link(dve.reciprocal(rs2[:, 0, ts], sd2[:, 0, ts]))
                link(dve.tensor_tensor(rs2[:, 1, ts], rs2[:, 0, ts], rs2[:, 0, ts], ALU.mult))
                link(dve.tensor_tensor(rs2[:, 2, ts], rs2[:, 1, ts], mv2[:, ts, 1], ALU.mult))
                dve.tensor_scalar(veps2[:, 1, ts], rs2[:, 2, ts], LN_EPS, None, ALU.add).then_inc(var2_ready, 1)
                dve.wait_ge(sd2_ready, 2 * b + 2)
                link(dve.reciprocal(rs2[:, 1, ts], sd2[:, 1, ts]))
                link(dve.tensor_tensor(rs2[:, 2, ts], rs2[:, 0, ts], rs2[:, 1, ts], ALU.mult))
                for t in range(b * BT, (b + 1) * BT):
                    ins = dve.tensor_scalar(u[:, t, :], xres[:, t, :], mv2[:, t, 0:1], rs2[:, 2, t:t + 1], ALU.subtract, ALU.mult)
                ins.then_inc(u_ready, 1)

            def top2(b):
                ts = slice(b * BT, (b + 1) * BT)
                dve.wait_ge(logit_psum, (b + 1) * BT)
                link(dve.tensor_tensor(lg[:, ts, :], bank[LOGIT[b % 2]][0:TP, 0:BT * EX].rearrange("p (t e) -> p t e", e=EX),
                                       brb[0:TP, :].unsqueeze(1).broadcast_to([TP, BT, EX]), ALU.add))
                for t in range(b * BT, (b + 1) * BT):
                    ins = dve.max(mx[:, t, :], lg[:, t, :])
                link(ins)
                for t in range(b * BT, (b + 1) * BT):
                    ins = dve.max_index(ix[:, t, :], mx[:, t, :], lg[:, t, :])
                link(ins)
                link(dve.tensor_copy(ixf[:, ts, :], ix[:, ts, 0:2]))
                for s in range(2):
                    ins = dve.tensor_tensor(pick[:, s, ts, :], iota8[0:TP, :].unsqueeze(1).broadcast_to([TP, BT, EX]),
                                            ixf[:, ts, s:s + 1].broadcast_to([TP, BT, EX]), ALU.is_equal)
                link(ins)
                ins = dve.tensor_tensor(m12[:, ts, :], pick[:, 0, ts, :], pick[:, 1, ts, :], ALU.add)
                link(ins)
                for t in range(b * BT, (b + 1) * BT):
                    link(dve.tensor_tensor(macc[:, t + 1, :], macc[:, t, :], m12[:, t, :], ALU.add))
                pick_done.append(steps[0])

            def positions(b):
                ts = slice(b * BT, (b + 1) * BT)
                dve.wait_ge(rank_psum, b + 1)
                link(dve.tensor_tensor(pp[:, ts, :], bank[RANK[b % 2]][0:TP, 0:BT * EX].rearrange("p (t e) -> p t e", e=EX),
                                       eoff[0:TP, :].unsqueeze(1).broadcast_to([TP, BT, EX]), ALU.add))
                for s in range(2):
                    ins = dve.tensor_tensor(ppm[:, s, ts, :], pp[:, ts, :], pick[:, s, ts, :], ALU.mult)
                link(ins)
                for s in range(2):
                    ins = dve.tensor_reduce(posf[:, s, ts], ppm[:, s, ts, :], AX_X, ALU.add)
                link(ins)
                for s in range(2):
                    ins = dve.tensor_copy(posi[:, s, ts], posf[:, s, ts])
                ins.then_inc(pos_ready, 1)

            dve.wait_ge(ffnw_in, FFN_LOADS * 16)
            for b in range(NB + 2):
                if b < NB:
                    x1_and_u(b)
                if 1 <= b <= NB:
                    top2(b - 1)
                if b >= 2:
                    positions(b - 2)

            dve.tensor_tensor(diff[:], mx[:, :, 1], mx[:, :, 0], ALU.subtract).then_inc(diff_ready, 1)
            dve.wait_ge(count_psum, 1)
            link(dve.tensor_scalar(cnti[:, 0, :], bank[RANK[0]][0:TP, 448:448 + EX], float(P - 1), None, ALU.add))
            link(dve.tensor_scalar(cnti[:, 1, :], cnti[:, 0, :], P.bit_length() - 1, None, ALU.logical_shift_right))
            link(dve.tensor_copy(cntf[:, 0, :], cnti[:, 1, :]))
            dve.tensor_scalar(cntf[:, 2, :], cntf[:, 0, :], -float(P), float(STRIDE), ALU.mult, ALU.add)
            link(dve.tensor_tensor(trin[:, :, :], cntf[:, 0, :].unsqueeze(1).broadcast_to([TP, EX, EX]), tri[0:TP, :, :], ALU.mult))
            link(dve.tensor_reduce(cntf[:, 1, :], trin[:, :, :], AX_X, ALU.add))
            link(dve.tensor_tensor(cond[:, 0, :, :], cntf[:, 1, :].unsqueeze(1).broadcast_to([TP, MT, EX]),
                                   iotaM[0:TP, :].unsqueeze(2).broadcast_to([TP, MT, EX]), ALU.is_le))
            dve.tensor_reduce(tabf[:, 0, :], cond[:, 0, :, :], AX_X, ALU.add)
            link(dve.tensor_tensor(cond[:, 1, :, :], cond[:, 0, :, :], cntf[:, 2, :].unsqueeze(1).broadcast_to([TP, MT, EX]), ALU.mult))
            link(dve.tensor_reduce(tabf[:, 1, :], cond[:, 1, :, :], AX_X, ALU.add))
            dve.tensor_scalar(tab_e[:], tabf[:, 0, :], float(EX - 1), None, ALU.min)
            link(dve.tensor_tensor(tabf[:, 2, :], tabf[:, 1, :], baseM[0:TP, :], ALU.add))
            dve.tensor_copy(tab_b[:], tabf[:, 2, :]).then_inc(table_ready, 1)
            link(dve.tensor_tensor(cntf[:, 3, :], cntf[:, 1, :], cntf[:, 0, :], ALU.subtract))
            link(dve.scalar_tensor_tensor(out=cntf[:, 4, :], in0=cntf[:, 3, :], scalar=-float(P), in1=eoff[0:TP, :],
                                          op0=ALU.mult, op1=ALU.add))
            flat = ppm.rearrange("p s t e -> p (s t) e")
            link(dve.tensor_tensor(flat, pick[:].rearrange("p s t e -> p (s t) e"),
                                   cntf[:, 4, :].unsqueeze(1).broadcast_to([TP, 2 * NT, EX]), ALU.mult))
            link(dve.tensor_reduce(backf[:, 0, :, :].rearrange("p s t -> p (s t)"), flat, AX_X, ALU.add))
            link(dve.tensor_tensor(backf[:, 1, :, :], posf[:], backf[:, 0, :, :], ALU.subtract))
            dve.tensor_copy(backi[:], backf[:, 1, :, :]).then_inc(back_ready, 1)
            dve.wait_ge(exd_ready, 1)
            link(dve.tensor_scalar(den[:], exd[:], 1.0, None, ALU.add))
            link(dve.reciprocal(wtop[:, 0, :], den[:]))
            link(dve.tensor_tensor(wtop[:, 1, :], wtop[:, 0, :], exd[:], ALU.mult))
            dve.wait_ge(table_ready, 1)

            dve.wait_ge(u_stored, NB * 16)
            dve.wait_ge(uT_psum, NT)

            def evac_xfT(q, k):
                i = q * U + k
                wait_from(dve, h_psum, i - 1)
                dve.wait_ge(ueT_psum, i + 1)
                for c in range(KC):
                    ins = dve.tensor_scalar(xfTe[:, k % 2, c, :], bank[k % 2][:, c * P:(c + 1) * P], gammaT[:, c:c + 1],
                                            betaT[:, c:c + 1], ALU.mult, ALU.add)
                ins.then_inc(xfTe_ready, 1)

            def evac_y(q, k):
                i = q * U + k
                e = dve.value_load(tab_e[0:1, slice(i, i + 1) if isinstance(i, int) else bass.ds(i, 1)], min_val=0, max_val=EX - 1)
                if not isinstance(q, int) or i >= 2:
                    dve.wait_ge(y_stored[k % 2], (q * (U // 2) + k // 2) * 16)
                dve.wait_ge(ye_psum, i + 1)
                dve.tensor_tensor(ye[:, k % 2, :], bank[4 + k % 2][:, 0:D], b2e[:, bass.ds(e, 1), :].rearrange("p a d -> p (a d)"),
                                  ALU.add).then_inc(ye_ready, 1)

            evac_xfT(0, 0)

            def turn_dve(q, last=False):
                for k in range(U):
                    if not (last and k == U - 1):
                        evac_xfT(q + (k + 1) // U, (k + 1) % U)
                    if not (isinstance(q, int) and q == 0 and k == 0):
                        evac_y(q + (k - 1) // U, (k - 1) % U)
            turn_dve(0)
            with dve.Fori(1, MT // U - 1) as it:
                turn_dve(it)
            turn_dve(MT // U - 1, last=True)
            evac_y(MT // U - 1, U - 1)

            for t in range(NT):
                s = t % FR
                dve.wait_ge(yback_in[s], (t // FR + 1) * 32)
                for a in range(2):
                    ins = dve.scalar_tensor_tensor(out=xres[:, t, :], in0=msg[:, 2 * s + a, :], scalar=wtop[:, a, t:t + 1],
                                                   in1=xres[:, t, :], op0=ALU.mult, op1=ALU.add)
                    if a == 0:
                        link(ins)
                ins.then_inc(res_ready, 1)

        @block.tensor
        def _(pe):
            pe.wait_ge(const_ready, CONSTS)
            for n, (t0, nt) in enumerate(PAIRS):
                if n >= 2:
                    pe.wait_ge(xnT_ready, n - 1)
                for t in range(t0, t0 + nt):
                    if t % BT == 0 or t == t0:
                        pe.wait_ge(xn_ready, t // BT + 1)
                    for c in range(KC):
                        o = c * nt * TP + (t - t0) * TP
                        ins = pe.transpose(bank[n % 2][:, o:o + TP], xn[:, t, c * P:(c + 1) * P], ident[0:TP, 0:TP])
                ins.then_inc(xnT_psum, 1)
                for t in range(t0, t0 + nt):
                    for m in range(KC):
                        ins = pe.matmul(bank[2 + m][:, 0:D + 1], xn[:, t, m * P:(m + 1) * P], xn[:, t, :],
                                        start=(t == 0), stop=(t == NT - 1))
            ins.then_inc(gram_psum, 1)

            pe.wait_ge(gmin_ready, 1)
            pe.transpose(bank[5][0:NG, 0:EP], gmin[:], ident[0:EP, 0:EP]).then_inc(edge_psum, 1)
            pe.wait_ge(gdiag_ready, 1)
            pe.matmul(bank[5][0:EP, P:P + NG], ones[0:NG, 0:EP], gdiag[:], start=True, stop=True).then_inc(edge_psum, 1)
            pe.wait_ge(relmax_ready, 1)
            pe.transpose(bank[5][0:1, 256:256 + EP], relmax[:], ident[0:EP, 0:EP]).then_inc(edge_psum, 1)

            pe.wait_ge(mixw_in, MIX_LOADS * 16)

            def transposed(w, b):
                for ci in range(KC):
                    for co in range(KC):
                        ins = pe.transpose(b[:, ci * D + co * P:ci * D + (co + 1) * P], w[:, co, ci * P:(ci + 1) * P], ident[:])
                ins.then_inc(mix_psum, 1)
            transposed(wk, bank[4])
            pe.wait_ge(flag_ready, 1)
            transposed(wv, bank[5])
            pe.wait_ge(act_done, 1)
            transposed(wf, bank[4])
            pe.wait_ge(act_done, 4)
            for c in range(KC):
                ins = pe.transpose(bank[4][0:1, c * P:(c + 1) * P], gram[:, c, D:D + 1], ident[:])
            ins.then_inc(mix_psum, 1)
            pe.wait_ge(act_done, 5)
            pe.wait_ge(xnT_ready, len(PAIRS))
            for c in range(KC):
                for k in range(KC):
                    pe.matmul(bank[0][:, c * D:(c + 1) * D], gram[:, k, c * P:(c + 1) * P], wkT[:, k, :], start=(k == 0), stop=False)
                pe.matmul(bank[0][:, c * D:(c + 1) * D], s_row[:, c * P:(c + 1) * P], bk_row, start=False, stop=True)
            for k in range(KC):
                ins = pe.matmul(bank[1][0:1, 0:D], gram[:, k, D:D + 1], wkT[:, k, :], start=(k == 0), stop=(k == KC - 1))
            ins.then_inc(mix_psum, 1)
            pe.wait_ge(act_done, 6)
            pe.wait_ge(tl_ready, 1)
            for c in range(KC):
                cs = slice(c * P, (c + 1) * P)
                o = bank[1][:, 256 + c * P:256 + (c + 1) * P]
                for k in range(KC):
                    pe.matmul(o, wvT[:, k, cs], t1[:, k, cs], start=(k == 0), stop=False)
                ins = pe.matmul(o, bv_row[:, cs], tl_row[:, cs], start=False, stop=True)
            ins.then_inc(mix_psum, 1)
            pe.wait_ge(ptm_ready, 1)
            for c in range(KC):
                ins = pe.matmul(bank[2][:, c * D:(c + 1) * D], ptm[:, c, :], wfT[:, c, :], start=True, stop=True)
            ins.then_inc(mix_psum, 1)
            pe.wait_ge(act_done, 7)
            for c in range(KC):
                for k in range(KC):
                    ins = pe.matmul(bank[3][:, c * D:(c + 1) * D], wq[:, k, c * P:(c + 1) * P], a2[:, k, :], start=(k == 0), stop=(k == KC - 1))
            ins.then_inc(mix_psum, 1)
            for k in range(KC):
                pe.matmul(bank[4][0:1, 0:D], bqc[:, k:k + 1], a2[:, k, :], start=(k == 0), stop=False)
            pe.matmul(bank[4][0:1, 0:D], ones[0:1, 0:1], bfc_row, start=False, stop=False)
            pe.matmul(bank[4][0:1, 0:D], ones[0:1, 0:1], b2_row, start=False, stop=True).then_inc(mix_psum, 1)
            pe.wait_ge(act_done, 9)
            pe.matmul(bank[4][0:TP, 256:256 + D], ones[0:1, 0:TP], bias_row, start=True, stop=True).then_inc(mix_psum, 1)

            def group(g, r, b):
                pe.wait_ge(onehot_ready, g + 1)
                for c in range(KC):
                    for j in range(G):
                        ins = pe.matmul(bank[6 + b][:, c * 256:c * 256 + W], msg[:, r * G + j, c * P:(c + 1) * P],
                                        onehot[:, b * G + j, :], start=(j == 0), stop=(j == G - 1))
                ins.then_inc(group_psum, 1)
            for r in range(RING):
                pe.wait_ge(msg_in[r], 16 * G)
                wait_from(pe, group_added, r - 1)
                group(r, r, r % 2)
            with pe.Fori(1, NG // RING) as it:
                for r in range(RING):
                    pe.wait_ge(msg_in[r], (it + 1) * (16 * G))
                    pe.wait_ge(group_added, it * RING + (r - 1))
                    group(it * RING + r, r, r % 2)
            pe.wait_ge(msg_in[0], (NG // RING + 1) * 16 * G)
            pe.wait_ge(group_added, NG - 2)
            group(NG - 1, 0, 0)

            wide = pe.value_load(flagi[0:1, 0:1], min_val=0, max_val=1)
            with pe.If(wide == 1):
                with pe.Fori(0, NG) as g:
                    pe.wait_ge(r_msg, (g + 1) * (16 * G))
                    pe.sem_inc(turn, 1)
                    with pe.Fori(0, NWIN - 1) as q:
                        n = g * (NWIN - 1) + q
                        pe.wait_ge(r_onehot, n + 1)
                        for c in range(KC):
                            for j in range(G):
                                ins = pe.matmul(bank[6][:, c * 256:c * 256 + W], msg[:, j, c * P:(c + 1) * P],
                                                onehot[:, j, :], start=(j == 0), stop=(j == G - 1))
                        ins.then_inc(r_psum, 1)
                pe.wait_ge(r_added, NG * (NWIN - 1))

            pe.wait_ge(group_added, NG)
            pe.wait_ge(gnnw_in, GNN_LOADS * 16)
            for n, (t0, nt) in enumerate(ZG):
                wait_from(pe, z_ready, n - 1)
                cols = slice(t0 * TP, (t0 + nt) * TP)
                for m in range(KC):
                    for k in range(KC):
                        ins = pe.matmul(bank[2 * (n % 2) + m][:, 0:nt * TP], gw1[:, k, m * P:(m + 1) * P], aggT[:, k, cols],
                                        start=(k == 0), stop=(k == KC - 1))
                ins.then_inc(z_psum, 1)

            def y_tile(t):
                pe.wait_ge(z_ready, t // 4 + 1)
                wait_from(pe, x1_ready, t - 1)
                o = bank[4 + t % 2][0:TP, 0:D]
                cols = slice(t * TP, (t + 1) * TP)
                for k in range(KC):
                    pe.matmul(o, aggT[:, k, cols], gw2[:, k, :], start=(k == 0), stop=False)
                for k in range(KC):
                    ins = pe.matmul(o, xnT[:, k, cols], mixm[:, k, :], start=False, stop=(k == KC - 1))
                ins.then_inc(y_psum, 1)

            def transposes(t):
                pe.wait_ge(u_ready, t // BT + 1)
                pe.wait_ge(z_ready, len(ZG))
                wait_from(pe, xfT_ready, t - 1)
                for c in range(KC):
                    ins = pe.transpose(bank[UT[t % 2]][:, c * P:c * P + TP], u[:, t, c * P:(c + 1) * P], ident[0:TP, 0:TP])
                ins.then_inc(uT_psum, 1)

            def logits(t):
                b = t // BT
                pe.wait_ge(xfT_ready, t + 1)
                o = t % BT * EX
                for c in range(KC):
                    ins = pe.matmul(bank[LOGIT[b % 2]][0:TP, o:o + EX], xfT[:, t % 2, c, :], wr[:, c, :], start=(c == 0), stop=(c == KC - 1))
                ins.then_inc(logit_psum, 1)

            def ranks(b):
                rank = bank[RANK[b % 2]]
                flat = m12[:, b * BT:(b + 1) * BT, :].rearrange("p t e -> p (t e)")
                pe.wait_ge(dve_done, picks[b])
                pe.matmul(rank[0:TP, 0:BT * EX], before[0:TP, 0:TP], flat, start=True, stop=False)
                pe.matmul(rank[0:TP, 0:BT * EX], onesb[0:TP, 0:TP],
                          macc[:, b * BT:(b + 1) * BT, :].rearrange("p t e -> p (t e)"), start=False, stop=True).then_inc(rank_psum, 1)

            for b in range(NB + 2):
                if b < NB:
                    for t in range(b * BT, (b + 1) * BT):
                        y_tile(t)
                if 1 <= b <= NB:
                    wait_from(pe, pos_ready, b - 2)
                    for t in range((b - 1) * BT, b * BT):
                        transposes(t)
                        if t > (b - 1) * BT:
                            logits(t - 1)
                    logits(b * BT - 1)
                if b >= 2:
                    ranks(b - 2)
            pe.wait_ge(diff_ready, 1)
            pe.matmul(bank[RANK[0]][0:TP, 448:448 + EX], onesb[0:TP, 0:TP], macc[:, NT, :], start=True, stop=True).then_inc(count_psum, 1)

            pe.wait_ge(w2_in, 16)
            pe.wait_ge(table_ready, 1)

            def u_transposes(q, k):
                i = q * U + k
                wait_from(pe, xfTe_ready, i - 1)
                pe.wait_ge(ue_in[k], (q + 1) * 16)
                for c in range(KC):
                    ins = pe.transpose(bank[k % 2][:, c * P:(c + 1) * P], ue[:, k, c * P:(c + 1) * P], ident[:])
                ins.then_inc(ueT_psum, 1)

            def first_layer(q, k):
                i = q * U + k
                pe.wait_ge(xfTe_ready, i + 1)
                wait_from(pe, h_ready, i - 1)
                pe.wait_ge(w1_in[k % 2], (q * (U // 2) + k // 2 + 1) * 16)
                for m in range(HC):
                    for c in range(KC):
                        ins = pe.matmul(bank[2 + k % 2][:, m * P:(m + 1) * P], w1s[:, k % 2, c, m * P:(m + 1) * P], xfTe[:, k % 2, c, :],
                                        start=(c == 0), stop=(c == KC - 1))
                ins.then_inc(h_psum, 1)

            def second_layer(q, k):
                i = q * U + k
                e = pe.value_load(tab_e[0:1, slice(i, i + 1) if isinstance(i, int) else bass.ds(i, 1)], min_val=0, max_val=EX - 1)
                pe.wait_ge(h_ready, i + 1)
                wait_from(pe, ye_ready, i - 1)
                for m in range(HC):
                    ins = pe.matmul(bank[4 + k % 2][:, 0:D], hT[:, k % 2, m, :], w2e[:, bass.ds(e, 1), m, :].rearrange("p a d -> p (a d)"),
                                    start=(m == 0), stop=(m == HC - 1))
                ins.then_inc(ye_psum, 1)

            u_transposes(0, 0)

            def turn_pe(q, last=False):
                for k in range(U):
                    first_layer(q, k)
                    if not (last and k == U - 1):
                        u_transposes(q + (k + 1) // U, (k + 1) % U)
                    if not (isinstance(q, int) and q == 0 and k == 0):
                        second_layer(q + (k - 1) // U, (k - 1) % U)
            turn_pe(0)
            with pe.Fori(1, MT // U - 1) as it:
                turn_pe(it)
            turn_pe(MT // U - 1, last=True)
            second_layer(MT // U - 1, U - 1)


def kernel(**inputs):
    import numpy as _np
    import concourse.bacc as _bacc
    from concourse import mybir as _mybir
    from concourse.bass_utils import run_bass_kernel_spmd as _run

    def cols(a, p):
        return _np.ascontiguousarray(_np.asarray(a).reshape(-1, p).T)

    plain = {k: _np.ascontiguousarray(v) for k, v in inputs.items()}
    laid = {
        "x": plain["x"],
        "src": cols(plain["src"], EP), "dst": cols(plain["dst"], EP), "edge_weight": cols(plain["edge_weight"], EP),
        "gnn_eps": plain["L0_gnn_eps"], "gnn_w1": plain["L0_gnn_w1"], "gnn_b1": cols(plain["L0_gnn_b1"], P),
        "gnn_w2": plain["L0_gnn_w2"], "gnn_b2": plain["L0_gnn_b2"],
        "Wq": plain["L0_mix_Wq"], "bq": cols(plain["L0_mix_bq"], P),
        "Wk": plain["L0_mix_Wk"], "bk": plain["L0_mix_bk"],
        "Wv": plain["L0_mix_Wv"], "bv": plain["L0_mix_bv"],
        "Wfc": plain["L0_mix_Wfc"], "bfc": plain["L0_mix_bfc"],
        "gamma": cols(plain["L0_ffn_gamma"], P), "beta": cols(plain["L0_ffn_beta"], P),
        "Wr": plain["L0_ffn_Wr"], "br": plain["L0_ffn_br"],
        "W1": plain["L0_ffn_W1"], "b1": cols(plain["L0_ffn_b1"], P),
        "W2": plain["L0_ffn_W2"], "b2": plain["L0_ffn_b2"],
    }
    nc = _bacc.Bacc("TRN2", target_bir_lowering=False, num_devices=1)
    args = [nc.dram_tensor(f"in_{k}", v.shape, _mybir.dt.from_np(v.dtype), kind="ExternalInput").ap() for k, v in laid.items()]
    out = nc.dram_tensor("out_0", (N, D), _mybir.dt.float32, kind="ExternalOutput").ap()
    build(nc, *args, out)
    r = _run(nc, [{f"in_{k}": v for k, v in laid.items()}], core_ids=[0])
    return r.results[0]["out_0"]
```

```python
from contextlib import ExitStack

import numpy as np
import concourse.bass as bass
from concourse import mybir

F32 = mybir.dt.float32
BF16 = mybir.dt.bfloat16
I32 = mybir.dt.int32
U32 = mybir.dt.uint32
ALU = mybir.AluOpType
ACT = mybir.ActivationFunctionType
AX_X = mybir.AxisListType.X

P = 128
N, D = 3125, 256
KC = D // P
TP = 125
NT = N // TP
BT = 5
NB = NT // BT
EDGES = 53125
EP = 125
ET = EDGES // EP
G = 5
NG = ET // G
W = 64
RING = 4
NWIN = -(-N // W)
HEADS = 8
DK = D // HEADS
EX, HID = 8, 512
HC = HID // P
S4 = 4
LN_EPS = 1e-5
CHUNKS = ((0, 2), (2, 2), (4, 1))
NCH = len(CHUNKS)
MT = [(2 * TP * BT * nb + EX * (P - 1)) // P for _, nb in CHUNKS]
T0 = [sum(MT[:c]) for c in range(NCH + 1)]
MTT = T0[NCH]
STRIDE = [-(-TP * BT * nb // P) * P for _, nb in CHUNKS]
LIST0 = [sum(EX * STRIDE[i] + MT[i] * P for i in range(c)) for c in range(NCH + 1)]
SLOTS = LIST0[NCH]
READY = (36, 70)
LN_EPS = 1e-5


def wait_from(eng, sem, value):
    if isinstance(value, int) and value <= 0:
        return
    eng.wait_ge(sem, value)


def build(nc, x, src, dst, edge_weight, gnn_eps, gnn_w1, gnn_b1, gnn_w2, gnn_b2,
          Wq, bq, Wk, bk, Wv, bv, Wfc, bfc, gamma, beta, Wr, br, W1, b1, W2, b2, out):
    ctx = ExitStack()
    with ctx:
        def sb(name, shape, dt=F32):
            return ctx.enter_context(nc.sbuf_tensor(name, shape, dt))

        def sem(name):
            return ctx.enter_context(nc.semaphore(name))

        xn_rows = nc.dram_tensor("xn_rows", (N, D), F32, kind="Internal").ap()
        u_rows = [nc.dram_tensor(f"u_rows{c}", (nb * BT * TP, D), F32, kind="Internal").ap() for c, (_, nb) in enumerate(CHUNKS)]
        token_list = nc.dram_tensor("token_list", (SLOTS, 1), I32, kind="Internal").ap()
        y_rows = [nc.dram_tensor(f"y_rows{c}", (MT[c] * P, D), F32, kind="Internal").ap() for c in range(NCH)]

        bank = [ctx.enter_context(nc.psum_tensor(f"bank{i}", [P, 512], F32)) for i in range(8)]

        def cutter(region):
            at = [0]

            def piece(n):
                at[0] += n
                return region[:, at[0] - n:at[0]]
            return piece

        xres = sb("xres", [TP, NT, D])
        shared = sb("shared", [P, S4 * KC * HID + 2 * BT * D])
        xn = shared[0:TP, 0:NT * (D + 1)].rearrange("p (t d) -> p t d", d=D + 1)
        piece = cutter(shared)
        w1s = piece(S4 * KC * HID).rearrange("p (s k h) -> p s k h", s=S4, k=KC)
        u = piece(2 * BT * D)[0:TP, :].rearrange("p (s t d) -> p s t d", s=2, t=BT)
        xnT = sb("xnT", [P, KC, N])
        aggT = sb("aggT", [P, KC, N + W])
        ring = sb("ring", [P, RING * G * D])
        msg = ring[0:EP, :].rearrange("p (s d) -> p s d", d=D)
        onehot = sb("onehot", [EP, 2 * G, W])
        w2e = sb("w2e", [P, EX, HC, D])
        b2e = sb("b2e", [P, EX, D])

        piece = cutter(w2e[:].rearrange("p e c d -> p (e c d)"))

        def square():
            return piece(KC * D).rearrange("p (c i) -> p c i", c=KC)
        wq, wk, wv, wf, wkT, wvT, wfT, t1, a2 = (square() for _ in range(9))
        gram = piece(KC * (D + 1)).rearrange("p (c i) -> p c i", c=KC)
        ptm = piece(KC * P).rearrange("p (c i) -> p c i", c=KC)
        rows = piece(7 * D)[0:1, :].rearrange("p (r d) -> p r d", d=D)
        bk_row, bv_row, bfc_row, b2_row, s_row, tl_row, bias_row = (rows[:, i, :] for i in range(7))
        gmin = piece(NG)[0:EP, :]
        gminT = piece(1)[0:NG, :]
        gdiag = piece(NG)[0:NG, :]
        dstf = piece(ET)[0:EP, :].rearrange("p (g j) -> p g j", j=G)
        dstt = sb("dstt", [EP, ET], I32)

        srct = sb("srct", [EP, ET], I32)
        wt = sb("wt", [EP, ET])
        rel = sb("rel", [EP, NG, G])
        basef = sb("basef", [EP, NG])
        basei = sb("basei", [1, NG], I32)
        relmax = sb("relmax", [EP, 1])
        flagf = sb("flagf", [1, 8])
        flagi = sb("flagi", [1, 2], I32)
        idxr = sb("idxr", [EP, RING * G], I32)
        relq = sb("relq", [EP, G])
        curf = sb("curf", [1, 1])
        curi = sb("curi", [1, 1], I32)

        ident = sb("ident", [P, P])
        ones = sb("ones", [P, P])
        onesb = sb("onesb", [P, P], BF16)
        before = sb("before", [P, P], BF16)
        hmask = sb("hmask", [P, P // DK, DK])
        iotaW = sb("iotaW", [P, W])
        iota8 = sb("iota8", [P, EX])
        eoff = sb("eoff", [P, NCH, EX])
        iotaM = sb("iotaM", [P, MTT])
        baseM = sb("baseM", [P, MTT])
        tri = sb("tri", [P, EX, EX])
        tokid = sb("tokid", [TP, NT], I32)
        zlist = sb("zlist", [P, SLOTS // P], I32)

        bqc = sb("bqc", [P, KC])
        mixm = sb("mixm", [P, KC, D])
        gw1 = sb("gw1", [P, KC, D])
        gw2 = sb("gw2", [P, KC, D])
        gb1 = sb("gb1", [P, KC])
        eps1 = sb("eps1", [P, 1])
        gammaT = sb("gammaT", [P, KC])
        betaT = sb("betaT", [P, KC])
        wr = sb("wr", [P, KC, EX])
        brb = sb("brb", [P, EX])
        b1T = sb("b1T", [P, EX * HC])

        st = sb("st", [TP, NT, 6])
        mv = sb("mv", [TP, NT, 2])
        veps = sb("veps", [TP, 2, NT])
        sd = sb("sd", [TP, 2, NT])
        rs = sb("rs", [TP, 3, NT])
        lg = sb("lg", [TP, BT, EX])
        mx = sb("mx", [TP, NT, 8])
        ix = sb("ix", [TP, BT, 8], U32)
        ixf = sb("ixf", [TP, BT, 2])
        pick = sb("pick", [TP, 2, NT, EX])
        m12 = sb("m12", [TP, NT, EX], BF16)
        macc = sb("macc", [TP, NT + NCH, EX], BF16)
        pp = sb("pp", [TP, BT, EX])
        ppm = sb("ppm", [TP, 2, BT, EX])
        posf = sb("posf", [TP, 2, NT])
        posi = sb("posi", [TP, 2, NT], I32)
        diff = sb("diff", [TP, NT])
        exd = sb("exd", [TP, NT])
        den = sb("den", [TP, NT])
        wtop = sb("wtop", [TP, 2, NT])
        cnti = sb("cnti", [TP, 2, EX], I32)
        cntf = sb("cntf", [TP, 5, EX])
        backf = sb("backf", [TP, 2, NT])
        backi = sb("backi", [TP, 2, NT], I32)
        trin = sb("trin", [TP, EX, EX])
        cond = sb("cond", [TP, max(MT), EX])
        tabf = sb("tabf", [TP, 3, max(MT)])
        tab_e = sb("tab_e", [TP, MTT], I32)
        tab_b = sb("tab_b", [TP, MTT], I32)

        xfT = sb("xfT", [P, 2, KC, TP])
        hT = sb("hT", [P, 2, HC, P])
        xfTe = sb("xfTe", [P, 2, KC, P])
        ye = sb("ye", [P, 2, D])
        ue = sb("ue", [P, S4, D])
        tok = sb("tok", [P, S4], I32)

        x_in = [sem(f"x_in{c}") for c in range(NB)]
        edges_in = sem("edges_in")
        mixw_in = sem("mixw_in")
        gnnw_in = sem("gnnw_in")
        eps_in = sem("eps_in")
        ffnw_in = sem("ffnw_in")
        w2_in = sem("w2_in")
        list_zeroed = sem("list_zeroed")
        const_ready = sem("const_ready")
        dve_done = sem("dve_done")
        act_done = sem("act_done")
        var_ready = sem("var_ready")
        sd_ready = sem("sd_ready")
        xn_ready = sem("xn_ready")
        xn_stored = sem("xn_stored")
        xnT_psum = sem("xnT_psum")
        xnT_ready = sem("xnT_ready")
        agg_ready = sem("agg_ready")
        gram_psum = sem("gram_psum")
        mix_psum = sem("mix_psum")
        tl_ready = sem("tl_ready")
        ptm_ready = sem("ptm_ready")
        xbias_ready = sem("xbias_ready")
        gmin_ready = sem("gmin_ready")
        edge_psum = sem("edge_psum")
        gdiag_ready = sem("gdiag_ready")
        relmax_ready = sem("relmax_ready")
        flag_ready = sem("flag_ready")
        idx_ready = sem("idx_ready")
        turn = sem("turn")
        act_turn = sem("act_turn")
        sp_turn = sem("sp_turn")
        msg_in = [sem(f"msg_in{r}") for r in range(RING)]
        onehot_ready = sem("onehot_ready")
        group_psum = sem("group_psum")
        group_added = sem("group_added")
        r_idx = sem("r_idx")
        r_msg = sem("r_msg")
        r_rel = sem("r_rel")
        r_onehot = sem("r_onehot")
        r_psum = sem("r_psum")
        r_cur = sem("r_cur")
        r_added = sem("r_added")
        z_psum = sem("z_psum")
        z_ready = sem("z_ready")
        y_psum = sem("y_psum")
        x1_ready = sem("x1_ready")
        var2_ready = sem("var2_ready")
        sd2_ready = sem("sd2_ready")
        u_ready = sem("u_ready")
        pick_ready = sem("pick_ready")
        u_stored = sem("u_stored")
        uT_psum = sem("uT_psum")
        xfT_ready = sem("xfT_ready")
        logit_psum = sem("logit_psum")
        rank_psum = sem("rank_psum")
        pos_ready = sem("pos_ready")
        listed = sem("listed")
        count_psum = sem("count_psum")
        exd_ready = sem("exd_ready")
        table_ready = sem("table_ready")
        tok_in = [sem(f"tok_in{s}") for s in range(S4)]
        w1_in = [sem(f"w1_in{s}") for s in range(S4)]
        ue_in = [sem(f"ue_in{s}") for s in range(S4)]
        eturn = sem("eturn")
        ueT_psum = sem("ueT_psum")
        xfTe_ready = sem("xfTe_ready")
        h_psum = sem("h_psum")
        h_ready = sem("h_ready")
        ye_psum = sem("ye_psum")
        ye_ready = sem("ye_ready")
        y_stored = [sem(f"y_stored{s}") for s in range(2)]
        yback_in = [sem(f"yback_in{s}") for s in range(RING * G // 2)]
        res_ready = sem("res_ready")
        out_stored = sem("out_stored")

        diff_ready = sem("diff_ready")
        late_ready = sem("late_ready")
        x_t = x.rearrange("(t p) d -> p t d", p=TP)
        xn_t = xn_rows.rearrange("(t p) d -> p t d", p=TP)
        u_t = [r.rearrange("(t p) d -> p t d", p=TP) for r in u_rows]
        out_t = out.rearrange("(t p) d -> p t d", p=TP)

        picks = []
        PAIRS = [(t, min(2, NT - t)) for t in range(0, NT, 2)]
        ZG = [[(t, min(4, (b0 + nb) * BT - t)) for t in range(b0 * BT, (b0 + nb) * BT, 4)] for b0, nb in CHUNKS]
        ZC = [sum(len(z) for z in ZG[:c]) for c in range(NCH + 1)]
        CONSTS = 13
        UT, LOGIT, RANK = (0, 1), 2, 3
        EPS_STEP = 1
        TA, GA, WA = 4, 3, 3
        MIX_STEPS = 10
        MIX_LOADS, GNN_LOADS, FFN_LOADS = 9, 3, 6
        FR = RING * G // 2

        PREFIX = []
        for n in range(1, MIX_STEPS + 1):
            PREFIX += [("group", n - 1), ("mix", n)]
        PREFIX += [("group", 10), ("group", 11)]

        def routing(c, groups):
            items = [("z", c)] + [("route", c, st) for st in range(CHUNKS[c][1] + 2)] + [("table", c), ("head", c)]
            out = []
            for it in items:
                out.append(it)
                if groups:
                    out.append(("group", groups.pop(0)))
            return out + [("group", g) for g in groups]

        def tiles(c, g0, g1):
            first, last = T0[c], T0[c + 1]
            out, i, g = [("tile", first)], first + 1, g0
            while i < first + 3:
                if g < g1:
                    out.append(("group", g))
                    g += 1
                out.append(("tile", i))
                i += 1
            if g1 - g0 >= S4:
                turns = min((min(g1, NG - 4) - g) // S4, (last - S4 - i) // S4)
                if turns > 0:
                    out.append(("both", g, i, turns))
                    i, g = i + S4 * turns, g + S4 * turns
            while i < last:
                if g < g1:
                    out.append(("group", g))
                    g += 1
                elif last - S4 - i >= S4 and g == g1:
                    turns = (last - S4 - i) // S4
                    out.append(("tiles", 0, i, turns))
                    i += S4 * turns
                out.append(("tile", i))
                i += 1
            return out + [("group", x) for x in range(g, g1)]

        RD = CHUNKS[0][1] + 5
        EARLY = [("groups", 12, 0, (READY[0] - 12) // S4)]
        EARLY += routing(0, list(range(READY[0], READY[0] + RD))) + tiles(0, READY[0] + RD, READY[1])
        EARLY += routing(1, list(range(READY[1], READY[1] + RD))) + tiles(1, READY[1] + RD, NG)
        LATE = [("groups", 12, 0, (NG - 4 - 12) // S4)] + [("group", g) for g in range(12 + (NG - 4 - 12) // S4 * S4, NG)] + [("residual",)]
        LATE += routing(0, []) + tiles(0, NG, NG) + routing(1, []) + tiles(1, NG, NG)
        TAIL = routing(2, [])
        backs = list(range(CHUNKS[2][0] * BT))
        for n, i in enumerate(range(T0[2], T0[3])):
            TAIL.append(("tile", i))
            while backs and backs[0] < (n + 1) * 20 // MT[2] + 1:
                TAIL.append(("back", backs.pop(0)))
        TAIL += [("back", t) for t in range(CHUNKS[2][0] * BT, NT)]

        def run(eng, items, do, state=None):
            for kind, *a in items:
                if kind in ("groups", "tiles", "both"):
                    g0, i0, turns = a
                    with eng.Fori(0, turns) as q:
                        for k in range(S4):
                            if kind != "groups":
                                do["tile"](q, i0 + k)
                            if kind != "tiles":
                                do["group"](q, g0 + k)
                elif kind in ("group", "tile"):
                    do[kind](0, a[0])
                elif kind in do:
                    do[kind](*a)

        def run_all(eng, do, mark=None):
            run(eng, PREFIX, do)
            eng.wait_ge(late_ready, 1)
            late = eng.value_load(flagi[0:1, 1:2], min_val=0, max_val=1)
            at = list(mark) if mark else None
            with eng.If(late == 0):
                run(eng, EARLY, do)
            with eng.If(late == 1):
                if mark:
                    end, mark[:] = list(mark), at
                run(eng, LATE, do)
                assert not mark or mark == end
            run(eng, TAIL, do)

        def chunk_of(i):
            return max(c for c in range(NCH) if T0[c] <= i)

        def num(q, k):
            return q * S4 + k

        def ds1(q, k):
            return slice(k, k + 1) if isinstance(q, int) else bass.ds(q * S4 + k, 1)

        block = ctx.enter_context(nc.Block())

        @block.sync
        def _(sp):
            for c in range(NB):
                sp.dma_start(xres[:, c * BT:(c + 1) * BT, :], x_t[:, c * BT:(c + 1) * BT, :]).then_inc(x_in[c], 16)
                if c == 0:
                    sp.dma_start(srct[:], src).then_inc(edges_in, 16)
                    sp.dma_start(dstt[:], dst).then_inc(edges_in, 16)
                    sp.dma_start(wt[:], edge_weight).then_inc(edges_in, 16)
            for c in range(NB):
                sp.wait_ge(xn_ready, c + 1)
                sp.dma_start(xn_t[:, c * BT:(c + 1) * BT, :], xn[:, c * BT:(c + 1) * BT, 0:D]).then_inc(xn_stored, 16)
            sp.wait_ge(const_ready, CONSTS)
            sp.dma_start(token_list.rearrange("(p k) a -> p (k a)", p=P), zlist[:]).then_inc(list_zeroed, 16)
            sp.wait_ge(mix_psum, 10)
            sp.dma_start(w2e[:].rearrange("p e c d -> p (e c) d"), W2.rearrange("e (c p) d -> p (e c) d", p=P)).then_inc(w2_in, 16)
            def route(c, st):
                b = CHUNKS[c][0] + st
                if st < CHUNKS[c][1]:
                    sp.wait_ge(u_ready, b + 1)
                    sp.dma_start(u_t[c][:, st * BT:(st + 1) * BT, :], u[:, b % 2, :, :]).then_inc(u_stored, 16)

            def load_tokens(q, k):
                at = sp.value_load(tab_b[0:1, ds1(q, k)], min_val=0, max_val=SLOTS - P)
                if k >= S4:
                    sp.wait_ge(ue_in[k % S4], (q + k // S4) * 16)
                sp.sem_inc(sp_turn, 1)
                sp.dma_start(tok[:, k % S4:k % S4 + 1], token_list[bass.ds(at, P), :]).then_inc(tok_in[k % S4], 16)

            def load_w1(q, k):
                e = sp.value_load(tab_e[0:1, ds1(q, k)], min_val=0, max_val=EX - 1)
                wait_from(sp, h_psum, num(q, k) - S4 + 1)
                sp.sem_inc(sp_turn, 1)
                sp.dma_start(w1s[:, k % S4, :, :], W1.rearrange("e (k p) h -> e p k h", p=P)[bass.ds(e, 1), :, :, :]
                             .rearrange("e p k h -> p (e k) h")).then_inc(w1_in[k % S4], 16)

            def head(c):
                sp.wait_ge(table_ready, c + 1)
                sp.wait_ge(listed, 2 * (CHUNKS[c][0] + CHUNKS[c][1]) * BT * 16)
                for i in range(T0[c], T0[c] + TA):
                    load_tokens(0, i)
                for i in range(T0[c], T0[c] + WA):
                    load_w1(0, i)

            def tile(q, k):
                inner = not isinstance(q, int)
                last = T0[chunk_of(k) + 1] - 1
                if inner or k + TA <= last:
                    load_tokens(q, k + TA)
                if inner or k + WA <= last:
                    load_w1(q, k + WA)

            def back(t):
                sp.wait_ge(res_ready, t + 1)
                sp.dma_start(out_t[:, t, :], xres[:, t, :]).then_inc(out_stored, 16)

            run_all(sp, {"group": lambda q, k: None, "route": route, "head": head, "tile": tile, "back": back})
            sp.wait_ge(out_stored, NT * 16)

        @block.gpsimd
        def _(pool):
            def const(ins):
                ins.then_inc(const_ready, 1)
            const(pool.memset(ident[:], 0.0))
            const(pool.memset(ones[:], 1.0))
            const(pool.memset(xn[:, :, D:D + 1], 1.0))
            const(pool.memset(onesb[:], 1.0))
            const(pool.memset(hmask[:], 1.0 / N))
            const(pool.memset(tri[:], 1.0))
            pool.iota(iotaW[:], [[1, W]], base=0, channel_multiplier=0, allow_small_or_imprecise_dtypes=True)
            pool.iota(iota8[:], [[1, EX]], base=0, channel_multiplier=0, allow_small_or_imprecise_dtypes=True)
            for c in range(NCH):
                pool.iota(eoff[:, c, :], [[STRIDE[c], EX]], base=LIST0[c], channel_multiplier=0, allow_small_or_imprecise_dtypes=True)
                pool.iota(iotaM[:, T0[c]:T0[c + 1]], [[1, MT[c]]], base=0, channel_multiplier=0, allow_small_or_imprecise_dtypes=True)
                pool.iota(baseM[:, T0[c]:T0[c + 1]], [[P, MT[c]]], base=LIST0[c], channel_multiplier=0, allow_small_or_imprecise_dtypes=True)
            for c, (b0, nb) in enumerate(CHUNKS):
                ins = pool.iota(tokid[:, b0 * BT:(b0 + nb) * BT], [[TP, nb * BT]], base=0, channel_multiplier=1)
            const(ins)
            const(pool.memset(zlist[:], 0))
            pool.wait_ge(const_ready, 8)
            const(pool.affine_select(out=ident[:], in_=ident[:], compare_op=ALU.not_equal, fill=1.0, base=0,
                                     pattern=[[-1, P]], channel_multiplier=1))
            const(pool.affine_select(out=before[:], in_=onesb[:], compare_op=ALU.is_gt, fill=0.0, base=0,
                                     pattern=[[1, P]], channel_multiplier=-1))
            const(pool.affine_select(out=hmask[:], in_=hmask[:], compare_op=ALU.is_ge, fill=0.0, base=0,
                                     pattern=[[-DK, P // DK], [0, DK]], channel_multiplier=1))
            pool.wait_ge(const_ready, 11)
            const(pool.affine_select(out=hmask[:], in_=hmask[:], compare_op=ALU.is_ge, fill=0.0, base=DK - 1,
                                     pattern=[[DK, P // DK], [0, DK]], channel_multiplier=-1))
            const(pool.affine_select(out=tri[:], in_=tri[:], compare_op=ALU.is_ge, fill=0.0, base=0,
                                     pattern=[[1, EX], [-1, EX]], channel_multiplier=0))
            pool.memset(macc[:], 0.0).then_inc(const_ready, 1)

            pool.wait_ge(xn_stored, NB * 16)

            def gather(q, k):
                r = k % RING
                pool.wait_ge(idx_ready, num(q, k) + 1)
                pool.sem_inc(turn, 1)
                for j in range(G):
                    pool.indirect_dma_start(out=msg[:, r * G + j, :], out_offset=None, in_=xn_rows,
                                            in_offset=bass.IndirectOffsetOnAxis(ap=idxr[:, r * G + j:r * G + j + 1], axis=0)
                                            ).then_inc(msg_in[r], 16)

            def group(q, k):
                if not isinstance(q, int) or k + RING < NG:
                    gather(q, k + RING)

            def residual():
                wide = pool.value_load(flagi[0:1, 0:1], min_val=0, max_val=1)
                with pool.If(wide == 1):
                    with pool.Fori(0, NG) as g:
                        pool.wait_ge(r_idx, g + 1)
                        pool.sem_inc(turn, 1)
                        for j in range(G):
                            pool.indirect_dma_start(out=msg[:, j, :], out_offset=None, in_=xn_rows,
                                                    in_offset=bass.IndirectOffsetOnAxis(ap=idxr[:, j:j + 1], axis=0)
                                                    ).then_inc(r_msg, 16)

            def route(c, st):
                b = CHUNKS[c][0] + st - 2
                if st < 2:
                    return
                if b == 0:
                    pool.wait_ge(list_zeroed, 16)
                pool.wait_ge(pos_ready, b + 1)
                for t in range(b * BT, (b + 1) * BT):
                    for s in range(2):
                        pool.indirect_dma_start(out=token_list, out_offset=bass.IndirectOffsetOnAxis(ap=posi[:, s, t:t + 1], axis=0),
                                                in_=tokid[:, t:t + 1], in_offset=None).then_inc(listed, 16)

            def gather_tokens(q, k):
                wait_from(pool, ueT_psum, num(q, k) - S4 + 1)
                if not isinstance(q, int):
                    pool.sem_inc(eturn, 1)
                pool.wait_ge(tok_in[k % S4], (q + k // S4 + 1) * 16)
                if not isinstance(q, int):
                    pool.sem_inc(eturn, 1)
                pool.indirect_dma_start(out=ue[:, k % S4, :], out_offset=None, in_=u_rows[chunk_of(k)],
                                        in_offset=bass.IndirectOffsetOnAxis(ap=tok[:, k % S4:k % S4 + 1], axis=0)).then_inc(ue_in[k % S4], 16)

            def head(c):
                pool.wait_ge(u_stored, (CHUNKS[c][0] + CHUNKS[c][1]) * 16)
                for i in range(T0[c], T0[c] + GA):
                    gather_tokens(0, i)

            def tile(q, k):
                if not isinstance(q, int) or k + GA < T0[chunk_of(k) + 1]:
                    gather_tokens(q, k + GA)

            def back(t):
                if t in (0, CHUNKS[-1][0] * BT):
                    n = T0[NCH - 1] if t == 0 else MTT
                    for s in range(2):
                        pool.wait_ge(y_stored[s], (n + 1 - s) // 2 * 16)
                    pool.wait_ge(table_ready, NCH)
                s = t % FR
                if t >= FR:
                    pool.wait_ge(res_ready, t - FR + 1)
                for a in range(2):
                    pool.indirect_dma_start(out=msg[:, 2 * s + a, :], out_offset=None, in_=y_rows[max(c for c in range(NCH) if CHUNKS[c][0] * BT <= t)],
                                            in_offset=bass.IndirectOffsetOnAxis(ap=backi[:, a, t:t + 1], axis=0)).then_inc(yback_in[s], 16)

            for g in range(RING):
                gather(0, g)
            run_all(pool, {"group": group, "residual": residual, "route": route, "head": head, "tile": tile, "back": back})

        @block.scalar
        def _(act):
            act.dma_start(eps1[:], gnn_eps.rearrange("(a n) -> a n", a=1).broadcast_to([P, 1])).then_inc(eps_in, 16)
            for w, t in ((Wk, wk), (Wv, wv), (Wfc, wf), (Wq, wq)):
                act.dma_start(t[:, :, :], w.rearrange("(c p) i -> p c i", p=P)).then_inc(mixw_in, 16)
            for v, r in ((bk, bk_row), (bv, bv_row), (bfc, bfc_row), (gnn_b2, b2_row)):
                act.dma_start(r, v.rearrange("(a n) -> a n", a=1)).then_inc(mixw_in, 16)
            act.dma_start(bqc[:], bq).then_inc(mixw_in, 16)

            for c in range(NB):
                act.wait_ge(var_ready, c + 1)
                act.activation(sd[:, 0, c * BT:(c + 1) * BT], veps[:, 0, c * BT:(c + 1) * BT], ACT.Sqrt).then_inc(sd_ready, 1)
            for w, t in ((gnn_w1, gw1), (gnn_w2, gw2)):
                act.dma_start(t[:], w.rearrange("(c p) i -> p c i", p=P)).then_inc(gnnw_in, 16)
            act.dma_start(gb1[:], gnn_b1).then_inc(gnnw_in, 16)
            act.dma_start(gammaT[:], gamma).then_inc(ffnw_in, 16)
            act.dma_start(betaT[:], beta).then_inc(ffnw_in, 16)
            act.dma_start(wr[:], Wr.rearrange("(c p) e -> p c e", p=P)).then_inc(ffnw_in, 16)
            act.dma_start(brb[:], br.rearrange("(a n) -> a n", a=1).broadcast_to([P, EX])).then_inc(ffnw_in, 16)
            act.dma_start(b1T[:], b1).then_inc(ffnw_in, 16)
            act.dma_start(b2e[:].rearrange("p e d -> p (e d)"),
                          b2.rearrange("e d -> (e d)").rearrange("(a n) -> a n", a=1).broadcast_to([P, EX * D])).then_inc(ffnw_in, 16)

            def copy_idx(q, k):
                r = k % RING
                act.activation(idxr[:, r * G:(r + 1) * G], srct[:, bass.ds(num(q, k) * G, G)], ACT.Copy).then_inc(idx_ready, 1)
            act.wait_ge(edges_in, 48)
            for g in range(RING):
                copy_idx(0, g)

            act.wait_ge(dve_done, EPS_STEP)
            for n, (t0, nt) in enumerate(PAIRS):
                act.wait_ge(xnT_psum, n + 1)
                v = bank[n % 2][:, 0:KC * nt * TP].rearrange("p (c n) -> p c n", c=KC)
                cols = slice(t0 * TP, (t0 + nt) * TP)
                act.activation(xnT[:, :, cols], v, ACT.Copy)
                act.activation(aggT[:, :, cols], v, ACT.Identity, scale=eps1[:, 0:1]).then_inc(xnT_ready, 1)
            act.wait_ge(gram_psum, 1)
            act.activation(gram[:, 0, :], bank[2][:, 0:D + 1], ACT.Copy)
            act.activation(gram[:, 1, :], bank[3][:, 0:D + 1], ACT.Copy).then_inc(act_done, 1)

            def flat(a):
                return a.rearrange("p c i -> p (c i)")

            def mix(n):
                o_i = {1: (flat(wkT), bank[4][:, :]), 2: (flat(wvT), bank[5][:, :]), 3: (flat(wfT), bank[4][:, :]),
                       4: (s_row, bank[4][0:1, 0:D]), 5: (flat(t1), bank[0][:, :]), 7: (flat(a2), bank[2][:, :]),
                       8: (flat(mixm[:]), bank[3][:, :]), 9: (bias_row, bank[4][0:1, 0:D])}
                if n in o_i:
                    act.wait_ge(mix_psum, n)
                    act.activation(*o_i[n], ACT.Copy).then_inc(act_done, 1)

            def group(q, k):
                if not isinstance(q, int) or k + RING < NG:
                    act.wait_ge(group_psum, num(q, k) + 1)
                    copy_idx(q, k + RING)

            def residual():
                wide = act.value_load(flagi[0:1, 0:1], min_val=0, max_val=1)
                with act.If(wide == 1):
                    act.wait_ge(group_psum, NG)
                    act.activation(idxr[:, 0:G], srct[:, 0:G], ACT.Copy).then_inc(r_idx, 1)
                    with act.Fori(1, NG) as g:
                        act.wait_ge(r_psum, g * (NWIN - 1))
                        act.activation(idxr[:, 0:G], srct[:, bass.ds(g * G, G)], ACT.Copy).then_inc(r_idx, 1)

            def z(c):
                act.wait_ge(gnnw_in, GNN_LOADS * 16)
                act.wait_ge(ffnw_in, FFN_LOADS * 16)
                for n, (t0, nt) in enumerate(ZG[c]):
                    act.wait_ge(z_psum, ZC[c] + n + 1)
                    for m in range(KC):
                        ins = act.activation(aggT[:, m, t0 * TP:(t0 + nt) * TP], bank[2 * (n % 2) + m][:, 0:nt * TP], ACT.Relu,
                                             bias=gb1[:, m:m + 1])
                    ins.then_inc(z_ready, 1)

            def route(c, st):
                b0, nb = CHUNKS[c]
                b = b0 + st
                if st < nb:
                    for s in range(2):
                        act.wait_ge(var2_ready, 2 * b + s + 1)
                        act.activation(sd[:, s, b * BT:(b + 1) * BT], veps[:, s, b * BT:(b + 1) * BT], ACT.Sqrt).then_inc(sd2_ready, 1)
                if 1 <= st <= nb:
                    for t in range((b - 1) * BT, b * BT):
                        act.wait_ge(uT_psum, t + 1)
                        wait_from(act, logit_psum, t - 1)
                        for i in range(KC):
                            ins = act.activation(xfT[:, t % 2, i, :], bank[UT[t % 2]][:, i * P:i * P + TP], ACT.Identity,
                                                 scale=gammaT[:, i:i + 1], bias=betaT[:, i:i + 1])
                        ins.then_inc(xfT_ready, 1)

            def table(c):
                if c == NCH - 1:
                    act.wait_ge(diff_ready, 1)
                    act.activation(exd[:], diff[:], ACT.Exp).then_inc(exd_ready, 1)
                act.wait_ge(table_ready, c + 1)

            def store_y(q, k):
                act.wait_ge(ye_ready, num(q, k) + 1)
                act.sem_inc(act_turn, 1)
                c = chunk_of(k)
                at = num(q, k - T0[c]) * P
                act.dma_start(y_rows[c][slice(at, at + P) if isinstance(q, int) else bass.ds(at, P), :],
                              ye[:, k % 2, :]).then_inc(y_stored[k % 2], 16)

            def tile(q, k):
                i = num(q, k)
                e = act.value_load(tab_e[0:1, ds1(q, k)], min_val=0, max_val=EX - 1)
                wait_from(act, ye_psum, i - 1)
                act.wait_ge(h_psum, i + 1)
                for m in range(HC):
                    ins = act.activation(hT[:, k % 2, m, :], bank[2 + k % 2][:, m * P:(m + 1) * P], ACT.Gelu,
                                         bias=b1T[:, bass.ds(e * HC + m, 1)])
                ins.then_inc(h_ready, 1)
                inner = not isinstance(q, int)
                if inner or k - 2 >= T0[chunk_of(k)]:
                    store_y(q, k - 2)
                if not inner and k + 1 == T0[chunk_of(k) + 1]:
                    store_y(0, k - 1)
                    store_y(0, k)

            run_all(act, {"group": group, "mix": mix, "residual": residual, "z": z, "route": route, "table": table, "tile": tile})

        @block.vector
        def _(dve):
            steps = [0]

            def link(ins):
                steps[0] += 1
                ins.then_inc(dve_done, 1)
                dve.wait_ge(dve_done, steps[0])

            dve.wait_ge(eps_in, 16)
            link(dve.tensor_scalar(eps1[:], eps1[:], 1.0, None, ALU.add))

            for c in range(NB):
                ts = slice(c * BT, (c + 1) * BT)
                dve.wait_ge(x_in[c], 16)
                for t in range(c * BT, (c + 1) * BT):
                    ins = dve.bn_stats(st[:, t, :], xres[:, t, :])
                link(ins)
                for t in range(c * BT, (c + 1) * BT):
                    ins = dve.bn_aggr(mv[:, t, :], st[:, t, :])
                link(ins)
                dve.tensor_scalar(veps[:, 0, ts], mv[:, ts, 1], LN_EPS, None, ALU.add).then_inc(var_ready, 1)
                dve.wait_ge(sd_ready, c + 1)
                link(dve.reciprocal(rs[:, 0, ts], sd[:, 0, ts]))
                for t in range(c * BT, (c + 1) * BT):
                    ins = dve.tensor_scalar(xn[:, t, 0:D], xres[:, t, :], mv[:, t, 0:1], rs[:, 0, t:t + 1], ALU.subtract, ALU.mult)
                ins.then_inc(xn_ready, 1)

            dve.wait_ge(const_ready, CONSTS + 1)
            dve.wait_ge(edges_in, 48)
            link(dve.tensor_copy(dstf.rearrange("p g j -> p (g j)"), dstt[:]))
            dve.tensor_reduce(gmin, dstf, AX_X, ALU.min).then_inc(gmin_ready, 1)
            dve.wait_ge(edge_psum, 1)
            link(dve.tensor_reduce(gminT, bank[5][0:NG, 0:EP], AX_X, ALU.min))
            dve.tensor_scalar(gdiag, ident[0:NG, 0:NG], gminT, None, ALU.mult).then_inc(gdiag_ready, 1)
            dve.wait_ge(edge_psum, 2)
            dve.tensor_copy(basei[:], bank[5][0:1, P:P + NG])
            link(dve.tensor_copy(basef[:], bank[5][0:EP, P:P + NG]))
            link(dve.tensor_tensor(rel[:], dstf, basef[:].unsqueeze(2).broadcast_to([EP, NG, G]), ALU.subtract))
            dve.tensor_reduce(relmax[:], rel[:].rearrange("p g j -> p (g j)"), AX_X, ALU.max).then_inc(relmax_ready, 1)
            dve.wait_ge(edge_psum, 3)
            link(dve.tensor_reduce(flagf[:, 0:1], bank[5][0:1, 256:256 + EP], AX_X, ALU.max))
            dve.tensor_scalar(flagf[:, 1:2], flagf[:, 0:1], float(W), None, ALU.is_ge).then_inc(flag_ready, 1)
            for c, g in enumerate(READY):
                ins = dve.tensor_reduce(flagf[:, 2 + c:3 + c], basef[0:1, g:NG], AX_X, ALU.min)
            link(ins)
            for c in range(len(READY)):
                last_node = (CHUNKS[c][0] + CHUNKS[c][1]) * BT * TP - 1
                ins = dve.tensor_scalar(flagf[:, 4 + c:5 + c], flagf[:, 2 + c:3 + c], float(last_node), None, ALU.is_le)
            link(ins)
            link(dve.tensor_tensor(flagf[:, 6:7], flagf[:, 4:5], flagf[:, 5:6], ALU.max))
            link(dve.tensor_tensor(flagf[:, 7:8], flagf[:, 6:7], flagf[:, 1:2], ALU.max))
            dve.tensor_copy(flagi[:, 0:1], flagf[:, 1:2])
            dve.tensor_copy(flagi[:, 1:2], flagf[:, 7:8]).then_inc(late_ready, 1)

            rel_flat = rel[:].rearrange("p g j -> p (g j)")

            def onehots(q, k):
                g = num(q, k)
                for j in range(G):
                    ins = dve.tensor_scalar(onehot[:, k % 2 * G + j, :], iotaW[0:EP, :], rel_flat[:, bass.ds(g * G + j, 1)],
                                            wt[:, bass.ds(g * G + j, 1)], ALU.is_equal, ALU.mult)
                ins.then_inc(onehot_ready, 1)

            def group(q, k):
                g = num(q, k)
                if k == 0:
                    dve.wait_ge(xnT_ready, len(PAIRS))
                dve.wait_ge(group_psum, g + 1)
                if not isinstance(q, int) or k + 2 < NG:
                    onehots(q, k + 2)
                base = dve.value_load(basei[0:1, bass.ds(g, 1)], min_val=0, max_val=N - 1)
                wait_from(dve, group_added, g)
                window = aggT[:, :, bass.ds(base, W)]
                dve.tensor_tensor(window, window, bank[6 + k % 2][:, :].rearrange("p (c n) -> p c n", c=KC)[:, :, 0:W],
                                  ALU.add).then_inc(group_added, 1)

            def mix(n):
                if n == 5:
                    dve.wait_ge(mix_psum, 5)
                    dve.scalar_tensor_tensor(out=tl_row, in0=bk_row, scalar=float(N), in1=bank[1][0:1, 0:D], op0=ALU.mult,
                                             op1=ALU.add).then_inc(tl_ready, 1)
                if n == 6:
                    dve.wait_ge(mix_psum, 6)
                    for c in range(KC):
                        ins = dve.tensor_tensor(ptm[:, c, :], bank[1][:, 256 + c * P:256 + (c + 1) * P],
                                                hmask[:].rearrange("p b d -> p (b d)"), ALU.mult)
                    ins.then_inc(ptm_ready, 1)
                if n == MIX_STEPS:
                    dve.wait_ge(mix_psum, MIX_STEPS)
                    link(dve.tensor_tensor(xres[:], xres[:], bank[4][0:TP, 256:256 + D].unsqueeze(1).broadcast_to([TP, NT, D]), ALU.add))

            def residual():
                wide = dve.value_load(flagi[0:1, 0:1], min_val=0, max_val=1)
                with dve.If(wide == 1):
                    dve.wait_ge(group_added, NG)
                    with dve.Fori(0, NG) as g:
                        dve.tensor_copy(relq[:], rel_flat[:, bass.ds(g * G, G)]).then_inc(r_rel, 1)
                        dve.tensor_copy(curf[:], basef[0:1, bass.ds(g, 1)]).then_inc(r_rel, 1)
                        with dve.Fori(0, NWIN - 1) as w:
                            n = g * (NWIN - 1) + w
                            c = g * 2 + n * 2 + 2
                            dve.wait_ge(r_rel, c)
                            dve.tensor_scalar(relq[:], relq[:], float(W), None, ALU.subtract).then_inc(r_rel, 1)
                            dve.tensor_scalar(curf[:], curf[:], float(W), float(N), ALU.add, ALU.min).then_inc(r_rel, 1)
                            dve.wait_ge(r_rel, c + 2)
                            dve.tensor_copy(curi[:], curf[:]).then_inc(r_cur, 1)
                            for j in range(G):
                                ins = dve.tensor_scalar(onehot[:, j, :], iotaW[0:EP, :], relq[:, j:j + 1],
                                                        wt[:, bass.ds(g * G + j, 1)], ALU.is_equal, ALU.mult)
                            ins.then_inc(r_onehot, 1)
                            dve.wait_ge(r_cur, n + 1)
                            dve.sem_inc(turn, 1)
                            base = dve.value_load(curi[0:1, 0:1], min_val=0, max_val=N)
                            dve.wait_ge(r_psum, n + 1)
                            window = aggT[:, :, bass.ds(base, W)]
                            dve.tensor_tensor(window, window, bank[6][:, :].rearrange("p (c n) -> p c n", c=KC)[:, :, 0:W],
                                              ALU.add).then_inc(r_added, 1)
                            dve.wait_ge(r_added, n + 1)

            def x1_and_u(b):
                ts = slice(b * BT, (b + 1) * BT)
                for t in range(b * BT, (b + 1) * BT):
                    dve.wait_ge(y_psum, t + 1)
                    ins = dve.tensor_tensor(xres[:, t, :], xres[:, t, :], bank[4 + t % 2][0:TP, 0:D], ALU.add)
                    ins.then_inc(x1_ready, 1)
                dve.wait_ge(x1_ready, (b + 1) * BT)
                for t in range(b * BT, (b + 1) * BT):
                    ins = dve.bn_stats(st[:, t, :], xres[:, t, :])
                link(ins)
                for t in range(b * BT, (b + 1) * BT):
                    ins = dve.bn_aggr(mv[:, t, :], st[:, t, :])
                link(ins)
                dve.tensor_scalar(veps[:, 0, ts], mv[:, ts, 1], LN_EPS, None, ALU.add).then_inc(var2_ready, 1)
                dve.wait_ge(sd2_ready, 2 * b + 1)
                link(dve.reciprocal(rs[:, 0, ts], sd[:, 0, ts]))
                link(dve.tensor_tensor(rs[:, 1, ts], rs[:, 0, ts], rs[:, 0, ts], ALU.mult))
                link(dve.tensor_tensor(rs[:, 2, ts], rs[:, 1, ts], mv[:, ts, 1], ALU.mult))
                dve.tensor_scalar(veps[:, 1, ts], rs[:, 2, ts], LN_EPS, None, ALU.add).then_inc(var2_ready, 1)
                dve.wait_ge(sd2_ready, 2 * b + 2)
                link(dve.reciprocal(rs[:, 1, ts], sd[:, 1, ts]))
                link(dve.tensor_tensor(rs[:, 2, ts], rs[:, 0, ts], rs[:, 1, ts], ALU.mult))
                if b >= 2:
                    dve.wait_ge(u_stored, (b - 1) * 16)
                    dve.wait_ge(uT_psum, (b - 1) * BT)
                for t in range(b * BT, (b + 1) * BT):
                    ins = dve.tensor_scalar(u[:, b % 2, t % BT, :], xres[:, t, :], mv[:, t, 0:1], rs[:, 2, t:t + 1], ALU.subtract, ALU.mult)
                ins.then_inc(u_ready, 1)

            def top2(c, b):
                ts = slice(b * BT, (b + 1) * BT)
                dve.wait_ge(logit_psum, (b + 1) * BT)
                link(dve.tensor_tensor(lg[:], bank[LOGIT][0:TP, 0:BT * EX].rearrange("p (t e) -> p t e", e=EX),
                                       brb[0:TP, :].unsqueeze(1).broadcast_to([TP, BT, EX]), ALU.add))
                for t in range(BT):
                    ins = dve.max(mx[:, b * BT + t, :], lg[:, t, :])
                link(ins)
                for t in range(BT):
                    ins = dve.max_index(ix[:, t, :], mx[:, b * BT + t, :], lg[:, t, :])
                link(ins)
                link(dve.tensor_copy(ixf[:], ix[:, :, 0:2]))
                for s in range(2):
                    ins = dve.tensor_tensor(pick[:, s, ts, :], iota8[0:TP, :].unsqueeze(1).broadcast_to([TP, BT, EX]),
                                            ixf[:, :, s:s + 1].broadcast_to([TP, BT, EX]), ALU.is_equal)
                link(ins)
                link(dve.tensor_tensor(m12[:, ts, :], pick[:, 0, ts, :], pick[:, 1, ts, :], ALU.add))
                for t in range(b * BT, (b + 1) * BT):
                    dve.tensor_tensor(macc[:, t + c + 1, :], macc[:, t + c, :], m12[:, t, :], ALU.add).then_inc(pick_ready, 1)
                    dve.wait_ge(pick_ready, t + 1)

            def positions(c, b):
                ts = slice(b * BT, (b + 1) * BT)
                dve.wait_ge(rank_psum, b + 1)
                link(dve.tensor_tensor(pp[:], bank[RANK][0:TP, 0:BT * EX].rearrange("p (t e) -> p t e", e=EX),
                                       eoff[0:TP, c:c + 1, :].broadcast_to([TP, BT, EX]), ALU.add))
                for s in range(2):
                    ins = dve.tensor_tensor(ppm[:, s, :, :], pp[:], pick[:, s, ts, :], ALU.mult)
                link(ins)
                for s in range(2):
                    ins = dve.tensor_reduce(posf[:, s, ts], ppm[:, s, :, :], AX_X, ALU.add)
                link(ins)
                for s in range(2):
                    ins = dve.tensor_copy(posi[:, s, ts], posf[:, s, ts])
                ins.then_inc(pos_ready, 1)

            def route(c, st):
                b0, nb = CHUNKS[c]
                if c == 0 and st == 0:
                    dve.wait_ge(ffnw_in, FFN_LOADS * 16)
                if st < nb:
                    x1_and_u(b0 + st)
                if 1 <= st <= nb:
                    top2(c, b0 + st - 1)
                if st >= 2:
                    positions(c, b0 + st - 2)

            def table(c):
                b0, nb = CHUNKS[c]
                if c == NCH - 1:
                    dve.tensor_tensor(diff[:], mx[:, :, 1], mx[:, :, 0], ALU.subtract).then_inc(diff_ready, 1)
                M, tl = MT[c], slice(T0[c], T0[c + 1])
                dve.wait_ge(count_psum, c + 1)
                link(dve.tensor_scalar(cnti[:, 0, :], bank[RANK][0:TP, 448:448 + EX], float(P - 1), None, ALU.add))
                link(dve.tensor_scalar(cnti[:, 1, :], cnti[:, 0, :], P.bit_length() - 1, None, ALU.logical_shift_right))
                link(dve.tensor_copy(cntf[:, 0, :], cnti[:, 1, :]))
                dve.tensor_scalar(cntf[:, 2, :], cntf[:, 0, :], -float(P), float(STRIDE[c]), ALU.mult, ALU.add)
                link(dve.tensor_tensor(trin[:], cntf[:, 0, :].unsqueeze(1).broadcast_to([TP, EX, EX]), tri[0:TP, :, :], ALU.mult))
                link(dve.tensor_reduce(cntf[:, 1, :], trin[:], AX_X, ALU.add))
                cd = cond[:, 0:M, :]
                link(dve.tensor_tensor(cd, cntf[:, 1, :].unsqueeze(1).broadcast_to([TP, M, EX]),
                                       iotaM[0:TP, tl].unsqueeze(2).broadcast_to([TP, M, EX]), ALU.is_le))
                link(dve.tensor_reduce(tabf[:, 0, 0:M], cd, AX_X, ALU.add))
                link(dve.tensor_tensor(cd, cd, cntf[:, 2, :].unsqueeze(1).broadcast_to([TP, M, EX]), ALU.mult))
                link(dve.tensor_reduce(tabf[:, 1, 0:M], cd, AX_X, ALU.add))
                dve.tensor_scalar(tab_e[:, tl], tabf[:, 0, 0:M], float(EX - 1), None, ALU.min)
                link(dve.tensor_tensor(tabf[:, 2, 0:M], tabf[:, 1, 0:M], baseM[0:TP, tl], ALU.add))
                link(dve.tensor_tensor(cntf[:, 3, :], cntf[:, 1, :], cntf[:, 0, :], ALU.subtract))
                link(dve.scalar_tensor_tensor(out=cntf[:, 4, :], in0=cntf[:, 3, :], scalar=-float(P), in1=eoff[0:TP, c, :],
                                              op0=ALU.mult, op1=ALU.add))
                for b in range(b0, b0 + nb):
                    ts = slice(b * BT, (b + 1) * BT)
                    for s in range(2):
                        ins = dve.tensor_tensor(ppm[:, s, :, :], pick[:, s, ts, :], cntf[:, 4:5, :].broadcast_to([TP, BT, EX]), ALU.mult)
                    link(ins)
                    for s in range(2):
                        ins = dve.tensor_reduce(backf[:, s, ts], ppm[:, s, :, :], AX_X, ALU.add)
                    link(ins)
                ts = slice(b0 * BT, (b0 + nb) * BT)
                link(dve.tensor_tensor(backi[:, :, ts], posf[:, :, ts], backf[:, :, ts], ALU.subtract))
                dve.tensor_copy(tab_b[:, tl], tabf[:, 2, 0:M]).then_inc(table_ready, 1)
                dve.wait_ge(table_ready, c + 1)
                if c == NCH - 1:
                    dve.wait_ge(exd_ready, 1)
                    link(dve.tensor_scalar(den[:], exd[:], 1.0, None, ALU.add))
                    link(dve.reciprocal(wtop[:, 0, :], den[:]))
                    link(dve.tensor_tensor(wtop[:, 1, :], wtop[:, 0, :], exd[:], ALU.mult))

            def evac_xfT(q, k):
                i = num(q, k)
                wait_from(dve, h_psum, i - 1)
                dve.wait_ge(ueT_psum, i + 1)
                for c in range(KC):
                    ins = dve.tensor_scalar(xfTe[:, k % 2, c, :], bank[k % 2][:, c * P:(c + 1) * P], gammaT[:, c:c + 1],
                                            betaT[:, c:c + 1], ALU.mult, ALU.add)
                ins.then_inc(xfTe_ready, 1)

            def evac_y(q, k):
                i = num(q, k)
                e = dve.value_load(tab_e[0:1, ds1(q, k)], min_val=0, max_val=EX - 1)
                if k >= 2:
                    dve.wait_ge(y_stored[k % 2], (q * (S4 // 2) + k // 2) * 16)
                dve.wait_ge(ye_psum, i + 1)
                dve.tensor_tensor(ye[:, k % 2, :], bank[4 + k % 2][:, 0:D], b2e[:, bass.ds(e, 1), :].rearrange("p a d -> p (a d)"),
                                  ALU.add).then_inc(ye_ready, 1)

            def head(c):
                evac_xfT(0, T0[c])

            def tile(q, k):
                c = chunk_of(k)
                inner = not isinstance(q, int)
                if inner or k + 1 < T0[c + 1]:
                    evac_xfT(q, k + 1)
                if inner or k > T0[c]:
                    evac_y(q, k - 1)
                if not inner and k + 1 == T0[c + 1]:
                    evac_y(q, k)

            def back(t):
                s = t % FR
                dve.wait_ge(yback_in[s], (t // FR + 1) * 32)
                for a in range(2):
                    ins = dve.scalar_tensor_tensor(out=xres[:, t, :], in0=msg[:, 2 * s + a, :], scalar=wtop[:, a, t:t + 1],
                                                   in1=xres[:, t, :], op0=ALU.mult, op1=ALU.add)
                    if a == 0:
                        link(ins)
                ins.then_inc(res_ready, 1)

            dve.memset(aggT[:, :, N:N + W], 0.0)
            onehots(0, 0)
            onehots(0, 1)
            run_all(dve, {"group": group, "mix": mix, "residual": residual, "route": route, "table": table, "head": head,
                          "tile": tile, "back": back}, mark=steps)

        @block.tensor
        def _(pe):
            pe.wait_ge(const_ready, CONSTS)
            for n, (t0, nt) in enumerate(PAIRS):
                if n >= 2:
                    pe.wait_ge(xnT_ready, n - 1)
                for t in range(t0, t0 + nt):
                    if t % BT == 0 or t == t0:
                        pe.wait_ge(xn_ready, t // BT + 1)
                    for c in range(KC):
                        o = c * nt * TP + (t - t0) * TP
                        ins = pe.transpose(bank[n % 2][:, o:o + TP], xn[:, t, c * P:(c + 1) * P], ident[0:TP, 0:TP])
                ins.then_inc(xnT_psum, 1)
                for t in range(t0, t0 + nt):
                    for m in range(KC):
                        ins = pe.matmul(bank[2 + m][:, 0:D + 1], xn[:, t, m * P:(m + 1) * P], xn[:, t, :],
                                        start=(t == 0), stop=(t == NT - 1))
            ins.then_inc(gram_psum, 1)

            pe.wait_ge(gmin_ready, 1)
            pe.transpose(bank[5][0:NG, 0:EP], gmin, ident[0:EP, 0:EP]).then_inc(edge_psum, 1)
            pe.wait_ge(gdiag_ready, 1)
            pe.matmul(bank[5][0:EP, P:P + NG], ones[0:NG, 0:EP], gdiag, start=True, stop=True).then_inc(edge_psum, 1)
            pe.wait_ge(relmax_ready, 1)
            pe.transpose(bank[5][0:1, 256:256 + EP], relmax[:], ident[0:EP, 0:EP]).then_inc(edge_psum, 1)

            def mix(n):
                if n <= 3:
                    if n == 1:
                        pe.wait_ge(mixw_in, MIX_LOADS * 16)
                        pe.wait_ge(flag_ready, 1)
                    if n == 3:
                        pe.wait_ge(act_done, 2)
                    w, b = (wk, wv, wf)[n - 1], bank[4 + (n == 2)]
                    for ci in range(KC):
                        for co in range(KC):
                            ins = pe.transpose(b[:, ci * D + co * P:ci * D + (co + 1) * P], w[:, co, ci * P:(ci + 1) * P], ident[:])
                elif n == 4:
                    pe.wait_ge(act_done, 4)
                    for c in range(KC):
                        ins = pe.transpose(bank[4][0:1, c * P:(c + 1) * P], gram[:, c, D:D + 1], ident[:])
                elif n == 5:
                    pe.wait_ge(act_done, 5)
                    pe.wait_ge(xnT_ready, len(PAIRS))
                    for c in range(KC):
                        o = bank[0][:, c * D:(c + 1) * D]
                        for k in range(KC):
                            pe.matmul(o, gram[:, k, c * P:(c + 1) * P], wkT[:, k, :], start=(k == 0), stop=False)
                        pe.matmul(o, s_row[:, c * P:(c + 1) * P], bk_row, start=False, stop=True)
                    for k in range(KC):
                        ins = pe.matmul(bank[1][0:1, 0:D], gram[:, k, D:D + 1], wkT[:, k, :], start=(k == 0), stop=(k == KC - 1))
                elif n == 6:
                    pe.wait_ge(act_done, 6)
                    pe.wait_ge(tl_ready, 1)
                    for c in range(KC):
                        cs = slice(c * P, (c + 1) * P)
                        o = bank[1][:, 256 + c * P:256 + (c + 1) * P]
                        for k in range(KC):
                            pe.matmul(o, wvT[:, k, cs], t1[:, k, cs], start=(k == 0), stop=False)
                        ins = pe.matmul(o, bv_row[:, cs], tl_row[:, cs], start=False, stop=True)
                elif n == 7:
                    pe.wait_ge(ptm_ready, 1)
                    for c in range(KC):
                        ins = pe.matmul(bank[2][:, c * D:(c + 1) * D], ptm[:, c, :], wfT[:, c, :], start=True, stop=True)
                elif n == 8:
                    pe.wait_ge(act_done, 7)
                    for c in range(KC):
                        for k in range(KC):
                            ins = pe.matmul(bank[3][:, c * D:(c + 1) * D], wq[:, k, c * P:(c + 1) * P], a2[:, k, :], start=(k == 0), stop=(k == KC - 1))
                elif n == 9:
                    for k in range(KC):
                        pe.matmul(bank[4][0:1, 0:D], bqc[:, k:k + 1], a2[:, k, :], start=(k == 0), stop=False)
                    pe.matmul(bank[4][0:1, 0:D], ones[0:1, 0:1], bfc_row, start=False, stop=False)
                    ins = pe.matmul(bank[4][0:1, 0:D], ones[0:1, 0:1], b2_row, start=False, stop=True)
                else:
                    pe.wait_ge(act_done, 9)
                    ins = pe.matmul(bank[4][0:TP, 256:256 + D], ones[0:1, 0:TP], bias_row, start=True, stop=True)
                ins.then_inc(mix_psum, 1)

            def group(q, k):
                g, r, b = num(q, k), k % RING, k % 2
                pe.wait_ge(msg_in[r], (q + k // RING + 1) * (16 * G))
                wait_from(pe, group_added, g - 1)
                pe.wait_ge(onehot_ready, g + 1)
                for c in range(KC):
                    for j in range(G):
                        ins = pe.matmul(bank[6 + b][:, c * 256:c * 256 + W], msg[:, r * G + j, c * P:(c + 1) * P],
                                        onehot[:, b * G + j, :], start=(j == 0), stop=(j == G - 1))
                ins.then_inc(group_psum, 1)

            def residual():
                wide = pe.value_load(flagi[0:1, 0:1], min_val=0, max_val=1)
                with pe.If(wide == 1):
                    with pe.Fori(0, NG) as g:
                        pe.wait_ge(r_msg, (g + 1) * (16 * G))
                        pe.sem_inc(turn, 1)
                        with pe.Fori(0, NWIN - 1) as w:
                            n = g * (NWIN - 1) + w
                            pe.wait_ge(r_onehot, n + 1)
                            for c in range(KC):
                                for j in range(G):
                                    ins = pe.matmul(bank[6][:, c * 256:c * 256 + W], msg[:, j, c * P:(c + 1) * P],
                                                    onehot[:, j, :], start=(j == 0), stop=(j == G - 1))
                            ins.then_inc(r_psum, 1)
                    pe.wait_ge(r_added, NG * (NWIN - 1))

            def z(c):
                pe.wait_ge(group_added, READY[c] if c < len(READY) else NG)
                pe.wait_ge(gnnw_in, GNN_LOADS * 16)
                wait_from(pe, ye_ready, T0[c])
                for n, (t0, nt) in enumerate(ZG[c]):
                    if n >= 2:
                        pe.wait_ge(z_ready, ZC[c] + n - 1)
                    cols = slice(t0 * TP, (t0 + nt) * TP)
                    for m in range(KC):
                        for k in range(KC):
                            ins = pe.matmul(bank[2 * (n % 2) + m][:, 0:nt * TP], gw1[:, k, m * P:(m + 1) * P], aggT[:, k, cols],
                                            start=(k == 0), stop=(k == KC - 1))
                    ins.then_inc(z_psum, 1)

            def y_tile(t):
                wait_from(pe, x1_ready, t - 1)
                o = bank[4 + t % 2][0:TP, 0:D]
                cols = slice(t * TP, (t + 1) * TP)
                for k in range(KC):
                    pe.matmul(o, aggT[:, k, cols], gw2[:, k, :], start=(k == 0), stop=False)
                for k in range(KC):
                    ins = pe.matmul(o, xnT[:, k, cols], mixm[:, k, :], start=False, stop=(k == KC - 1))
                ins.then_inc(y_psum, 1)

            def transposes(t):
                pe.wait_ge(u_ready, t // BT + 1)
                wait_from(pe, xfT_ready, t - 1)
                for c in range(KC):
                    ins = pe.transpose(bank[UT[t % 2]][:, c * P:c * P + TP], u[:, t // BT % 2, t % BT, c * P:(c + 1) * P], ident[0:TP, 0:TP])
                ins.then_inc(uT_psum, 1)

            def logits(t):
                pe.wait_ge(xfT_ready, t + 1)
                o = t % BT * EX
                for c in range(KC):
                    ins = pe.matmul(bank[LOGIT][0:TP, o:o + EX], xfT[:, t % 2, c, :], wr[:, c, :], start=(c == 0), stop=(c == KC - 1))
                ins.then_inc(logit_psum, 1)

            def ranks(c, b):
                ts = slice(b * BT, (b + 1) * BT)
                rank = bank[RANK][0:TP, 0:BT * EX]
                pe.matmul(rank, before[0:TP, 0:TP], m12[:, ts, :].rearrange("p t e -> p (t e)"), start=True, stop=False)
                pe.matmul(rank, onesb[0:TP, 0:TP], macc[:, b * BT + c:(b + 1) * BT + c, :].rearrange("p t e -> p (t e)"),
                          start=False, stop=True).then_inc(rank_psum, 1)

            def route(c, st):
                b0, nb = CHUNKS[c]
                b = b0 + st
                if st == 0:
                    pe.wait_ge(z_ready, ZC[c + 1])
                if st < nb:
                    for t in range(b * BT, (b + 1) * BT):
                        y_tile(t)
                if 1 <= st <= nb:
                    wait_from(pe, pick_ready, (b - 1) * BT)
                    for t in range((b - 1) * BT, b * BT):
                        transposes(t)
                        if t > (b - 1) * BT:
                            logits(t - 1)
                    logits(b * BT - 1)
                if st >= 2:
                    wait_from(pe, pos_ready, b - 2)
                    pe.wait_ge(pick_ready, (b - 1) * BT)
                    ranks(c, b - 2)

            def table(c):
                last = CHUNKS[c][0] + CHUNKS[c][1]
                pe.wait_ge(pos_ready, last)
                pe.matmul(bank[RANK][0:TP, 448:448 + EX], onesb[0:TP, 0:TP], macc[:, last * BT + c, :], start=True, stop=True).then_inc(count_psum, 1)

            def u_transposes(q, k):
                i = num(q, k)
                wait_from(pe, xfTe_ready, i - 1)
                pe.wait_ge(ue_in[k % S4], (q + k // S4 + 1) * 16)
                for c in range(KC):
                    ins = pe.transpose(bank[k % 2][:, c * P:(c + 1) * P], ue[:, k % S4, c * P:(c + 1) * P], ident[:])
                ins.then_inc(ueT_psum, 1)

            def first_layer(q, k):
                i = num(q, k)
                pe.wait_ge(xfTe_ready, i + 1)
                wait_from(pe, h_ready, i - 1)
                pe.wait_ge(w1_in[k % S4], (q + k // S4 + 1) * 16)
                for m in range(HC):
                    for c in range(KC):
                        ins = pe.matmul(bank[2 + k % 2][:, m * P:(m + 1) * P], w1s[:, k % S4, c, m * P:(m + 1) * P], xfTe[:, k % 2, c, :],
                                        start=(c == 0), stop=(c == KC - 1))
                ins.then_inc(h_psum, 1)

            def second_layer(q, k):
                i = num(q, k)
                e = pe.value_load(tab_e[0:1, ds1(q, k)], min_val=0, max_val=EX - 1)
                pe.wait_ge(h_ready, i + 1)
                wait_from(pe, ye_ready, i - 1)
                for m in range(HC):
                    ins = pe.matmul(bank[4 + k % 2][:, 0:D], hT[:, k % 2, m, :], w2e[:, bass.ds(e, 1), m, :].rearrange("p a d -> p (a d)"),
                                    start=(m == 0), stop=(m == HC - 1))
                ins.then_inc(ye_psum, 1)

            def head(c):
                pe.wait_ge(w2_in, 16)
                pe.wait_ge(table_ready, c + 1)
                u_transposes(0, T0[c])

            def tile(q, k):
                c = chunk_of(k)
                inner = not isinstance(q, int)
                first_layer(q, k)
                if inner or k + 1 < T0[c + 1]:
                    u_transposes(q, k + 1)
                if inner or k > T0[c]:
                    second_layer(q, k - 1)
                if not inner and k + 1 == T0[c + 1]:
                    second_layer(q, k)

            run_all(pe, {"group": group, "mix": mix, "residual": residual, "z": z, "route": route, "table": table,
                         "head": head, "tile": tile})


def kernel(**inputs):
    import numpy as _np
    import concourse.bacc as _bacc
    from concourse import mybir as _mybir
    from concourse.bass_utils import run_bass_kernel_spmd as _run

    def cols(a, p):
        return _np.ascontiguousarray(_np.asarray(a).reshape(-1, p).T)

    plain = {k: _np.ascontiguousarray(v) for k, v in inputs.items()}
    laid = {
        "x": plain["x"],
        "src": cols(plain["src"], EP), "dst": cols(plain["dst"], EP), "edge_weight": cols(plain["edge_weight"], EP),
        "gnn_eps": plain["L0_gnn_eps"], "gnn_w1": plain["L0_gnn_w1"], "gnn_b1": cols(plain["L0_gnn_b1"], P),
        "gnn_w2": plain["L0_gnn_w2"], "gnn_b2": plain["L0_gnn_b2"],
        "Wq": plain["L0_mix_Wq"], "bq": cols(plain["L0_mix_bq"], P),
        "Wk": plain["L0_mix_Wk"], "bk": plain["L0_mix_bk"],
        "Wv": plain["L0_mix_Wv"], "bv": plain["L0_mix_bv"],
        "Wfc": plain["L0_mix_Wfc"], "bfc": plain["L0_mix_bfc"],
        "gamma": cols(plain["L0_ffn_gamma"], P), "beta": cols(plain["L0_ffn_beta"], P),
        "Wr": plain["L0_ffn_Wr"], "br": plain["L0_ffn_br"],
        "W1": plain["L0_ffn_W1"], "b1": cols(plain["L0_ffn_b1"], P),
        "W2": plain["L0_ffn_W2"], "b2": plain["L0_ffn_b2"],
    }
    nc = _bacc.Bacc("TRN2", target_bir_lowering=False, num_devices=1)
    args = [nc.dram_tensor(f"in_{k}", v.shape, _mybir.dt.from_np(v.dtype), kind="ExternalInput").ap() for k, v in laid.items()]
    out = nc.dram_tensor("out_0", (N, D), _mybir.dt.float32, kind="ExternalOutput").ap()
    build(nc, *args, out)
    r = _run(nc, [{f"in_{k}": v for k, v in laid.items()}], core_ids=[0])
    return r.results[0]["out_0"]
```

```python
from contextlib import ExitStack

import numpy as np
import concourse.bass as bass
from concourse import mybir

F32 = mybir.dt.float32
BF16 = mybir.dt.bfloat16
I32 = mybir.dt.int32
U32 = mybir.dt.uint32
ALU = mybir.AluOpType
ACT = mybir.ActivationFunctionType
AX_X = mybir.AxisListType.X

P = 128
N, D = 3125, 256
KC = D // P
TP = 125
NT = N // TP
BT = 5
NB = NT // BT
EDGES = 53125
EP = 125
ET = EDGES // EP
G = 5
NG = ET // G
W = 64
RING = 4
NWIN = -(-N // W)
HEADS = 8
DK = D // HEADS
EX, HID = 8, 512
HC = HID // P
S4 = 4
LN_EPS = 1e-5
NCH = NB
CHUNKS = tuple((b, 1) for b in range(NCH))
MT = [(2 * TP * BT * nb + EX * (P - 1)) // P for _, nb in CHUNKS]
T0 = [sum(MT[:c]) for c in range(NCH + 1)]
MTT = T0[NCH]
STRIDE = [-(-TP * BT * nb // P) * P for _, nb in CHUNKS]
LIST0 = [sum(EX * STRIDE[i] + MT[i] * P for i in range(c)) for c in range(NCH + 1)]
SLOTS = LIST0[NCH]
READY = tuple(NG * (b0 + nb) // NB + 1 for b0, nb in CHUNKS[:-1])
LN_EPS = 1e-5


def wait_from(eng, sem, value):
    if isinstance(value, int) and value <= 0:
        return
    eng.wait_ge(sem, value)


def build(nc, x, src, dst, edge_weight, gnn_eps, gnn_w1, gnn_b1, gnn_w2, gnn_b2,
          Wq, bq, Wk, bk, Wv, bv, Wfc, bfc, gamma, beta, Wr, br, W1, b1, W2, b2, out):
    ctx = ExitStack()
    with ctx:
        def sb(name, shape, dt=F32):
            return ctx.enter_context(nc.sbuf_tensor(name, shape, dt))

        def sem(name):
            return ctx.enter_context(nc.semaphore(name))

        xn_rows = nc.dram_tensor("xn_rows", (N, D), F32, kind="Internal").ap()
        u_rows = [nc.dram_tensor(f"u_rows{c}", (nb * BT * TP, D), F32, kind="Internal").ap() for c, (_, nb) in enumerate(CHUNKS)]
        token_list = nc.dram_tensor("token_list", (SLOTS, 1), I32, kind="Internal").ap()
        y_rows = [nc.dram_tensor(f"y_rows{c}", (MT[c] * P, D), F32, kind="Internal").ap() for c in range(NCH)]

        bank = [ctx.enter_context(nc.psum_tensor(f"bank{i}", [P, 512], F32)) for i in range(8)]

        def cutter(region):
            at = [0]

            def piece(n):
                at[0] += n
                return region[:, at[0] - n:at[0]]
            return piece

        xres = sb("xres", [TP, NT, D])
        shared = sb("shared", [P, S4 * KC * HID + 2 * BT * D])
        xn = shared[0:TP, 0:NT * (D + 1)].rearrange("p (t d) -> p t d", d=D + 1)
        piece = cutter(shared)
        w1s = piece(S4 * KC * HID).rearrange("p (s k h) -> p s k h", s=S4, k=KC)
        u = piece(2 * BT * D)[0:TP, :].rearrange("p (s t d) -> p s t d", s=2, t=BT)
        xnT = sb("xnT", [P, KC, N])
        aggT = sb("aggT", [P, KC, N + W])
        ring = sb("ring", [P, RING * G * D])
        msg = ring[0:EP, :].rearrange("p (s d) -> p s d", d=D)
        onehot = sb("onehot", [EP, 2 * G, W])
        w2e = sb("w2e", [P, EX, HC, D])
        b2e = sb("b2e", [P, EX, D])

        piece = cutter(w2e[:].rearrange("p e c d -> p (e c d)"))

        def square():
            return piece(KC * D).rearrange("p (c i) -> p c i", c=KC)
        wq, wk, wv, wf, wkT, wvT, wfT, t1, a2 = (square() for _ in range(9))
        gram = piece(KC * (D + 1)).rearrange("p (c i) -> p c i", c=KC)
        ptm = piece(KC * P).rearrange("p (c i) -> p c i", c=KC)
        rows = piece(7 * D)[0:1, :].rearrange("p (r d) -> p r d", d=D)
        bk_row, bv_row, bfc_row, b2_row, s_row, tl_row, bias_row = (rows[:, i, :] for i in range(7))
        gmin = piece(NG)[0:EP, :]
        gminT = piece(1)[0:NG, :]
        gdiag = piece(NG)[0:NG, :]
        dstf = piece(ET)[0:EP, :].rearrange("p (g j) -> p g j", j=G)
        dstt = sb("dstt", [EP, ET], I32)

        srct = sb("srct", [EP, ET], I32)
        wt = sb("wt", [EP, ET])
        rel = sb("rel", [EP, NG, G])
        basef = sb("basef", [EP, NG])
        basei = sb("basei", [1, NG], I32)
        relmax = sb("relmax", [EP, 1])
        flagf = sb("flagf", [1, 16])
        flagi = sb("flagi", [1, 2], I32)
        idxr = sb("idxr", [EP, RING * G], I32)
        relq = sb("relq", [EP, G])
        curf = sb("curf", [1, 1])
        curi = sb("curi", [1, 1], I32)

        ident = sb("ident", [P, P])
        ones = sb("ones", [P, P])
        onesb = sb("onesb", [P, P], BF16)
        before = sb("before", [P, P], BF16)
        hmask = sb("hmask", [P, P // DK, DK])
        iotaW = sb("iotaW", [P, W])
        iota8 = sb("iota8", [P, EX])
        eoff = sb("eoff", [P, NCH, EX])
        iotaM = sb("iotaM", [P, MTT])
        baseM = sb("baseM", [P, MTT])
        tri = sb("tri", [P, EX, EX])
        tokid = sb("tokid", [TP, NT], I32)
        zlist = sb("zlist", [P, SLOTS // P], I32)

        bqc = sb("bqc", [P, KC])
        mixm = sb("mixm", [P, KC, D])
        gw1 = sb("gw1", [P, KC, D])
        gw2 = sb("gw2", [P, KC, D])
        gb1 = sb("gb1", [P, KC])
        shift = sb("shift", [TP, NT])
        eps1 = sb("eps1", [P, 1])
        gammaT = sb("gammaT", [P, KC])
        betaT = sb("betaT", [P, KC])
        wr = sb("wr", [P, KC, EX])
        brb = sb("brb", [P, EX])
        b1T = sb("b1T", [P, EX * HC])

        st = sb("st", [TP, NT, 6])
        mv = sb("mv", [TP, NT, 2])
        veps = sb("veps", [TP, 2, NT])
        sd = sb("sd", [TP, 2, NT])
        rs = sb("rs", [TP, 3, NT])
        lg = sb("lg", [TP, BT, EX])
        mx = sb("mx", [TP, NT, 8])
        ix = sb("ix", [TP, BT, 8], U32)
        ixf = sb("ixf", [TP, BT, 2])
        pick = sb("pick", [TP, 2, NT, EX])
        m12 = sb("m12", [TP, NT, EX], BF16)
        macc = sb("macc", [TP, NT + NCH, EX], BF16)
        pp = sb("pp", [TP, BT, EX])
        ppm = sb("ppm", [TP, 2, BT, EX])
        posf = sb("posf", [TP, 2, NT])
        posi = sb("posi", [TP, 2, NT], I32)
        diff = sb("diff", [TP, NT])
        exd = sb("exd", [TP, NT])
        den = sb("den", [TP, NT])
        wtop = sb("wtop", [TP, 2, NT])
        cnti = sb("cnti", [TP, 2, EX], I32)
        cntf = sb("cntf", [TP, 5, EX])
        backf = sb("backf", [TP, 2, NT])
        backi = sb("backi", [TP, 2, NT], I32)
        trin = sb("trin", [TP, EX, EX])
        cond = sb("cond", [TP, max(MT), EX])
        tabf = sb("tabf", [TP, 3, max(MT)])
        tab_e = sb("tab_e", [TP, MTT], I32)
        tab_u = sb("tab_u", [TP, MTT], I32)
        tab_b = sb("tab_b", [TP, MTT], I32)

        xfT = sb("xfT", [P, 2, KC, 2 * TP])
        hT = sb("hT", [P, 2, HC, P])
        xfTe = sb("xfTe", [P, 2, KC, P])
        ye = sb("ye", [P, 2, D])
        ue = sb("ue", [P, S4, D])
        tok = sb("tok", [P, S4], I32)

        x_in = [sem(f"x_in{c}") for c in range(NB)]
        edges_in = sem("edges_in")
        mixw_in = sem("mixw_in")
        gnnw_in = sem("gnnw_in")
        eps_in = sem("eps_in")
        ffnw_in = sem("ffnw_in")
        w2_in = sem("w2_in")
        list_zeroed = sem("list_zeroed")
        const_ready = sem("const_ready")
        dve_done = sem("dve_done")
        act_done = sem("act_done")
        var_ready = sem("var_ready")
        sd_ready = sem("sd_ready")
        xn_ready = sem("xn_ready")
        xn_act_ready = sem("xn_act_ready")
        shift_ready = sem("shift_ready")
        xn_stored = sem("xn_stored")
        xnT_psum = sem("xnT_psum")
        xnT_ready = sem("xnT_ready")
        gram_psum = sem("gram_psum")
        mix_psum = sem("mix_psum")
        tl_ready = sem("tl_ready")
        ptm_ready = sem("ptm_ready")
        xbias_ready = sem("xbias_ready")
        mixrow_psum = sem("mixrow_psum")
        mixed_ready = sem("mixed_ready")
        gmin_ready = sem("gmin_ready")
        edge_psum = sem("edge_psum")
        gdiag_ready = sem("gdiag_ready")
        relmax_ready = sem("relmax_ready")
        flag_ready = sem("flag_ready")
        idx_ready = sem("idx_ready")
        turn = sem("turn")
        act_turn = sem("act_turn")
        sp_turn = sem("sp_turn")
        msg_in = [sem(f"msg_in{r}") for r in range(RING)]
        onehot_ready = sem("onehot_ready")
        group_psum = sem("group_psum")
        group_added = sem("group_added")
        r_idx = sem("r_idx")
        r_msg = sem("r_msg")
        r_rel = sem("r_rel")
        r_onehot = sem("r_onehot")
        r_psum = sem("r_psum")
        r_cur = sem("r_cur")
        r_added = sem("r_added")
        z_psum = sem("z_psum")
        z_ready = sem("z_ready")
        y_psum = sem("y_psum")
        x1_ready = sem("x1_ready")
        var2_ready = sem("var2_ready")
        sd2_ready = sem("sd2_ready")
        u_ready = sem("u_ready")
        pick_ready = sem("pick_ready")
        u_stored = sem("u_stored")
        uT_psum = sem("uT_psum")
        xfT_ready = sem("xfT_ready")
        logit_psum = sem("logit_psum")
        rank_psum = sem("rank_psum")
        pos_ready = sem("pos_ready")
        listed = sem("listed")
        count_psum = sem("count_psum")
        exd_ready = sem("exd_ready")
        table_ready = sem("table_ready")
        tok_in = [sem(f"tok_in{s}") for s in range(S4)]
        w1_in = [sem(f"w1_in{s}") for s in range(S4)]
        ue_in = [sem(f"ue_in{s}") for s in range(S4)]
        eturn = sem("eturn")
        ueT_psum = sem("ueT_psum")
        xfTe_ready = sem("xfTe_ready")
        h_psum = sem("h_psum")
        h_ready = sem("h_ready")
        ye_psum = sem("ye_psum")
        ye_ready = sem("ye_ready")
        y_stored = [sem(f"y_stored{s}") for s in range(2)]
        yback_in = [sem(f"yback_in{s}") for s in range(RING * G // 2)]
        res_ready = sem("res_ready")
        out_stored = sem("out_stored")

        diff_ready = sem("diff_ready")
        late_ready = sem("late_ready")
        x_t = x.rearrange("(t p) d -> p t d", p=TP)
        xn_t = xn_rows.rearrange("(t p) d -> p t d", p=TP)
        u_t = [r.rearrange("(t p) d -> p t d", p=TP) for r in u_rows]
        out_t = out.rearrange("(t p) d -> p t d", p=TP)

        picks = []
        PAIRS = [(t, min(2, NT - t)) for t in range(0, NT, 2)]
        ZG = [[(t, min(4, (b0 + nb) * BT - t)) for t in range(b0 * BT, (b0 + nb) * BT, 4)] for b0, nb in CHUNKS]
        ZC = [sum(len(z) for z in ZG[:c]) for c in range(NCH + 1)]
        CONSTS = 13
        TPAIRS = [(t, min(2, (b + 1) * BT - t)) for b in range(NB) for t in range(b * BT, (b + 1) * BT, 2)]
        BP = len(TPAIRS) // NB
        UT, RANK, LOGIT, COUNT = 4, 4, 5, 5
        EPS_STEP = 1
        MIN_TILES = [-(-2 * nb * BT * TP // P) for _, nb in CHUNKS]
        LN_DVE = 3
        TA, GA, WA = 4, 3, 3
        MIX_STEPS = 10
        MIX_LOADS, GNN_LOADS, FFN_LOADS = 9, 3, 6
        FR = RING * G // 2

        PREFIX = []
        for n in range(1, MIX_STEPS + 1):
            PREFIX += [("group", n - 1), ("mix", n)]
        mixrows = [("mixrow", t) for t in range(NT)]
        G0 = 16
        for n in range(MIX_STEPS, G0):
            PREFIX += [("group", n), mixrows.pop(0), mixrows.pop(0)]

        def routing(c):
            return ([(("z", c), 1, 1), (("route", c, 0), 1, 1), (("unit", c), 1, 1), (("route", c, 1), 1, 1),
                     (("route", c, 2), 1, 1)]
                    + [(("scatter", c, n), 0, 0) for n in range(BT - 1)] + [(("scatter", c, BT - 1), 1, 1)]
                    + [(("table", c), 1, 1)])

        def between(steps, groups, left):
            out = []
            for step, *counts in steps:
                out.append(step)
                for turn in range(max(counts)):
                    for other, n in zip((groups, left), counts):
                        if other and turn < n:
                            out.append(other.pop(0))
            return out

        def ahead(c, groups, left):
            out = []
            for j in range(TA):
                turn = max(1, len(left) - (S4 - 1 - j)) if left else 1
                for _ in range(turn):
                    for other in (groups, left):
                        if other:
                            out.append(other.pop(0))
                out.append(("tokens", c, j))
                if j > 0:
                    out.append(("row", c, j - 1))
            return out + [("head", c)]

        def chunk_of_node_tile(t):
            return max(c for c in range(NCH) if CHUNKS[c][0] * BT <= t)

        def tiles(c):
            i = T0[c] + 3
            turns = (T0[c + 1] - S4 - i) // S4
            return ([("tile", n) for n in range(T0[c], i)] + [("tiles", 0, i, turns)]
                    + [("tile", n) for n in range(i + S4 * turns, T0[c + 1])])

        EARLY = [("group", g) for g in range(G0, READY[0])]
        left = []
        for c in range(NCH - 1):
            g = [("group", n) for n in range(READY[c], READY[c + 1] if c + 2 < NCH else NG)]
            EARLY += between(routing(c), g, left)
            EARLY += ahead(c, g, left)
            left = [("tile", n) for n in range(T0[c], T0[c + 1])]
            while g:
                EARLY += [g.pop(0), left.pop(0)]
        LATE = list(mixrows)
        at = 0
        while mixrows:
            at += 1
            if EARLY[at - 1][0] == "group":
                for _ in range(2 if EARLY[at - 1][1] < READY[0] else 1):
                    EARLY.insert(at, mixrows.pop(0))
                    at += 1
        turns = (NG - RING - G0) // S4
        LATE += [("groups", G0, 0, turns)] + [("group", g) for g in range(G0 + S4 * turns, NG)] + [("residual",)]
        for c in range(NCH - 1):
            LATE += [step for step, *_ in routing(c)] + ahead(c, [], [])
            if c < NCH - 2:
                LATE += tiles(c)
        done = MT[NCH - 2] - len(left)
        LATE += [("tile", n) for n in range(T0[NCH - 2], T0[NCH - 2] + done)]
        TAIL_ROUTING = [(step, 0, n) for (step, *_), n in zip(routing(NCH - 1), (1, 1, 1, 2, 1, 0, 0, 0, 0, 1, 1))]
        TAIL = between(TAIL_ROUTING, [], left)
        TAIL += ahead(NCH - 1, [], left)
        TAIL += [("tile", n) for n in range(T0[NCH - 1], T0[NCH])]
        behind, fetched, added = TAIL.index(("table", NCH - 1)), 0, 0
        for item in TAIL[behind:]:
            behind += 1
            if item[0] == "tile" and item[1] >= T0[chunk_of_node_tile(fetched) + 1] + 1 and fetched < CHUNKS[-1][0] * BT:
                TAIL.insert(behind, ("fetch", fetched))
                behind, fetched = behind + 1, fetched + 1
                if fetched - added > 2:
                    TAIL.insert(behind, ("back", added))
                    behind, added = behind + 1, added + 1
        while added < NT:
            if fetched < NT:
                TAIL.append(("fetch", fetched))
                fetched += 1
            if fetched - added > 4 or fetched == NT:
                TAIL.append(("back", added))
                added += 1

        def run(eng, items, do, state=None):
            for kind, *a in items:
                if kind in ("groups", "tiles"):
                    g0, i0, turns = a
                    with eng.Fori(0, turns) as q:
                        for k in range(S4):
                            if kind == "tiles":
                                do["tile"](q, i0 + k)
                            else:
                                do["group"](q, g0 + k)
                elif kind in ("group", "tile"):
                    do[kind](0, a[0])
                elif kind in do:
                    do[kind](*a)

        def run_all(eng, do, mark=None):
            run(eng, PREFIX, do)
            eng.wait_ge(late_ready, 1)
            late = eng.value_load(flagi[0:1, 1:2], min_val=0, max_val=1)
            at = list(mark) if mark else None
            with eng.If(late == 0):
                run(eng, EARLY, do)
            with eng.If(late == 1):
                if mark:
                    end, mark[:] = list(mark), at
                run(eng, LATE, do)
                assert not mark or mark == end
            run(eng, TAIL, do)

        def chunk_of(i):
            return max(c for c in range(NCH) if T0[c] <= i)

        def num(q, k):
            return q * S4 + k

        def if_used(eng, q, k, do, leave):
            if not isinstance(q, int) or k < T0[chunk_of(k)] + MIN_TILES[chunk_of(k)]:
                do()
                return
            used = eng.value_load(tab_u[0:1, k:k + 1], min_val=0, max_val=1)
            with eng.If(used == 1):
                do()
            with eng.If(used == 0):
                leave()

        def ds1(q, k):
            return slice(k, k + 1) if isinstance(q, int) else bass.ds(q * S4 + k, 1)

        block = ctx.enter_context(nc.Block())

        @block.sync
        def _(sp):
            for c in range(NB):
                sp.dma_start(xres[:, c * BT:(c + 1) * BT, :], x_t[:, c * BT:(c + 1) * BT, :]).then_inc(x_in[c], 16)
                if c == 0:
                    sp.dma_start(srct[:], src).then_inc(edges_in, 16)
                    sp.dma_start(dstt[:], dst).then_inc(edges_in, 16)
                    sp.dma_start(wt[:], edge_weight).then_inc(edges_in, 16)
            for c in range(NB):
                sp.wait_ge(xn_ready, c + 1)
                sp.wait_ge(xn_act_ready, c + 1)
                sp.dma_start(xn_t[:, c * BT:(c + 1) * BT, :], xn[:, c * BT:(c + 1) * BT, 0:D]).then_inc(xn_stored, 16)
            for w, t in ((Wk, wk), (Wv, wv), (Wfc, wf), (Wq, wq)):
                sp.dma_start(t[:, :, :], w.rearrange("(c p) i -> p c i", p=P)).then_inc(mixw_in, 16)
            for v, r in ((bk, bk_row), (bv, bv_row), (bfc, bfc_row), (gnn_b2, b2_row)):
                sp.dma_start(r, v.rearrange("(a n) -> a n", a=1)).then_inc(mixw_in, 16)
            sp.dma_start(bqc[:], bq).then_inc(mixw_in, 16)
            for w, t in ((gnn_w1, gw1), (gnn_w2, gw2)):
                sp.dma_start(t[:], w.rearrange("(c p) i -> p c i", p=P)).then_inc(gnnw_in, 16)
            sp.dma_start(gb1[:], gnn_b1).then_inc(gnnw_in, 16)
            sp.dma_start(gammaT[:], gamma).then_inc(ffnw_in, 16)
            sp.dma_start(betaT[:], beta).then_inc(ffnw_in, 16)
            sp.dma_start(wr[:], Wr.rearrange("(c p) e -> p c e", p=P)).then_inc(ffnw_in, 16)
            sp.dma_start(brb[:], br.rearrange("(a n) -> a n", a=1).broadcast_to([P, EX])).then_inc(ffnw_in, 16)
            sp.dma_start(b1T[:], b1).then_inc(ffnw_in, 16)
            sp.dma_start(b2e[:].rearrange("p e d -> p (e d)"),
                          b2.rearrange("e d -> (e d)").rearrange("(a n) -> a n", a=1).broadcast_to([P, EX * D])).then_inc(ffnw_in, 16)
            sp.wait_ge(const_ready, CONSTS)
            sp.dma_start(token_list.rearrange("(p k) a -> p (k a)", p=P), zlist[:]).then_inc(list_zeroed, 16)
            sp.wait_ge(mix_psum, 10)
            sp.dma_start(w2e[:].rearrange("p e c d -> p (e c) d"), W2.rearrange("e (c p) d -> p (e c) d", p=P)).then_inc(w2_in, 16)
            def route(c, st):
                b = CHUNKS[c][0] + st
                if st < CHUNKS[c][1]:
                    sp.wait_ge(u_ready, b + 1)
                    sp.dma_start(u_t[c][:, st * BT:(st + 1) * BT, :], u[:, b % 2, :, :]).then_inc(u_stored, 16)

            def load_tokens(q, k):
                at = sp.value_load(tab_b[0:1, ds1(q, k)], min_val=0, max_val=SLOTS - P)
                if k >= S4:
                    sp.wait_ge(ue_in[k % S4], (q + k // S4) * 16)
                sp.sem_inc(sp_turn, 1)
                sp.dma_start(tok[:, k % S4:k % S4 + 1], token_list[bass.ds(at, P), :]).then_inc(tok_in[k % S4], 16)

            def load_w1(q, k):
                e = sp.value_load(tab_e[0:1, ds1(q, k)], min_val=0, max_val=EX - 1)
                wait_from(sp, h_psum, num(q, k) - S4 + 1)
                sp.sem_inc(sp_turn, 1)

                def load():
                    sp.dma_start(w1s[:, k % S4, :, :], W1.rearrange("e (k p) h -> e p k h", p=P)[bass.ds(e, 1), :, :, :]
                                 .rearrange("e p k h -> p (e k) h")).then_inc(w1_in[k % S4], 16)
                if_used(sp, q, k, load, lambda: sp.sem_inc(w1_in[k % S4], 16))

            def tokens(c, j):
                if j == 0:
                    sp.wait_ge(table_ready, c + 1)
                    sp.wait_ge(listed, 2 * (CHUNKS[c][0] + CHUNKS[c][1]) * BT * 16)
                load_tokens(0, T0[c] + j)
                if j < WA:
                    load_w1(0, T0[c] + j)

            def tile(q, k):
                inner = not isinstance(q, int)
                last = T0[chunk_of(k) + 1] - 1
                if inner or k + TA <= last:
                    load_tokens(q, k + TA)
                if inner or k + WA <= last:
                    load_w1(q, k + WA)

            def back(t):
                sp.wait_ge(res_ready, t + 1)
                sp.dma_start(out_t[:, t, :], xres[:, t, :]).then_inc(out_stored, 16)

            run_all(sp, {"group": lambda q, k: None, "route": route, "tokens": tokens, "tile": tile, "back": back})
            sp.wait_ge(out_stored, NT * 16)

        @block.gpsimd
        def _(pool):
            def const(ins):
                ins.then_inc(const_ready, 1)
            const(pool.memset(ident[:], 0.0))
            const(pool.memset(ones[:], 1.0))
            const(pool.memset(xn[:, :, D:D + 1], 1.0))
            const(pool.memset(onesb[:], 1.0))
            const(pool.memset(hmask[:], 1.0 / N))
            const(pool.memset(tri[:], 1.0))
            pool.iota(iotaW[:], [[1, W]], base=0, channel_multiplier=0, allow_small_or_imprecise_dtypes=True)
            pool.iota(iota8[:], [[1, EX]], base=0, channel_multiplier=0, allow_small_or_imprecise_dtypes=True)
            for c in range(NCH):
                pool.iota(eoff[:, c, :], [[STRIDE[c], EX]], base=LIST0[c], channel_multiplier=0, allow_small_or_imprecise_dtypes=True)
                pool.iota(iotaM[:, T0[c]:T0[c + 1]], [[1, MT[c]]], base=0, channel_multiplier=0, allow_small_or_imprecise_dtypes=True)
                pool.iota(baseM[:, T0[c]:T0[c + 1]], [[P, MT[c]]], base=LIST0[c], channel_multiplier=0, allow_small_or_imprecise_dtypes=True)
            for c, (b0, nb) in enumerate(CHUNKS):
                ins = pool.iota(tokid[:, b0 * BT:(b0 + nb) * BT], [[TP, nb * BT]], base=0, channel_multiplier=1)
            const(ins)
            const(pool.memset(zlist[:], 0))
            pool.wait_ge(const_ready, 8)
            const(pool.affine_select(out=ident[:], in_=ident[:], compare_op=ALU.not_equal, fill=1.0, base=0,
                                     pattern=[[-1, P]], channel_multiplier=1))
            const(pool.affine_select(out=before[:], in_=onesb[:], compare_op=ALU.is_gt, fill=0.0, base=0,
                                     pattern=[[1, P]], channel_multiplier=-1))
            const(pool.affine_select(out=hmask[:], in_=hmask[:], compare_op=ALU.is_ge, fill=0.0, base=0,
                                     pattern=[[-DK, P // DK], [0, DK]], channel_multiplier=1))
            pool.wait_ge(const_ready, 11)
            const(pool.affine_select(out=hmask[:], in_=hmask[:], compare_op=ALU.is_ge, fill=0.0, base=DK - 1,
                                     pattern=[[DK, P // DK], [0, DK]], channel_multiplier=-1))
            const(pool.affine_select(out=tri[:], in_=tri[:], compare_op=ALU.is_ge, fill=0.0, base=0,
                                     pattern=[[1, EX], [-1, EX]], channel_multiplier=0))
            pool.memset(macc[:], 0.0).then_inc(const_ready, 1)

            pool.wait_ge(xn_stored, NB * 16)

            def gather(q, k):
                r = k % RING
                pool.wait_ge(idx_ready, num(q, k) + 1)
                pool.sem_inc(turn, 1)
                for j in range(G):
                    pool.indirect_dma_start(out=msg[:, r * G + j, :], out_offset=None, in_=xn_rows,
                                            in_offset=bass.IndirectOffsetOnAxis(ap=idxr[:, r * G + j:r * G + j + 1], axis=0)
                                            ).then_inc(msg_in[r], 16)

            def group(q, k):
                if not isinstance(q, int) or k + RING < NG:
                    gather(q, k + RING)

            def residual():
                wide = pool.value_load(flagi[0:1, 0:1], min_val=0, max_val=1)
                with pool.If(wide == 1):
                    with pool.Fori(0, NG) as g:
                        pool.wait_ge(r_idx, g + 1)
                        pool.sem_inc(turn, 1)
                        for j in range(G):
                            pool.indirect_dma_start(out=msg[:, j, :], out_offset=None, in_=xn_rows,
                                                    in_offset=bass.IndirectOffsetOnAxis(ap=idxr[:, j:j + 1], axis=0)
                                                    ).then_inc(r_msg, 16)

            def scatter(c, n):
                b = CHUNKS[c][0]
                if b + n == 0:
                    pool.wait_ge(list_zeroed, 16)
                if n == 0:
                    pool.wait_ge(pos_ready, b + 1)
                t = b * BT + n
                for s in range(2):
                    pool.indirect_dma_start(out=token_list, out_offset=bass.IndirectOffsetOnAxis(ap=posi[:, s, t:t + 1], axis=0),
                                            in_=tokid[:, t:t + 1], in_offset=None).then_inc(listed, 16)

            def gather_tokens(q, k):
                wait_from(pool, ueT_psum, num(q, k) - S4 + 1)
                if not isinstance(q, int):
                    pool.sem_inc(eturn, 1)
                pool.wait_ge(tok_in[k % S4], (q + k // S4 + 1) * 16)
                if not isinstance(q, int):
                    pool.sem_inc(eturn, 1)
                pool.indirect_dma_start(out=ue[:, k % S4, :], out_offset=None, in_=u_rows[chunk_of(k)],
                                        in_offset=bass.IndirectOffsetOnAxis(ap=tok[:, k % S4:k % S4 + 1], axis=0)).then_inc(ue_in[k % S4], 16)

            def row(c, j):
                if j == 0:
                    pool.wait_ge(u_stored, (CHUNKS[c][0] + CHUNKS[c][1]) * 16)
                gather_tokens(0, T0[c] + j)

            def tile(q, k):
                if not isinstance(q, int) or k + GA < T0[chunk_of(k) + 1]:
                    gather_tokens(q, k + GA)

            def fetch(t):
                c = chunk_of_node_tile(t)
                if t == 0:
                    pool.wait_ge(group_psum, NG)
                if t == CHUNKS[c][0] * BT:
                    for s in range(2):
                        pool.wait_ge(y_stored[s], (T0[c + 1] + 1 - s) // 2 * 16)
                    pool.wait_ge(table_ready, c + 1)
                s = t % FR
                if t >= FR:
                    pool.wait_ge(res_ready, t - FR + 1)
                for a in range(2):
                    pool.indirect_dma_start(out=msg[:, 2 * s + a, :], out_offset=None, in_=y_rows[c],
                                            in_offset=bass.IndirectOffsetOnAxis(ap=backi[:, a, t:t + 1], axis=0)).then_inc(yback_in[s], 16)

            for g in range(RING):
                gather(0, g)
            run_all(pool, {"group": group, "residual": residual, "scatter": scatter, "row": row, "tile": tile, "fetch": fetch})

        @block.scalar
        def _(act):
            act.dma_start(eps1[:], gnn_eps.rearrange("(a n) -> a n", a=1).broadcast_to([P, 1])).then_inc(eps_in, 16)
            def copy_idx(q, k):
                r = k % RING
                act.activation(idxr[:, r * G:(r + 1) * G], srct[:, bass.ds(num(q, k) * G, G)], ACT.Copy).then_inc(idx_ready, 1)

            def evac_pair(n):
                t0, nt = PAIRS[n]
                act.wait_ge(xnT_psum, n + 1)
                v = bank[n % 2][:, 0:KC * nt * TP].rearrange("p (c n) -> p c n", c=KC)
                cols = slice(t0 * TP, (t0 + nt) * TP)
                act.activation(xnT[:, :, cols], v, ACT.Copy)
                act.activation(aggT[:, :, cols], v, ACT.Identity, scale=eps1[:, 0:1]).then_inc(xnT_ready, 1)

            pairs = list(range(len(PAIRS)))
            for c in range(NB + 1):
                if c < NB:
                    act.wait_ge(var_ready, c + 1)
                    act.activation(sd[:, 0, c * BT:(c + 1) * BT], veps[:, 0, c * BT:(c + 1) * BT], ACT.Sqrt).then_inc(sd_ready, 1)
                if c > 0:
                    act.wait_ge(shift_ready, c)
                    for t in range((c - 1) * BT + LN_DVE, c * BT):
                        ins = act.activation(xn[:, t, 0:D], xres[:, t, :], ACT.Identity, scale=rs[:, 0, t:t + 1], bias=shift[:, t:t + 1])
                    ins.then_inc(xn_act_ready, 1)
                if c == 1:
                    act.wait_ge(dve_done, EPS_STEP)
                for _ in range(2 if c > 1 else 0):
                    evac_pair(pairs.pop(0))
                if c == 2:
                    act.wait_ge(edges_in, 48)
                    for g in range(RING):
                        copy_idx(0, g)
            for n in pairs:
                evac_pair(n)
            act.wait_ge(gram_psum, 1)
            act.activation(gram[:, 0, :], bank[2][:, 0:D + 1], ACT.Copy)
            act.activation(gram[:, 1, :], bank[3][:, 0:D + 1], ACT.Copy).then_inc(act_done, 1)

            def flat(a):
                return a.rearrange("p c i -> p (c i)")

            def mix(n):
                o_i = {1: (flat(wkT), bank[4][:, :]), 2: (flat(wvT), bank[5][:, :]), 3: (flat(wfT), bank[4][:, :]),
                       4: (s_row, bank[4][0:1, 0:D]), 5: (flat(t1), bank[0][:, :]), 7: (flat(a2), bank[2][:, :]),
                       8: (flat(mixm[:]), bank[3][:, :]), 9: (bias_row, bank[4][0:1, 0:D])}
                if n in o_i:
                    act.wait_ge(mix_psum, n)
                    act.activation(*o_i[n], ACT.Copy).then_inc(act_done, 1)

            def group(q, k):
                if not isinstance(q, int) or k + RING < NG:
                    act.wait_ge(group_psum, num(q, k) + 1)
                    copy_idx(q, k + RING)

            def residual():
                wide = act.value_load(flagi[0:1, 0:1], min_val=0, max_val=1)
                with act.If(wide == 1):
                    act.wait_ge(group_psum, NG)
                    act.activation(idxr[:, 0:G], srct[:, 0:G], ACT.Copy).then_inc(r_idx, 1)
                    with act.Fori(1, NG) as g:
                        act.wait_ge(r_psum, g * (NWIN - 1))
                        act.activation(idxr[:, 0:G], srct[:, bass.ds(g * G, G)], ACT.Copy).then_inc(r_idx, 1)

            def z(c):
                act.wait_ge(gnnw_in, GNN_LOADS * 16)
                act.wait_ge(ffnw_in, FFN_LOADS * 16)
                for n, (t0, nt) in enumerate(ZG[c]):
                    act.wait_ge(z_psum, ZC[c] + n + 1)
                    for m in range(KC):
                        ins = act.activation(aggT[:, m, t0 * TP:(t0 + nt) * TP], bank[4 + m][:, 0:nt * TP], ACT.Relu,
                                             bias=gb1[:, m:m + 1])
                    ins.then_inc(z_ready, 1)

            def root(b, s):
                act.wait_ge(var2_ready, 2 * b + s + 1)
                act.activation(sd[:, s, b * BT:(b + 1) * BT], veps[:, s, b * BT:(b + 1) * BT], ACT.Sqrt).then_inc(sd2_ready, 1)

            def unit(c):
                root(CHUNKS[c][0], 1)

            def route(c, st):
                b0, nb = CHUNKS[c]
                b = b0 + st
                if st < nb:
                    root(b, 0)
                if 1 <= st <= nb:
                    for n in range((b - 1) * BP, b * BP):
                        act.wait_ge(uT_psum, n + 1)
                        wait_from(act, logit_psum, n - 1)
                        w = TPAIRS[n][1] * TP
                        for i in range(KC):
                            ins = act.activation(xfT[:, n % 2, i, 0:w], bank[UT][:, i * w:(i + 1) * w], ACT.Identity,
                                                 scale=gammaT[:, i:i + 1], bias=betaT[:, i:i + 1])
                        ins.then_inc(xfT_ready, 1)

            def table(c):
                if c == NCH - 1:
                    act.wait_ge(diff_ready, 1)
                    act.activation(exd[:], diff[:], ACT.Exp).then_inc(exd_ready, 1)
                act.wait_ge(table_ready, c + 1)

            def store_y(q, k):
                act.wait_ge(ye_ready, num(q, k) + 1)
                act.sem_inc(act_turn, 1)
                c = chunk_of(k)
                at = num(q, k - T0[c]) * P
                act.dma_start(y_rows[c][slice(at, at + P) if isinstance(q, int) else bass.ds(at, P), :],
                              ye[:, k % 2, :]).then_inc(y_stored[k % 2], 16)

            def tile(q, k):
                i = num(q, k)
                e = act.value_load(tab_e[0:1, ds1(q, k)], min_val=0, max_val=EX - 1)
                wait_from(act, ye_psum, i - 1)
                act.wait_ge(h_psum, i + 1)
                for m in range(HC):
                    ins = act.activation(hT[:, k % 2, m, :], bank[1 + k % 2][:, m * P:(m + 1) * P], ACT.Gelu,
                                         bias=b1T[:, bass.ds(e * HC + m, 1)])
                ins.then_inc(h_ready, 1)
                inner = not isinstance(q, int)
                if inner or k - 2 >= T0[chunk_of(k)]:
                    store_y(q, k - 2)
                if not inner and k + 1 == T0[chunk_of(k) + 1]:
                    store_y(0, k - 1)
                    store_y(0, k)

            run_all(act, {"group": group, "mix": mix, "residual": residual, "z": z, "route": route, "unit": unit, "table": table, "tile": tile})

        @block.vector
        def _(dve):
            steps = [0]

            def link(ins):
                steps[0] += 1
                ins.then_inc(dve_done, 1)
                dve.wait_ge(dve_done, steps[0])

            dve.wait_ge(eps_in, 16)
            link(dve.tensor_scalar(eps1[:], eps1[:], 1.0, None, ALU.add))

            def statistics(c):
                ts = slice(c * BT, (c + 1) * BT)
                dve.wait_ge(x_in[c], 16)
                for t in range(c * BT, (c + 1) * BT):
                    ins = dve.bn_stats(st[:, t, :], xres[:, t, :])
                link(ins)
                for t in range(c * BT, (c + 1) * BT):
                    ins = dve.bn_aggr(mv[:, t, :], st[:, t, :])
                link(ins)
                dve.tensor_scalar(veps[:, 0, ts], mv[:, ts, 1], LN_EPS, None, ALU.add).then_inc(var_ready, 1)

            def normalise(c):
                ts = slice(c * BT, (c + 1) * BT)
                dve.wait_ge(sd_ready, c + 1)
                link(dve.reciprocal(rs[:, 0, ts], sd[:, 0, ts]))
                dve.scalar_tensor_tensor(out=shift[:, ts], in0=mv[:, ts, 0], scalar=-1.0, in1=rs[:, 0, ts], op0=ALU.mult,
                                         op1=ALU.mult).then_inc(shift_ready, 1)
                for t in range(c * BT, c * BT + LN_DVE):
                    ins = dve.tensor_scalar(xn[:, t, 0:D], xres[:, t, :], mv[:, t, 0:1], rs[:, 0, t:t + 1], ALU.subtract, ALU.mult)
                ins.then_inc(xn_ready, 1)

            def edges(part):
                if part == 0:
                    dve.wait_ge(edges_in, 48)
                    link(dve.tensor_copy(dstf.rearrange("p g j -> p (g j)"), dstt[:]))
                    dve.tensor_reduce(gmin, dstf, AX_X, ALU.min).then_inc(gmin_ready, 1)
                if part == 1:
                    dve.wait_ge(const_ready, CONSTS + 1)
                    dve.wait_ge(edge_psum, 1)
                    link(dve.tensor_reduce(gminT, bank[5][0:NG, 0:EP], AX_X, ALU.min))
                    dve.tensor_scalar(gdiag, ident[0:NG, 0:NG], gminT, None, ALU.mult).then_inc(gdiag_ready, 1)
                if part == 2:
                    dve.wait_ge(edge_psum, 2)
                    dve.tensor_copy(basei[:], bank[5][0:1, P:P + NG])
                    link(dve.tensor_copy(basef[:], bank[5][0:EP, P:P + NG]))
                    link(dve.tensor_tensor(rel[:], dstf, basef[:].unsqueeze(2).broadcast_to([EP, NG, G]), ALU.subtract))
                    dve.tensor_reduce(relmax[:], rel[:].rearrange("p g j -> p (g j)"), AX_X, ALU.max).then_inc(relmax_ready, 1)
                if part == 3:
                    dve.wait_ge(edge_psum, 3)
                    link(dve.tensor_reduce(flagf[:, 0:1], bank[5][0:1, 256:256 + EP], AX_X, ALU.max))
                    dve.tensor_scalar(flagf[:, 1:2], flagf[:, 0:1], float(W), None, ALU.is_ge).then_inc(flag_ready, 1)
                    R = len(READY)
                    for c, g in enumerate(READY):
                        ins = dve.tensor_reduce(flagf[:, 2 + c:3 + c], basef[0:1, g:NG], AX_X, ALU.min)
                    link(ins)
                    for c in range(R):
                        last_node = (CHUNKS[c][0] + CHUNKS[c][1]) * BT * TP - 1
                        ins = dve.tensor_scalar(flagf[:, 2 + R + c:3 + R + c], flagf[:, 2 + c:3 + c], float(last_node), None, ALU.is_le)
                    link(ins)
                    link(dve.tensor_reduce(flagf[:, 2 + 2 * R:3 + 2 * R], flagf[:, 2 + R:2 + 2 * R], AX_X, ALU.max))
                    link(dve.tensor_tensor(flagf[:, 3 + 2 * R:4 + 2 * R], flagf[:, 2 + 2 * R:3 + 2 * R], flagf[:, 1:2], ALU.max))
                    dve.tensor_copy(flagi[:, 0:1], flagf[:, 1:2])
                    dve.tensor_copy(flagi[:, 1:2], flagf[:, 3 + 2 * R:4 + 2 * R]).then_inc(late_ready, 1)

            for c in range(NB):
                statistics(c)
                if c > 0:
                    normalise(c - 1)
                if c % 2 == 0:
                    edges(c // 2)
            normalise(NB - 1)
            edges(3)

            rel_flat = rel[:].rearrange("p g j -> p (g j)")

            def onehots(q, k):
                g = num(q, k)
                for j in range(G):
                    ins = dve.tensor_scalar(onehot[:, k % 2 * G + j, :], iotaW[0:EP, :], rel_flat[:, bass.ds(g * G + j, 1)],
                                            wt[:, bass.ds(g * G + j, 1)], ALU.is_equal, ALU.mult)
                ins.then_inc(onehot_ready, 1)

            def group(q, k):
                g = num(q, k)
                if k == 0:
                    dve.wait_ge(xnT_ready, len(PAIRS))
                dve.wait_ge(group_psum, g + 1)
                if not isinstance(q, int) or k + 2 < NG:
                    onehots(q, k + 2)
                base = dve.value_load(basei[0:1, bass.ds(g, 1)], min_val=0, max_val=N - 1)
                wait_from(dve, group_added, g)
                window = aggT[:, :, bass.ds(base, W)]
                dve.tensor_tensor(window, window, bank[6 + k % 2][:, :].rearrange("p (c n) -> p c n", c=KC)[:, :, 0:W],
                                  ALU.add).then_inc(group_added, 1)

            def mix(n):
                if n == 5:
                    dve.wait_ge(mix_psum, 5)
                    dve.scalar_tensor_tensor(out=tl_row, in0=bk_row, scalar=float(N), in1=bank[1][0:1, 0:D], op0=ALU.mult,
                                             op1=ALU.add).then_inc(tl_ready, 1)
                if n == 6:
                    dve.wait_ge(mix_psum, 6)
                    for c in range(KC):
                        ins = dve.tensor_tensor(ptm[:, c, :], bank[1][:, 256 + c * P:256 + (c + 1) * P],
                                                hmask[:].rearrange("p b d -> p (b d)"), ALU.mult)
                    ins.then_inc(ptm_ready, 1)
                if n == MIX_STEPS:
                    dve.wait_ge(mix_psum, MIX_STEPS)
                    link(dve.tensor_tensor(xres[:], xres[:], bank[4][0:TP, 256:256 + D].unsqueeze(1).broadcast_to([TP, NT, D]), ALU.add))
                    dve.sem_inc(xbias_ready, 1)

            def residual():
                wide = dve.value_load(flagi[0:1, 0:1], min_val=0, max_val=1)
                with dve.If(wide == 1):
                    dve.wait_ge(group_added, NG)
                    with dve.Fori(0, NG) as g:
                        dve.tensor_copy(relq[:], rel_flat[:, bass.ds(g * G, G)]).then_inc(r_rel, 1)
                        dve.tensor_copy(curf[:], basef[0:1, bass.ds(g, 1)]).then_inc(r_rel, 1)
                        with dve.Fori(0, NWIN - 1) as w:
                            n = g * (NWIN - 1) + w
                            c = g * 2 + n * 2 + 2
                            dve.wait_ge(r_rel, c)
                            dve.tensor_scalar(relq[:], relq[:], float(W), None, ALU.subtract).then_inc(r_rel, 1)
                            dve.tensor_scalar(curf[:], curf[:], float(W), float(N), ALU.add, ALU.min).then_inc(r_rel, 1)
                            dve.wait_ge(r_rel, c + 2)
                            dve.tensor_copy(curi[:], curf[:]).then_inc(r_cur, 1)
                            for j in range(G):
                                ins = dve.tensor_scalar(onehot[:, j, :], iotaW[0:EP, :], relq[:, j:j + 1],
                                                        wt[:, bass.ds(g * G + j, 1)], ALU.is_equal, ALU.mult)
                            ins.then_inc(r_onehot, 1)
                            dve.wait_ge(r_cur, n + 1)
                            dve.sem_inc(turn, 1)
                            base = dve.value_load(curi[0:1, 0:1], min_val=0, max_val=N)
                            dve.wait_ge(r_psum, n + 1)
                            window = aggT[:, :, bass.ds(base, W)]
                            dve.tensor_tensor(window, window, bank[6][:, :].rearrange("p (c n) -> p c n", c=KC)[:, :, 0:W],
                                              ALU.add).then_inc(r_added, 1)
                            dve.wait_ge(r_added, n + 1)

            def mixrow(t):
                dve.wait_ge(mixrow_psum, t + 1)
                dve.tensor_tensor(xres[:, t, :], xres[:, t, :], bank[t % 4][0:TP, 0:D], ALU.add).then_inc(mixed_ready, 1)

            def x1_rows(b):
                ts = slice(b * BT, (b + 1) * BT)
                dve.wait_ge(mixed_ready, (b + 1) * BT)
                for t in range(b * BT, (b + 1) * BT):
                    dve.wait_ge(y_psum, t + 1)
                    ins = dve.tensor_tensor(xres[:, t, :], xres[:, t, :], bank[4 + t % 2][0:TP, 0:D], ALU.add)
                    ins.then_inc(x1_ready, 1)
                dve.wait_ge(x1_ready, (b + 1) * BT)
                for t in range(b * BT, (b + 1) * BT):
                    ins = dve.bn_stats(st[:, t, :], xres[:, t, :])
                link(ins)
                for t in range(b * BT, (b + 1) * BT):
                    ins = dve.bn_aggr(mv[:, t, :], st[:, t, :])
                link(ins)
                dve.tensor_scalar(veps[:, 0, ts], mv[:, ts, 1], LN_EPS, None, ALU.add).then_inc(var2_ready, 1)

            def units(b):
                ts = slice(b * BT, (b + 1) * BT)
                dve.wait_ge(sd2_ready, 2 * b + 1)
                link(dve.reciprocal(rs[:, 0, ts], sd[:, 0, ts]))
                link(dve.tensor_tensor(rs[:, 1, ts], rs[:, 0, ts], rs[:, 0, ts], ALU.mult))
                link(dve.tensor_tensor(rs[:, 2, ts], rs[:, 1, ts], mv[:, ts, 1], ALU.mult))
                dve.tensor_scalar(veps[:, 1, ts], rs[:, 2, ts], LN_EPS, None, ALU.add).then_inc(var2_ready, 1)
                dve.wait_ge(sd2_ready, 2 * b + 2)
                link(dve.reciprocal(rs[:, 1, ts], sd[:, 1, ts]))
                link(dve.tensor_tensor(rs[:, 2, ts], rs[:, 0, ts], rs[:, 1, ts], ALU.mult))
                if b >= 2:
                    dve.wait_ge(u_stored, (b - 1) * 16)
                    dve.wait_ge(uT_psum, (b - 1) * BP)
                for t in range(b * BT, (b + 1) * BT):
                    ins = dve.tensor_scalar(u[:, b % 2, t % BT, :], xres[:, t, :], mv[:, t, 0:1], rs[:, 2, t:t + 1], ALU.subtract, ALU.mult)
                ins.then_inc(u_ready, 1)

            def top2(c, b):
                ts = slice(b * BT, (b + 1) * BT)
                dve.wait_ge(logit_psum, (b + 1) * BP)
                link(dve.tensor_tensor(lg[:], bank[LOGIT][0:TP, 0:BT * EX].rearrange("p (t e) -> p t e", e=EX),
                                       brb[0:TP, :].unsqueeze(1).broadcast_to([TP, BT, EX]), ALU.add))
                for t in range(BT):
                    ins = dve.max(mx[:, b * BT + t, :], lg[:, t, :])
                link(ins)
                for t in range(BT):
                    ins = dve.max_index(ix[:, t, :], mx[:, b * BT + t, :], lg[:, t, :])
                link(ins)
                link(dve.tensor_copy(ixf[:], ix[:, :, 0:2]))
                for s in range(2):
                    ins = dve.tensor_tensor(pick[:, s, ts, :], iota8[0:TP, :].unsqueeze(1).broadcast_to([TP, BT, EX]),
                                            ixf[:, :, s:s + 1].broadcast_to([TP, BT, EX]), ALU.is_equal)
                link(ins)
                link(dve.tensor_tensor(m12[:, ts, :], pick[:, 0, ts, :], pick[:, 1, ts, :], ALU.add))
                for t in range(b * BT, (b + 1) * BT):
                    dve.tensor_tensor(macc[:, t + c + 1, :], macc[:, t + c, :], m12[:, t, :], ALU.add).then_inc(pick_ready, 1)
                    dve.wait_ge(pick_ready, t + 1)

            def positions(c, b):
                ts = slice(b * BT, (b + 1) * BT)
                dve.wait_ge(rank_psum, b + 1)
                link(dve.tensor_tensor(pp[:], bank[RANK][0:TP, 0:BT * EX].rearrange("p (t e) -> p t e", e=EX),
                                       eoff[0:TP, c:c + 1, :].broadcast_to([TP, BT, EX]), ALU.add))
                for s in range(2):
                    ins = dve.tensor_tensor(ppm[:, s, :, :], pp[:], pick[:, s, ts, :], ALU.mult)
                link(ins)
                for s in range(2):
                    ins = dve.tensor_reduce(posf[:, s, ts], ppm[:, s, :, :], AX_X, ALU.add)
                link(ins)
                for s in range(2):
                    ins = dve.tensor_copy(posi[:, s, ts], posf[:, s, ts])
                ins.then_inc(pos_ready, 1)

            def route(c, st):
                b0, nb = CHUNKS[c]
                if c == 0 and st == 0:
                    dve.wait_ge(ffnw_in, FFN_LOADS * 16)
                if st < nb:
                    x1_rows(b0 + st)
                if 1 <= st <= nb:
                    top2(c, b0 + st - 1)
                if st >= 2:
                    positions(c, b0 + st - 2)

            def unit(c):
                units(CHUNKS[c][0])

            def table(c):
                b0, nb = CHUNKS[c]
                if c == NCH - 1:
                    dve.tensor_tensor(diff[:], mx[:, :, 1], mx[:, :, 0], ALU.subtract).then_inc(diff_ready, 1)
                M, tl = MT[c], slice(T0[c], T0[c + 1])
                dve.wait_ge(count_psum, c + 1)
                link(dve.tensor_scalar(cnti[:, 0, :], bank[COUNT][0:TP, 448:448 + EX], float(P - 1), None, ALU.add))
                link(dve.tensor_scalar(cnti[:, 1, :], cnti[:, 0, :], P.bit_length() - 1, None, ALU.logical_shift_right))
                link(dve.tensor_copy(cntf[:, 0, :], cnti[:, 1, :]))
                dve.tensor_scalar(cntf[:, 2, :], cntf[:, 0, :], -float(P), float(STRIDE[c]), ALU.mult, ALU.add)
                link(dve.tensor_tensor(trin[:], cntf[:, 0, :].unsqueeze(1).broadcast_to([TP, EX, EX]), tri[0:TP, :, :], ALU.mult))
                link(dve.tensor_reduce(cntf[:, 1, :], trin[:], AX_X, ALU.add))
                cd = cond[:, 0:M, :]
                link(dve.tensor_tensor(cd, cntf[:, 1, :].unsqueeze(1).broadcast_to([TP, M, EX]),
                                       iotaM[0:TP, tl].unsqueeze(2).broadcast_to([TP, M, EX]), ALU.is_le))
                link(dve.tensor_reduce(tabf[:, 0, 0:M], cd, AX_X, ALU.add))
                link(dve.tensor_tensor(cd, cd, cntf[:, 2, :].unsqueeze(1).broadcast_to([TP, M, EX]), ALU.mult))
                link(dve.tensor_reduce(tabf[:, 1, 0:M], cd, AX_X, ALU.add))
                dve.tensor_scalar(tab_e[:, tl], tabf[:, 0, 0:M], float(EX - 1), None, ALU.min)
                dve.tensor_scalar(tab_u[:, tl], tabf[:, 0, 0:M], float(EX), None, ALU.is_lt)
                link(dve.tensor_tensor(tabf[:, 2, 0:M], tabf[:, 1, 0:M], baseM[0:TP, tl], ALU.add))
                link(dve.tensor_tensor(cntf[:, 3, :], cntf[:, 1, :], cntf[:, 0, :], ALU.subtract))
                link(dve.scalar_tensor_tensor(out=cntf[:, 4, :], in0=cntf[:, 3, :], scalar=-float(P), in1=eoff[0:TP, c, :],
                                              op0=ALU.mult, op1=ALU.add))
                for b in range(b0, b0 + nb):
                    ts = slice(b * BT, (b + 1) * BT)
                    for s in range(2):
                        ins = dve.tensor_tensor(ppm[:, s, :, :], pick[:, s, ts, :], cntf[:, 4:5, :].broadcast_to([TP, BT, EX]), ALU.mult)
                    link(ins)
                    for s in range(2):
                        ins = dve.tensor_reduce(backf[:, s, ts], ppm[:, s, :, :], AX_X, ALU.add)
                    link(ins)
                ts = slice(b0 * BT, (b0 + nb) * BT)
                link(dve.tensor_tensor(backi[:, :, ts], posf[:, :, ts], backf[:, :, ts], ALU.subtract))
                dve.tensor_copy(tab_b[:, tl], tabf[:, 2, 0:M]).then_inc(table_ready, 1)
                dve.wait_ge(table_ready, c + 1)
                if c == NCH - 1:
                    dve.wait_ge(exd_ready, 1)
                    link(dve.tensor_scalar(den[:], exd[:], 1.0, None, ALU.add))
                    link(dve.reciprocal(wtop[:, 0, :], den[:]))
                    link(dve.tensor_tensor(wtop[:, 1, :], wtop[:, 0, :], exd[:], ALU.mult))

            def evac_xfT(q, k):
                i = num(q, k)
                wait_from(dve, h_psum, i - 1)
                dve.wait_ge(ueT_psum, i + 1)
                for c in range(KC):
                    ins = dve.tensor_scalar(xfTe[:, k % 2, c, :], bank[0][:, c * P:(c + 1) * P], gammaT[:, c:c + 1],
                                            betaT[:, c:c + 1], ALU.mult, ALU.add)
                ins.then_inc(xfTe_ready, 1)

            def evac_y(q, k):
                i = num(q, k)
                e = dve.value_load(tab_e[0:1, ds1(q, k)], min_val=0, max_val=EX - 1)
                if k >= 2:
                    dve.wait_ge(y_stored[k % 2], (q * (S4 // 2) + k // 2) * 16)
                dve.wait_ge(ye_psum, i + 1)
                dve.tensor_tensor(ye[:, k % 2, :], bank[3][:, 0:D], b2e[:, bass.ds(e, 1), :].rearrange("p a d -> p (a d)"),
                                  ALU.add).then_inc(ye_ready, 1)

            def head(c):
                evac_xfT(0, T0[c])

            def tile(q, k):
                c = chunk_of(k)
                inner = not isinstance(q, int)
                if inner or k + 1 < T0[c + 1]:
                    evac_xfT(q, k + 1)
                if inner or k > T0[c]:
                    evac_y(q, k - 1)
                if not inner and k + 1 == T0[c + 1]:
                    evac_y(q, k)

            def back(t):
                s = t % FR
                dve.wait_ge(yback_in[s], (t // FR + 1) * 32)
                for a in range(2):
                    ins = dve.scalar_tensor_tensor(out=xres[:, t, :], in0=msg[:, 2 * s + a, :], scalar=wtop[:, a, t:t + 1],
                                                   in1=xres[:, t, :], op0=ALU.mult, op1=ALU.add)
                    if a == 0:
                        link(ins)
                ins.then_inc(res_ready, 1)

            dve.memset(aggT[:, :, N:N + W], 0.0)
            onehots(0, 0)
            onehots(0, 1)
            run_all(dve, {"group": group, "mix": mix, "mixrow": mixrow, "residual": residual, "route": route, "unit": unit, "table": table, "head": head,
                          "tile": tile, "back": back}, mark=steps)

        @block.tensor
        def _(pe):
            pe.wait_ge(const_ready, CONSTS)

            def edges(part):
                if part == 0:
                    pe.wait_ge(gmin_ready, 1)
                    pe.transpose(bank[5][0:NG, 0:EP], gmin, ident[0:EP, 0:EP]).then_inc(edge_psum, 1)
                if part == 1:
                    pe.wait_ge(gdiag_ready, 1)
                    pe.matmul(bank[5][0:EP, P:P + NG], ones[0:NG, 0:EP], gdiag, start=True, stop=True).then_inc(edge_psum, 1)
                if part == 2:
                    pe.wait_ge(relmax_ready, 1)
                    pe.transpose(bank[5][0:1, 256:256 + EP], relmax[:], ident[0:EP, 0:EP]).then_inc(edge_psum, 1)

            for n, (t0, nt) in enumerate(PAIRS):
                if n in (0, 2, 7):
                    edges((0, 2, 7).index(n))
                if n >= 2:
                    pe.wait_ge(xnT_ready, n - 1)
                for t in range(t0, t0 + nt):
                    if t % BT == 0 or t == t0:
                        pe.wait_ge(xn_ready, t // BT + 1)
                        pe.wait_ge(xn_act_ready, t // BT + 1)
                    for c in range(KC):
                        o = c * nt * TP + (t - t0) * TP
                        ins = pe.transpose(bank[n % 2][:, o:o + TP], xn[:, t, c * P:(c + 1) * P], ident[0:TP, 0:TP])
                ins.then_inc(xnT_psum, 1)
                for t in range(t0, t0 + nt):
                    for m in range(KC):
                        ins = pe.matmul(bank[2 + m][:, 0:D + 1], xn[:, t, m * P:(m + 1) * P], xn[:, t, :],
                                        start=(t == 0), stop=(t == NT - 1))
            ins.then_inc(gram_psum, 1)

            def mix(n):
                if n <= 3:
                    if n == 1:
                        pe.wait_ge(mixw_in, MIX_LOADS * 16)
                        pe.wait_ge(flag_ready, 1)
                    if n == 3:
                        pe.wait_ge(act_done, 2)
                    w, b = (wk, wv, wf)[n - 1], bank[4 + (n == 2)]
                    for ci in range(KC):
                        for co in range(KC):
                            ins = pe.transpose(b[:, ci * D + co * P:ci * D + (co + 1) * P], w[:, co, ci * P:(ci + 1) * P], ident[:])
                elif n == 4:
                    pe.wait_ge(act_done, 4)
                    for c in range(KC):
                        ins = pe.transpose(bank[4][0:1, c * P:(c + 1) * P], gram[:, c, D:D + 1], ident[:])
                elif n == 5:
                    pe.wait_ge(act_done, 5)
                    pe.wait_ge(xnT_ready, len(PAIRS))
                    for c in range(KC):
                        o = bank[0][:, c * D:(c + 1) * D]
                        for k in range(KC):
                            pe.matmul(o, gram[:, k, c * P:(c + 1) * P], wkT[:, k, :], start=(k == 0), stop=False)
                        pe.matmul(o, s_row[:, c * P:(c + 1) * P], bk_row, start=False, stop=True)
                    for k in range(KC):
                        ins = pe.matmul(bank[1][0:1, 0:D], gram[:, k, D:D + 1], wkT[:, k, :], start=(k == 0), stop=(k == KC - 1))
                elif n == 6:
                    pe.wait_ge(act_done, 6)
                    pe.wait_ge(tl_ready, 1)
                    for c in range(KC):
                        cs = slice(c * P, (c + 1) * P)
                        o = bank[1][:, 256 + c * P:256 + (c + 1) * P]
                        for k in range(KC):
                            pe.matmul(o, wvT[:, k, cs], t1[:, k, cs], start=(k == 0), stop=False)
                        ins = pe.matmul(o, bv_row[:, cs], tl_row[:, cs], start=False, stop=True)
                elif n == 7:
                    pe.wait_ge(ptm_ready, 1)
                    for c in range(KC):
                        ins = pe.matmul(bank[2][:, c * D:(c + 1) * D], ptm[:, c, :], wfT[:, c, :], start=True, stop=True)
                elif n == 8:
                    pe.wait_ge(act_done, 7)
                    for c in range(KC):
                        for k in range(KC):
                            ins = pe.matmul(bank[3][:, c * D:(c + 1) * D], wq[:, k, c * P:(c + 1) * P], a2[:, k, :], start=(k == 0), stop=(k == KC - 1))
                elif n == 9:
                    for k in range(KC):
                        pe.matmul(bank[4][0:1, 0:D], bqc[:, k:k + 1], a2[:, k, :], start=(k == 0), stop=False)
                    pe.matmul(bank[4][0:1, 0:D], ones[0:1, 0:1], bfc_row, start=False, stop=False)
                    ins = pe.matmul(bank[4][0:1, 0:D], ones[0:1, 0:1], b2_row, start=False, stop=True)
                else:
                    pe.wait_ge(act_done, 9)
                    ins = pe.matmul(bank[4][0:TP, 256:256 + D], ones[0:1, 0:TP], bias_row, start=True, stop=True)
                ins.then_inc(mix_psum, 1)

            def group(q, k):
                g, r, b = num(q, k), k % RING, k % 2
                pe.wait_ge(msg_in[r], (q + k // RING + 1) * (16 * G))
                wait_from(pe, group_added, g - 1)
                pe.wait_ge(onehot_ready, g + 1)
                for c in range(KC):
                    for j in range(G):
                        ins = pe.matmul(bank[6 + b][:, c * 256:c * 256 + W], msg[:, r * G + j, c * P:(c + 1) * P],
                                        onehot[:, b * G + j, :], start=(j == 0), stop=(j == G - 1))
                ins.then_inc(group_psum, 1)

            def residual():
                wide = pe.value_load(flagi[0:1, 0:1], min_val=0, max_val=1)
                with pe.If(wide == 1):
                    with pe.Fori(0, NG) as g:
                        pe.wait_ge(r_msg, (g + 1) * (16 * G))
                        pe.sem_inc(turn, 1)
                        with pe.Fori(0, NWIN - 1) as w:
                            n = g * (NWIN - 1) + w
                            pe.wait_ge(r_onehot, n + 1)
                            for c in range(KC):
                                for j in range(G):
                                    ins = pe.matmul(bank[6][:, c * 256:c * 256 + W], msg[:, j, c * P:(c + 1) * P],
                                                    onehot[:, j, :], start=(j == 0), stop=(j == G - 1))
                            ins.then_inc(r_psum, 1)
                    pe.wait_ge(r_added, NG * (NWIN - 1))

            def z(c):
                pe.wait_ge(group_added, READY[c] if c < len(READY) else NG)
                pe.wait_ge(gnnw_in, GNN_LOADS * 16)
                if c:
                    pe.wait_ge(table_ready, c)
                else:
                    pe.wait_ge(xbias_ready, 1)
                for n, (t0, nt) in enumerate(ZG[c]):
                    if n >= 1:
                        pe.wait_ge(z_ready, ZC[c] + n)
                    cols = slice(t0 * TP, (t0 + nt) * TP)
                    for m in range(KC):
                        for k in range(KC):
                            ins = pe.matmul(bank[4 + m][:, 0:nt * TP], gw1[:, k, m * P:(m + 1) * P], aggT[:, k, cols],
                                            start=(k == 0), stop=(k == KC - 1))
                    ins.then_inc(z_psum, 1)

            def y_tile(t):
                wait_from(pe, x1_ready, t - 1)
                o = bank[4 + t % 2][0:TP, 0:D]
                for k in range(KC):
                    ins = pe.matmul(o, aggT[:, k, t * TP:(t + 1) * TP], gw2[:, k, :], start=(k == 0), stop=(k == KC - 1))
                ins.then_inc(y_psum, 1)

            def mixrow(t):
                wait_from(pe, mixed_ready, t - 3)
                for k in range(KC):
                    ins = pe.matmul(bank[t % 4][0:TP, 0:D], xnT[:, k, t * TP:(t + 1) * TP], mixm[:, k, :],
                                    start=(k == 0), stop=(k == KC - 1))
                ins.then_inc(mixrow_psum, 1)

            def transposes(n):
                t0, nt = TPAIRS[n]
                wait_from(pe, xfT_ready, n)
                for t in range(t0, t0 + nt):
                    for c in range(KC):
                        o = (c * nt + t - t0) * TP
                        ins = pe.transpose(bank[UT][:, o:o + TP], u[:, t // BT % 2, t % BT, c * P:(c + 1) * P], ident[0:TP, 0:TP])
                ins.then_inc(uT_psum, 1)

            def logits(n):
                t0, nt = TPAIRS[n]
                pe.wait_ge(xfT_ready, n + 1)
                for t in range(t0, t0 + nt):
                    o = t % BT * EX
                    for c in range(KC):
                        ins = pe.matmul(bank[LOGIT][0:TP, o:o + EX], xfT[:, n % 2, c, (t - t0) * TP:(t - t0 + 1) * TP], wr[:, c, :],
                                        start=(c == 0), stop=(c == KC - 1))
                ins.then_inc(logit_psum, 1)

            def ranks(c, b):
                ts = slice(b * BT, (b + 1) * BT)
                rank = bank[RANK][0:TP, 0:BT * EX]
                pe.matmul(rank, before[0:TP, 0:TP], m12[:, ts, :].rearrange("p t e -> p (t e)"), start=True, stop=False)
                pe.matmul(rank, onesb[0:TP, 0:TP], macc[:, b * BT + c:(b + 1) * BT + c, :].rearrange("p t e -> p (t e)"),
                          start=False, stop=True).then_inc(rank_psum, 1)

            def route(c, st):
                b0, nb = CHUNKS[c]
                b = b0 + st
                if st == 0:
                    pe.wait_ge(z_ready, ZC[c + 1])
                if st < nb:
                    for t in range(b * BT, (b + 1) * BT):
                        y_tile(t)
                if 1 <= st <= nb:
                    pe.wait_ge(u_ready, b)
                    for n in range((b - 1) * BP, b * BP):
                        transposes(n)
                        if n > (b - 1) * BP:
                            logits(n - 1)
                    logits(b * BP - 1)
                if st >= 2:
                    pe.wait_ge(pick_ready, (b - 1) * BT)
                    ranks(c, b - 2)

            def table(c):
                last = CHUNKS[c][0] + CHUNKS[c][1]
                pe.matmul(bank[COUNT][0:TP, 448:448 + EX], onesb[0:TP, 0:TP], macc[:, last * BT + c, :], start=True, stop=True).then_inc(count_psum, 1)

            def u_transposes(q, k, used=True):
                i = num(q, k)
                wait_from(pe, xfTe_ready, i)
                pe.wait_ge(ue_in[k % S4], (q + k // S4 + 1) * 16)
                if not used:
                    pe.sem_inc(ueT_psum, 1)
                    return
                for c in range(KC):
                    ins = pe.transpose(bank[0][:, c * P:(c + 1) * P], ue[:, k % S4, c * P:(c + 1) * P], ident[:])
                ins.then_inc(ueT_psum, 1)

            def first_layer(q, k, used=True):
                i = num(q, k)
                pe.wait_ge(xfTe_ready, i + 1)
                wait_from(pe, h_ready, i - 1 if used else i)
                pe.wait_ge(w1_in[k % S4], (q + k // S4 + 1) * 16)
                if not used:
                    pe.sem_inc(h_psum, 1)
                    return
                for m in range(HC):
                    for c in range(KC):
                        ins = pe.matmul(bank[1 + k % 2][:, m * P:(m + 1) * P], w1s[:, k % S4, c, m * P:(m + 1) * P], xfTe[:, k % 2, c, :],
                                        start=(c == 0), stop=(c == KC - 1))
                ins.then_inc(h_psum, 1)

            def second_layer(q, k, used=True):
                i = num(q, k)
                pe.wait_ge(h_ready, i + 1)
                wait_from(pe, ye_ready, i)
                if not used:
                    pe.sem_inc(ye_psum, 1)
                    return
                e = pe.value_load(tab_e[0:1, ds1(q, k)], min_val=0, max_val=EX - 1)
                for m in range(HC):
                    ins = pe.matmul(bank[3][:, 0:D], hT[:, k % 2, m, :], w2e[:, bass.ds(e, 1), m, :].rearrange("p a d -> p (a d)"),
                                    start=(m == 0), stop=(m == HC - 1))
                ins.then_inc(ye_psum, 1)

            def head(c):
                pe.wait_ge(w2_in, 16)
                pe.wait_ge(table_ready, c + 1)
                pe.wait_ge(mixed_ready, NT)
                u_transposes(0, T0[c])

            def steps(q, k, used=True):
                c = chunk_of(k)
                inner = not isinstance(q, int)
                first_layer(q, k, used)
                if inner or k + 1 < T0[c + 1]:
                    u_transposes(q, k + 1, used)
                if used and (inner or k > T0[c]):
                    second_layer(q, k - 1)
                if used and not inner and k + 1 == T0[c + 1]:
                    second_layer(q, k)

            def tile(q, k):
                c = chunk_of(k)
                if not isinstance(q, int) or k < T0[c] + MIN_TILES[c]:
                    steps(q, k)
                    return
                this = pe.value_load(tab_u[0:1, k:k + 1], min_val=0, max_val=1)
                with pe.If(this == 1):
                    steps(q, k)
                with pe.If(this == 0):
                    steps(q, k, used=False)
                    last = pe.value_load(tab_u[0:1, k - 1:k], min_val=0, max_val=1)
                    with pe.If(last == 1):
                        second_layer(q, k - 1)
                    with pe.If(last == 0):
                        second_layer(q, k - 1, used=False)
                    if k + 1 == T0[c + 1]:
                        second_layer(q, k, used=False)

            run_all(pe, {"group": group, "mix": mix, "mixrow": mixrow, "residual": residual, "z": z, "route": route, "table": table,
                         "head": head, "tile": tile})


def kernel(**inputs):
    import numpy as _np
    import concourse.bacc as _bacc
    from concourse import mybir as _mybir
    from concourse.bass_utils import run_bass_kernel_spmd as _run

    def cols(a, p):
        return _np.ascontiguousarray(_np.asarray(a).reshape(-1, p).T)

    plain = {k: _np.ascontiguousarray(v) for k, v in inputs.items()}
    laid = {
        "x": plain["x"],
        "src": cols(plain["src"], EP), "dst": cols(plain["dst"], EP), "edge_weight": cols(plain["edge_weight"], EP),
        "gnn_eps": plain["L0_gnn_eps"], "gnn_w1": plain["L0_gnn_w1"], "gnn_b1": cols(plain["L0_gnn_b1"], P),
        "gnn_w2": plain["L0_gnn_w2"], "gnn_b2": plain["L0_gnn_b2"],
        "Wq": plain["L0_mix_Wq"], "bq": cols(plain["L0_mix_bq"], P),
        "Wk": plain["L0_mix_Wk"], "bk": plain["L0_mix_bk"],
        "Wv": plain["L0_mix_Wv"], "bv": plain["L0_mix_bv"],
        "Wfc": plain["L0_mix_Wfc"], "bfc": plain["L0_mix_bfc"],
        "gamma": cols(plain["L0_ffn_gamma"], P), "beta": cols(plain["L0_ffn_beta"], P),
        "Wr": plain["L0_ffn_Wr"], "br": plain["L0_ffn_br"],
        "W1": plain["L0_ffn_W1"], "b1": cols(plain["L0_ffn_b1"], P),
        "W2": plain["L0_ffn_W2"], "b2": plain["L0_ffn_b2"],
    }
    nc = _bacc.Bacc("TRN2", target_bir_lowering=False, num_devices=1)
    args = [nc.dram_tensor(f"in_{k}", v.shape, _mybir.dt.from_np(v.dtype), kind="ExternalInput").ap() for k, v in laid.items()]
    out = nc.dram_tensor("out_0", (N, D), _mybir.dt.float32, kind="ExternalOutput").ap()
    build(nc, *args, out)
    r = _run(nc, [{f"in_{k}": v for k, v in laid.items()}], core_ids=[0])
    return r.results[0]["out_0"]
```
